# Optimizing a Trainium2 kernel written in Bass

```python
import numpy as np
import jax
import jax.numpy as jnp

def _softmax(x, axis=-1):
    return jax.nn.softmax(x, axis=axis)

def _gelu(x):
    return jax.nn.gelu(x, approximate=True)

def _silu(x):
    return jax.nn.silu(x)

def _sigmoid(x):
    return jax.nn.sigmoid(x)

def _layernorm(x, axis=-1, eps=1e-05):
    m = jnp.mean(x, axis=axis, keepdims=True)
    v = jnp.var(x, axis=axis, keepdims=True)
    return (x - m) / jnp.sqrt(v + eps)

def _scatter_add(tgt, idx, src, axis=0):
    return tgt.at[idx].add(src)

def _segment_sum(src, seg, n):
    return jax.ops.segment_sum(src, seg, n)
kernel_name = 'mk_flamingo_gated_d4_seqx_r8_260af6'

def setup_inputs(seed: int=0):
    np.random.seed(seed)
    _w = jnp.asarray

    def _rec_inputs():
        import jax
        import jax.numpy as jnp
        _rk = jax.random.key(seed)
        x = -0.0002928 + 1 * jax.random.normal(jax.random.fold_in(_rk, 1), (8, 256, 128), jnp.float32)
        _lenS = 256 - jax.random.randint(jax.random.fold_in(_rk, 7), (8,), 0, max(1, 256 // 4) + 1, jnp.int32)
        _lenS2 = 256 - jax.random.randint(jax.random.fold_in(_rk, 8), (8,), 0, max(1, 256 // 4) + 1, jnp.int32)
        _ctx_1024P = jax.random.normal(jax.random.fold_in(_rk, 11), (8, 16, 128), jnp.float32)
        _ctx_1024c = jax.random.dirichlet(jax.random.fold_in(_rk, 511), 0.3 * jnp.ones((16,), jnp.float32), (8, 256))
        _ctx_1024t = jnp.einsum('bsk,bkd->bsd', _ctx_1024c, _ctx_1024P)
        _ctx_1024t = _ctx_1024t * jax.lax.rsqrt(jnp.mean(jnp.square(_ctx_1024t)) + 1e-12) * 0.953939
        ctx_1024 = -1.39393e-06 + 0.999914 * (_ctx_1024t + 0.3 * jax.random.normal(jax.random.fold_in(_rk, 611), (8, 256, 128), jnp.float32))
        fside_BxSxS2_0 = jax.random.uniform(jax.random.fold_in(_rk, 12), (8, 256, 256), jnp.float32, 0.0, 1)
        _validS = jnp.arange(256)[None, :] < _lenS[:, None]
        _validS2 = jnp.arange(256)[None, :] < _lenS2[:, None]
        _causal = jnp.tril(jnp.ones((256, 256), dtype=bool))
        mask_BxSxS2_ik1 = jnp.where(jnp.broadcast_to(_validS2[:, None, :], (8, 256, 256)), 1, 0).astype(jnp.int32)
        _g = jax.random.normal(jax.random.fold_in(_rk, 9001), (2, 4), jnp.float32)
        _g = jnp.sign(_g) * jnp.maximum(jnp.abs(_g), 1.0) + (_g == 0) * 1.0
        g_xattn = _g[0]
        g_ffn = _g[1]
        return (x, ctx_1024, fside_BxSxS2_0, mask_BxSxS2_ik1, g_xattn, g_ffn)
    x, ctx_1024, fside_BxSxS2_0, mask_BxSxS2_ik1, g_xattn, g_ffn = _rec_inputs()

    def _L0_xattn_setup():
        import jax, jax.numpy as jnp
        import numpy as np
        EPS_BACKEND = 1e-06
        NORM_EPS = 1e-06
        NUM_HEADS = 4

        def _mlstm_forward(q, k, v, ig_kernel, ig_bias, fg_kernel, fg_bias, outnorm_weight):
            B, S, E = q.shape
            NH = ig_bias.shape[0]
            DH = E // NH
            gate_input = jnp.concatenate([q, k, v], axis=-1)
            igate = gate_input @ ig_kernel + ig_bias
            fgate = gate_input @ fg_kernel + fg_bias
            qh = q.reshape(B, S, NH, DH).transpose(0, 2, 1, 3)
            kh = k.reshape(B, S, NH, DH).transpose(0, 2, 1, 3)
            vh = v.reshape(B, S, NH, DH).transpose(0, 2, 1, 3)
            ig = igate.transpose(0, 2, 1)
            fg = fgate.transpose(0, 2, 1)
            log_fg = jax.nn.log_sigmoid(fg)
            cums = jnp.concatenate([jnp.zeros((B, NH, 1), log_fg.dtype), jnp.cumsum(log_fg, axis=-1)], axis=-1)
            fg_mat = cums[..., :, None] - cums[..., None, :]
            mask = jnp.tril(jnp.ones((S + 1, S + 1), bool))
            fg_mat = jnp.where(mask, fg_mat, -jnp.inf)[..., 1:, 1:]
            log_D = fg_mat + ig[..., None, :]
            max_log_D = jnp.max(log_D, axis=-1, keepdims=True)
            D = jnp.exp(log_D - max_log_D)
            qk = jnp.einsum('bnsd,bntd->bnst', qh, kh) / jnp.sqrt(jnp.float32(DH))
            C = qk * D
            normalizer = jnp.maximum(jnp.abs(C.sum(-1, keepdims=True)), jnp.exp(-max_log_D))
            h = jnp.einsum('bnst,bntd->bnsd', C / (normalizer + EPS_BACKEND), vh)
            h = h.transpose(0, 2, 1, 3)
            mean = h.mean(-1, keepdims=True)
            var = h.var(-1, keepdims=True)
            hn = (h - mean) * jax.lax.rsqrt(var + NORM_EPS) * outnorm_weight
            return hn.reshape(B, S, E)
        key = jax.random.key(seed)
        ks = jax.random.split(key, 8)
        B, S, E, NH = (2, 256, 128, NUM_HEADS)
        DH = E // NH
        q = jax.random.normal(ks[0], (B, S, E), jnp.float32)
        k = jax.random.normal(ks[1], (B, S, E), jnp.float32)
        v = jax.random.normal(ks[2], (B, S, E), jnp.float32)
        ig_kernel = jax.random.normal(ks[3], (3 * E, NH), jnp.float32) * 0.02
        fg_kernel = jax.random.normal(ks[4], (3 * E, NH), jnp.float32) * 0.02
        ig_bias = jax.random.normal(ks[5], (NH,), jnp.float32) * 0.1
        fg_bias = jnp.linspace(3.0, 6.0, NH, dtype=jnp.float32)
        outnorm_weight = jnp.ones((NH, DH), jnp.float32)
        return {'q': q, 'k': k, 'v': v, 'ig_kernel': ig_kernel, 'ig_bias': ig_bias, 'fg_kernel': fg_kernel, 'fg_bias': fg_bias, 'outnorm_weight': outnorm_weight}
    _L0_xattn_all = _L0_xattn_setup()
    _L0_xattn_in = {k: v for k, v in _L0_xattn_all.items() if k in ('ig_kernel', 'ig_bias', 'fg_kernel', 'fg_bias', 'outnorm_weight')}
    del _L0_xattn_all

    def _L0_ffn_setup():
        import jax, jax.numpy as jnp
        import numpy as np
        B, T, DIM = (2, 256, 128)
        H, DH, E, K = (16, 64, 8, 2)
        key = jax.random.key(seed)
        ks = jax.random.split(key, 7)
        s = 0.02
        return {'x': jax.random.normal(ks[0], (B, T, DIM), jnp.float32), 'Wq': jax.random.normal(ks[1], (H, DH, DIM), jnp.float32) * s, 'Wk': jax.random.normal(ks[2], (H, DH, DIM), jnp.float32) * s, 'Wv': jax.random.normal(ks[3], (E, DH, DIM), jnp.float32) * s, 'Ws': jax.random.normal(ks[4], (H, E, DIM), jnp.float32) * s, 'Wd': jax.random.normal(ks[5], (H, E, DIM), jnp.float32) * s, 'Wo': jax.random.normal(ks[6], (E, DIM, DH), jnp.float32) * s}
    _L0_ffn_all = _L0_ffn_setup()
    _L0_ffn_in = {k: v for k, v in _L0_ffn_all.items() if k in ('Wq', 'Wk', 'Wv', 'Ws', 'Wd', 'Wo')}
    del _L0_ffn_all

    def _L1_xattn_setup():
        import jax, jax.numpy as jnp
        import numpy as np
        NUM_HEADS = 16
        HIDDEN = 128
        B, S = (2, 256)

        def _split_heads(x, H):
            b, s, d = x.shape
            return x.reshape(b, s, H, d // H).transpose(0, 2, 1, 3)
        key = jax.random.key(seed)
        ks = jax.random.split(key, 14)
        D = HIDDEN
        scale = 1.0 / np.sqrt(D)
        inp = {'query': jax.random.normal(ks[0], (B, S, D), jnp.float32), 'key_in': jax.random.normal(ks[1], (B, S, D), jnp.float32), 'value': jax.random.normal(ks[2], (B, S, D), jnp.float32), 'group_prob': jax.random.uniform(ks[3], (B, S, S), jnp.float32), 'mask': jax.random.randint(ks[4], (B, S, S), 0, 2, jnp.int32), 'wq_k': jax.random.normal(ks[5], (D, D), jnp.float32) * scale, 'wq_b': jnp.zeros((D,), jnp.float32), 'wk_k': jax.random.normal(ks[6], (D, D), jnp.float32) * scale, 'wk_b': jnp.zeros((D,), jnp.float32), 'wv_k': jax.random.normal(ks[7], (D, D), jnp.float32) * scale, 'wv_b': jnp.zeros((D,), jnp.float32), 'wo_k': jax.random.normal(ks[8], (D, D), jnp.float32) * scale, 'wo_b': jnp.zeros((D,), jnp.float32)}
        return inp
    _L1_xattn_all = _L1_xattn_setup()
    _L1_xattn_in = {k: v for k, v in _L1_xattn_all.items() if k in ('wq_k', 'wq_b', 'wk_k', 'wk_b', 'wv_k', 'wv_b', 'wo_k', 'wo_b')}
    del _L1_xattn_all

    def _L1_ffn_setup():
        import jax, jax.numpy as jnp
        import numpy as np
        H = 16
        TOP_K = 2
        LN_EPS = 1e-05
        key = jax.random.key(seed)
        ks = jax.random.split(key, 8)
        B, S, E, NE = (2, 128, 128, 8)
        w = lambda k, shp: jax.random.normal(k, shp, dtype=jnp.float32) * 0.02
        return {'x': jax.random.normal(ks[0], (B, S, E), dtype=jnp.float32), 'rW1': w(ks[1], (E // 2, E)), 'rb1': jnp.zeros((E // 2,), jnp.float32), 'ln_g': jnp.ones((E // 2,), jnp.float32), 'ln_b': jnp.zeros((E // 2,), jnp.float32), 'rW2': w(ks[2], (NE, E // 2)), 'rb2': jnp.zeros((NE,), jnp.float32), 'qW': w(ks[3], (NE, E, E)), 'qb': jnp.zeros((NE, E), jnp.float32), 'kW': w(ks[4], (NE, E, E)), 'kb': jnp.zeros((NE, E), jnp.float32), 'vW': w(ks[5], (NE, E, E)), 'vb': jnp.zeros((NE, E), jnp.float32), 'oW': w(ks[6], (NE, E, E)), 'ob': jnp.zeros((NE, E), jnp.float32)}
    _L1_ffn_all = _L1_ffn_setup()
    _L1_ffn_in = {k: v for k, v in _L1_ffn_all.items() if k in ('rW1', 'rb1', 'ln_g', 'ln_b', 'rW2', 'rb2', 'qW', 'qb', 'kW', 'kb', 'vW', 'vb', 'oW', 'ob')}
    del _L1_ffn_all

    def _L2_xattn_setup():
        import jax, jax.numpy as jnp
        import numpy as np
        NUM_HEADS = 8

        def _split_heads(x, h):
            b, n, c = x.shape
            return x.reshape(b, n, h, c // h).transpose(0, 2, 1, 3)
        key = jax.random.key(seed)
        ks = jax.random.split(key, 5)
        B, N, K, C = (16, 512, 64, 128)
        return {'img_fea': jax.random.normal(ks[0], (B, N, C), dtype=jnp.float32), 'aud_fea': jax.random.normal(ks[1], (B, K, C), dtype=jnp.float32), 'Wq': jax.random.normal(ks[2], (C, C), dtype=jnp.float32) * 0.02, 'Wk': jax.random.normal(ks[3], (C, C), dtype=jnp.float32) * 0.02, 'Wv': jax.random.normal(ks[4], (C, C), dtype=jnp.float32) * 0.02, 'aq': 1, 'sigmoid': 0, 'softmax': 1}
    _L2_xattn_all = _L2_xattn_setup()
    _L2_xattn_in = {k: v for k, v in _L2_xattn_all.items() if k in ('Wq', 'Wk', 'Wv')}
    del _L2_xattn_all

    def _L2_ffn_setup():
        import jax, jax.numpy as jnp
        import numpy as np
        D, H, E, K = (128, 128, 8, 2)

        def _moe(x, router_w, w_in, b_in, w_out, b_out):
            B, S, Dm = x.shape
            T = B * S
            x2 = x.reshape(T, Dm)
            logits = x2 @ router_w
            probs = jax.nn.softmax(logits, axis=-1)
            top_p, top_e = jax.lax.top_k(probs, K)
            flat_e = top_e.reshape(-1)
            flat_p = top_p.reshape(-1)
            tok = jnp.repeat(jnp.arange(T), K)
            order = jnp.argsort(flat_e)
            se, sp, st = (flat_e[order], flat_p[order], tok[order])
            xd = x2[st]
            N = xd.shape[0]
            h = jnp.zeros((N, H), x.dtype)
            for e in range(E):
                m = (se == e)[:, None]
                h = h + jnp.where(m, jax.nn.gelu(xd @ w_in[e] + b_in[e]), 0.0)
            y = jnp.zeros((N, Dm), x.dtype)
            for e in range(E):
                m = (se == e)[:, None]
                y = y + jnp.where(m, h @ w_out[e] + b_out[e], 0.0)
            y = y * sp[:, None]
            out = jnp.zeros((T, Dm), x.dtype).at[st].add(y)
            return out.reshape(B, S, Dm)
        key = jax.random.key(seed)
        ks = jax.random.split(key, 5)
        s = lambda k, shape, scale: jax.random.normal(k, shape, dtype=jnp.float32) * scale
        return {'input_batch': s(ks[0], (2, 64, D), 1.0), 'router_w': s(ks[1], (D, E), D ** (-0.5)), 'w_in': s(ks[2], (E, D, H), D ** (-0.5)), 'b_in': jnp.zeros((E, H), jnp.float32), 'w_out': s(ks[3], (E, H, D), H ** (-0.5)), 'b_out': jnp.zeros((E, D), jnp.float32)}
    _L2_ffn_all = _L2_ffn_setup()
    _L2_ffn_in = {k: v for k, v in _L2_ffn_all.items() if k in ('router_w', 'w_in', 'b_in', 'w_out', 'b_out')}
    del _L2_ffn_all

    def _L3_xattn_setup():
        import jax, jax.numpy as jnp
        import numpy as np
        D_MODEL = 128
        B, S = (4, 256)
        key = jax.random.key(seed)
        ks = jax.random.split(key, 10)
        s = 1.0 / np.sqrt(D_MODEL)
        return {'k': jax.random.normal(ks[0], (B, S, D_MODEL), jnp.float32), 'v': jax.random.normal(ks[1], (B, S, D_MODEL), jnp.float32), 'q': jax.random.normal(ks[2], (B, S, D_MODEL), jnp.float32), 'Wk': jax.random.normal(ks[3], (D_MODEL, D_MODEL), jnp.float32) * s, 'Wv': jax.random.normal(ks[4], (D_MODEL, D_MODEL), jnp.float32) * s, 'bv': jnp.zeros((D_MODEL,), jnp.float32), 'Wq': jax.random.normal(ks[5], (D_MODEL, D_MODEL), jnp.float32) * s, 'bq': jnp.zeros((D_MODEL,), jnp.float32), 'Wo': jax.random.normal(ks[6], (D_MODEL, D_MODEL), jnp.float32) * s, 'bo': jnp.zeros((D_MODEL,), jnp.float32)}
    _L3_xattn_all = _L3_xattn_setup()
    _L3_xattn_in = {k: v for k, v in _L3_xattn_all.items() if k in ('Wk', 'Wv', 'bv', 'Wq', 'bq', 'Wo', 'bo')}
    del _L3_xattn_all

    def _L3_ffn_setup():
        import jax, jax.numpy as jnp
        import numpy as np
        import math
        B, T, D, H, E, TOPK, CAPF = (4, 256, 128, 16, 8, 2, 2.0)
        HD = D // H

        def layernorm(x, g, b, eps=1e-05):
            m = jnp.mean(x, -1, keepdims=True)
            v = jnp.mean(jnp.square(x - m), -1, keepdims=True)
            return (x - m) * jax.lax.rsqrt(v + eps) * g + b

        def block_forward(x, ln1_g, ln1_b, Wqkv, Wproj, ln2_g, ln2_b, Wgate, W1, b1, W2, b2):
            Bb, Tt, d = x.shape
            hd = HD
            half = hd // 2
            h = layernorm(x, ln1_g, ln1_b)
            qkv = (h @ Wqkv).reshape(Bb, Tt, H, 3 * hd)
            q, k, v = (qkv[..., :hd], qkv[..., hd:2 * hd], qkv[..., 2 * hd:])
            inv_freq = 1.0 / 10000.0 ** (jnp.arange(0, hd, 2, dtype=jnp.float32) / hd)
            ang = jnp.arange(Tt, dtype=jnp.float32)[:, None] * inv_freq
            sin = jnp.sin(ang)[None, :, None, :].astype(x.dtype)
            cos = jnp.cos(ang)[None, :, None, :].astype(x.dtype)

            def rope(t):
                t1, t2 = (t[..., :half], t[..., half:])
                return jnp.concatenate([t1 * cos - t2 * sin, t1 * sin + t2 * cos], -1)
            q, k = (rope(q), rope(k))
            scores = jnp.einsum('bqhd,bkhd->bhqk', q, k) / math.sqrt(hd)
            causal = jnp.tril(jnp.ones((Tt, Tt), dtype=bool))
            scores = jnp.where(causal, scores, jnp.asarray(-1000000000.0, scores.dtype))
            probs = jax.nn.softmax(scores, axis=-1)
            attn = jnp.einsum('bhqk,bkhd->bqhd', probs, v).reshape(Bb, Tt, d) @ Wproj
            x = x + attn
            h2 = layernorm(x, ln2_g, ln2_b)
            flat = h2.reshape(-1, d)
            N = flat.shape[0]
            capacity = int(math.ceil(CAPF * N / E))
            gates = jax.nn.softmax((flat @ Wgate).astype(jnp.float32), -1).astype(flat.dtype)
            _, top_inds = jax.lax.top_k(gates, TOPK)
            mask = jnp.zeros((N, E), dtype=bool).at[jnp.arange(N)[:, None], top_inds].set(True)
            pos = jnp.cumsum(mask.astype(jnp.int32), axis=0) * mask - 1
            keep = (pos < capacity) & mask
            t_flat = jnp.repeat(jnp.arange(N), TOPK)
            e_flat = top_inds.reshape(-1)
            p = pos[t_flat, e_flat]
            kp = keep[t_flat, e_flat]
            p_eff = jnp.where(kp, p, capacity)
            exp_in = jnp.zeros((E, capacity, d), flat.dtype).at[e_flat, p_eff].set(flat[t_flat], mode='drop')
            hmid = jax.nn.gelu(jnp.einsum('ecd,edf->ecf', exp_in, W1) + b1[:, None, :], approximate=False)
            exp_out = jnp.einsum('ecf,efd->ecd', hmid, W2) + b2[:, None, :]
            gate = gates[t_flat, e_flat] * kp.astype(flat.dtype)
            p_g = jnp.minimum(p_eff, capacity - 1)
            moe = jnp.zeros((N, d), flat.dtype).at[t_flat].add(exp_out[e_flat, p_g] * gate[:, None])
            return x + moe.reshape(Bb, Tt, d)
        key = jax.random.key(seed)
        ks = jax.random.split(key, 8)
        s = 0.02
        return {'x': jax.random.normal(ks[0], (B, T, D), jnp.float32), 'ln1_g': jnp.ones((D,), jnp.float32), 'ln1_b': jnp.zeros((D,), jnp.float32), 'Wqkv': jax.random.normal(ks[1], (D, 3 * D), jnp.float32) * s, 'Wproj': jax.random.normal(ks[2], (D, D), jnp.float32) * s, 'ln2_g': jnp.ones((D,), jnp.float32), 'ln2_b': jnp.zeros((D,), jnp.float32), 'Wgate': jax.random.normal(ks[3], (D, E), jnp.float32) * s, 'W1': jax.random.normal(ks[4], (E, D, 4 * D), jnp.float32) * s, 'b1': jnp.zeros((E, 4 * D), jnp.float32), 'W2': jax.random.normal(ks[5], (E, 4 * D, D), jnp.float32) * s, 'b2': jnp.zeros((E, D), jnp.float32)}
    _L3_ffn_all = _L3_ffn_setup()
    _L3_ffn_in = {k: v for k, v in _L3_ffn_all.items() if k in ('ln1_g', 'ln1_b', 'Wqkv', 'Wproj', 'ln2_g', 'ln2_b', 'Wgate', 'W1', 'b1', 'W2', 'b2')}
    del _L3_ffn_all
    return {'x': x, 'ctx_1024': ctx_1024, 'fside_BxSxS2_0': fside_BxSxS2_0, 'mask_BxSxS2_ik1': mask_BxSxS2_ik1, 'g_xattn': g_xattn, 'g_ffn': g_ffn, 'L0_xattn_ig_kernel': _L0_xattn_in['ig_kernel'], 'L0_xattn_ig_bias': _L0_xattn_in['ig_bias'], 'L0_xattn_fg_kernel': _L0_xattn_in['fg_kernel'], 'L0_xattn_fg_bias': _L0_xattn_in['fg_bias'], 'L0_xattn_outnorm_weight': _L0_xattn_in['outnorm_weight'], 'L0_ffn_Wq': _L0_ffn_in['Wq'], 'L0_ffn_Wk': _L0_ffn_in['Wk'], 'L0_ffn_Wv': _L0_ffn_in['Wv'], 'L0_ffn_Ws': _L0_ffn_in['Ws'], 'L0_ffn_Wd': _L0_ffn_in['Wd'], 'L0_ffn_Wo': _L0_ffn_in['Wo'], 'L1_xattn_wq_k': _L1_xattn_in['wq_k'], 'L1_xattn_wq_b': _L1_xattn_in['wq_b'], 'L1_xattn_wk_k': _L1_xattn_in['wk_k'], 'L1_xattn_wk_b': _L1_xattn_in['wk_b'], 'L1_xattn_wv_k': _L1_xattn_in['wv_k'], 'L1_xattn_wv_b': _L1_xattn_in['wv_b'], 'L1_xattn_wo_k': _L1_xattn_in['wo_k'], 'L1_xattn_wo_b': _L1_xattn_in['wo_b'], 'L1_ffn_rW1': _L1_ffn_in['rW1'], 'L1_ffn_rb1': _L1_ffn_in['rb1'], 'L1_ffn_ln_g': _L1_ffn_in['ln_g'], 'L1_ffn_ln_b': _L1_ffn_in['ln_b'], 'L1_ffn_rW2': _L1_ffn_in['rW2'], 'L1_ffn_rb2': _L1_ffn_in['rb2'], 'L1_ffn_qW': _L1_ffn_in['qW'], 'L1_ffn_qb': _L1_ffn_in['qb'], 'L1_ffn_kW': _L1_ffn_in['kW'], 'L1_ffn_kb': _L1_ffn_in['kb'], 'L1_ffn_vW': _L1_ffn_in['vW'], 'L1_ffn_vb': _L1_ffn_in['vb'], 'L1_ffn_oW': _L1_ffn_in['oW'], 'L1_ffn_ob': _L1_ffn_in['ob'], 'L2_xattn_Wq': _L2_xattn_in['Wq'], 'L2_xattn_Wk': _L2_xattn_in['Wk'], 'L2_xattn_Wv': _L2_xattn_in['Wv'], 'L2_ffn_router_w': _L2_ffn_in['router_w'], 'L2_ffn_w_in': _L2_ffn_in['w_in'], 'L2_ffn_b_in': _L2_ffn_in['b_in'], 'L2_ffn_w_out': _L2_ffn_in['w_out'], 'L2_ffn_b_out': _L2_ffn_in['b_out'], 'L3_xattn_Wk': _L3_xattn_in['Wk'], 'L3_xattn_Wv': _L3_xattn_in['Wv'], 'L3_xattn_bv': _L3_xattn_in['bv'], 'L3_xattn_Wq': _L3_xattn_in['Wq'], 'L3_xattn_bq': _L3_xattn_in['bq'], 'L3_xattn_Wo': _L3_xattn_in['Wo'], 'L3_xattn_bo': _L3_xattn_in['bo'], 'L3_ffn_ln1_g': _L3_ffn_in['ln1_g'], 'L3_ffn_ln1_b': _L3_ffn_in['ln1_b'], 'L3_ffn_Wqkv': _L3_ffn_in['Wqkv'], 'L3_ffn_Wproj': _L3_ffn_in['Wproj'], 'L3_ffn_ln2_g': _L3_ffn_in['ln2_g'], 'L3_ffn_ln2_b': _L3_ffn_in['ln2_b'], 'L3_ffn_Wgate': _L3_ffn_in['Wgate'], 'L3_ffn_W1': _L3_ffn_in['W1'], 'L3_ffn_b1': _L3_ffn_in['b1'], 'L3_ffn_W2': _L3_ffn_in['W2'], 'L3_ffn_b2': _L3_ffn_in['b2']}

def reference(x, ctx_1024, fside_BxSxS2_0, mask_BxSxS2_ik1, g_xattn, g_ffn, L0_xattn_ig_kernel, L0_xattn_ig_bias, L0_xattn_fg_kernel, L0_xattn_fg_bias, L0_xattn_outnorm_weight, L0_ffn_Wq, L0_ffn_Wk, L0_ffn_Wv, L0_ffn_Ws, L0_ffn_Wd, L0_ffn_Wo, L1_xattn_wq_k, L1_xattn_wq_b, L1_xattn_wk_k, L1_xattn_wk_b, L1_xattn_wv_k, L1_xattn_wv_b, L1_xattn_wo_k, L1_xattn_wo_b, L1_ffn_rW1, L1_ffn_rb1, L1_ffn_ln_g, L1_ffn_ln_b, L1_ffn_rW2, L1_ffn_rb2, L1_ffn_qW, L1_ffn_qb, L1_ffn_kW, L1_ffn_kb, L1_ffn_vW, L1_ffn_vb, L1_ffn_oW, L1_ffn_ob, L2_xattn_Wq, L2_xattn_Wk, L2_xattn_Wv, L2_ffn_router_w, L2_ffn_w_in, L2_ffn_b_in, L2_ffn_w_out, L2_ffn_b_out, L3_xattn_Wk, L3_xattn_Wv, L3_xattn_bv, L3_xattn_Wq, L3_xattn_bq, L3_xattn_Wo, L3_xattn_bo, L3_ffn_ln1_g, L3_ffn_ln1_b, L3_ffn_Wqkv, L3_ffn_Wproj, L3_ffn_ln2_g, L3_ffn_ln2_b, L3_ffn_Wgate, L3_ffn_W1, L3_ffn_b1, L3_ffn_W2, L3_ffn_b2):
    import jax
    import jax.numpy as jnp

    def _L0_xattn_ref(q, k, v, ig_kernel, ig_bias, fg_kernel, fg_bias, outnorm_weight):
        import jax, jax.numpy as jnp
        import numpy as np
        EPS_BACKEND = 1e-06
        NORM_EPS = 1e-06
        NUM_HEADS = 4

        def _mlstm_forward(q, k, v, ig_kernel, ig_bias, fg_kernel, fg_bias, outnorm_weight):
            B, S, E = q.shape
            NH = ig_bias.shape[0]
            DH = E // NH
            gate_input = jnp.concatenate([q, k, v], axis=-1)
            igate = gate_input @ ig_kernel + ig_bias
            fgate = gate_input @ fg_kernel + fg_bias
            qh = q.reshape(B, S, NH, DH).transpose(0, 2, 1, 3)
            kh = k.reshape(B, S, NH, DH).transpose(0, 2, 1, 3)
            vh = v.reshape(B, S, NH, DH).transpose(0, 2, 1, 3)
            ig = igate.transpose(0, 2, 1)
            fg = fgate.transpose(0, 2, 1)
            log_fg = jax.nn.log_sigmoid(fg)
            cums = jnp.concatenate([jnp.zeros((B, NH, 1), log_fg.dtype), jnp.cumsum(log_fg, axis=-1)], axis=-1)
            fg_mat = cums[..., :, None] - cums[..., None, :]
            mask = jnp.tril(jnp.ones((S + 1, S + 1), bool))
            fg_mat = jnp.where(mask, fg_mat, -jnp.inf)[..., 1:, 1:]
            log_D = fg_mat + ig[..., None, :]
            max_log_D = jnp.max(log_D, axis=-1, keepdims=True)
            D = jnp.exp(log_D - max_log_D)
            qk = jnp.einsum('bnsd,bntd->bnst', qh, kh) / jnp.sqrt(jnp.float32(DH))
            C = qk * D
            normalizer = jnp.maximum(jnp.abs(C.sum(-1, keepdims=True)), jnp.exp(-max_log_D))
            h = jnp.einsum('bnst,bntd->bnsd', C / (normalizer + EPS_BACKEND), vh)
            h = h.transpose(0, 2, 1, 3)
            mean = h.mean(-1, keepdims=True)
            var = h.var(-1, keepdims=True)
            hn = (h - mean) * jax.lax.rsqrt(var + NORM_EPS) * outnorm_weight
            return hn.reshape(B, S, E)
        return _mlstm_forward(q, k, v, ig_kernel, ig_bias, fg_kernel, fg_bias, outnorm_weight)

    def _L0_ffn_ref(x, Wq, Wk, Wv, Ws, Wd, Wo):
        import jax, jax.numpy as jnp
        import numpy as np
        B, T, DIM = (2, 256, 128)
        H, DH, E, K = (16, 64, 8, 2)
        scale = DH ** (-0.5)
        q = jnp.einsum('btc,hdc->bhtd', x, Wq)
        k = jnp.einsum('btc,hdc->bhtd', x, Wk)
        gate_v = jnp.einsum('btc,hec->bthe', x, Ws)
        w, sel = jax.lax.top_k(gate_v, K)
        wsig = jax.nn.sigmoid(w)
        oh = jax.nn.one_hot(sel, E, dtype=x.dtype)
        mix_v = jnp.einsum('bthk,bthke->bthe', wsig, oh)
        proj_v = jnp.einsum('btc,edc->bted', x, Wv)
        v = jnp.einsum('bthe,bted->bhtd', mix_v, proj_v)
        scores = jnp.einsum('bhid,bhjd->bhij', q * scale, k)
        probs = jax.nn.softmax(scores, axis=-1)
        attn = jnp.einsum('bhij,bhjd->bihd', probs, v)
        gate_o = jnp.einsum('btc,hec->bthe', x, Wd)
        _, sel_o = jax.lax.top_k(gate_o, K)
        mask_o = jax.nn.one_hot(sel_o, E, dtype=x.dtype).sum(axis=3)
        res = jnp.einsum('bthe,bthd,efd->bthf', mask_o, attn, Wo)
        return res.sum(axis=2)

    def _L1_xattn_ref(query, key_in, value, group_prob, mask, wq_k, wq_b, wk_k, wk_b, wv_k, wv_b, wo_k, wo_b):
        import jax, jax.numpy as jnp
        import numpy as np
        NUM_HEADS = 16
        HIDDEN = 128
        B, S = (2, 256)

        def _split_heads(x, H):
            b, s, d = x.shape
            return x.reshape(b, s, H, d // H).transpose(0, 2, 1, 3)
        H = NUM_HEADS
        dh = query.shape[-1] // H
        q = _split_heads(query @ wq_k + wq_b, H)
        k = _split_heads(key_in @ wk_k + wk_b, H)
        v = _split_heads(value @ wv_k + wv_b, H)
        logits = jnp.einsum('bhqd,bhkd->bhqk', q, k) / jnp.sqrt(jnp.asarray(dh, q.dtype))
        neg = (1.0 - mask.astype(q.dtype)) * -1000000000.0
        logits = logits + neg[:, None, :, :]
        attn = jax.nn.softmax(logits, axis=-1)
        attn = attn * group_prob[:, None, :, :]
        out = jnp.einsum('bhqk,bhkd->bhqd', attn, v)
        out = out.transpose(0, 2, 1, 3).reshape(query.shape[0], -1, H * dh)
        return out @ wo_k + wo_b

    def _L1_ffn_ref(x, rW1, rb1, ln_g, ln_b, rW2, rb2, qW, qb, kW, kb, vW, vb, oW, ob):
        import jax, jax.numpy as jnp
        import numpy as np
        H = 16
        TOP_K = 2
        LN_EPS = 1e-05
        B, S, E = x.shape
        NE = qW.shape[0]
        Dh = E // H
        scale = 1.0 / jnp.sqrt(jnp.asarray(Dh, x.dtype))
        h = x @ rW1.T + rb1
        mu = h.mean(-1, keepdims=True)
        var = ((h - mu) ** 2).mean(-1, keepdims=True)
        h = (h - mu) * jax.lax.rsqrt(var + LN_EPS) * ln_g + ln_b
        h = jax.nn.relu(h)
        logits = h @ rW2.T + rb2
        probs = jax.nn.softmax(logits, axis=-1)
        tp, ti = jax.lax.top_k(probs, TOP_K)
        tp = tp / tp.sum(-1, keepdims=True)
        expert_mask = (jax.nn.one_hot(ti, NE, dtype=probs.dtype) * tp[..., None]).sum(-2)
        gates = jnp.moveaxis(expert_mask, -1, 0)

        def expert_step(acc, params):
            qw, qb_, kw, kb_, vw, vb_, ow, ob_, g = params
            q = (x @ qw.T + qb_).reshape(B, S, H, Dh).transpose(0, 2, 1, 3)
            k = (x @ kw.T + kb_).reshape(B, S, H, Dh).transpose(0, 2, 1, 3)
            v = (x @ vw.T + vb_).reshape(B, S, H, Dh).transpose(0, 2, 1, 3)
            scores = jnp.einsum('bhqd,bhkd->bhqk', q, k) * scale
            p = jax.nn.softmax(scores, axis=-1)
            o = jnp.einsum('bhqk,bhkd->bhqd', p, v)
            o = o.transpose(0, 2, 1, 3).reshape(B, S, E) @ ow.T + ob_
            return (acc + o * g[..., None], None)
        out, _ = jax.lax.scan(expert_step, jnp.zeros_like(x), (qW, qb, kW, kb, vW, vb, oW, ob, gates))
        return out

    def _L2_xattn_ref(img_fea, aud_fea, Wq, Wk, Wv, aq, sigmoid, softmax):
        import jax, jax.numpy as jnp
        import numpy as np
        NUM_HEADS = 8

        def _split_heads(x, h):
            b, n, c = x.shape
            return x.reshape(b, n, h, c // h).transpose(0, 2, 1, 3)
        if aq:
            query, key, value = (aud_fea, img_fea, img_fea)
        else:
            query, key, value = (img_fea, aud_fea, aud_fea)
        B, Nq, C = query.shape
        h = NUM_HEADS
        scale = (C // h) ** (-0.5)
        q = _split_heads(query @ Wq.T, h)
        k = _split_heads(key @ Wk.T, h)
        v = _split_heads(value @ Wv.T, h)
        attn = jnp.einsum('bhnd,bhmd->bhnm', q, k) * scale
        if sigmoid:
            attn = jax.nn.sigmoid(attn)
        if softmax:
            attn = jax.nn.softmax(attn, axis=-1)
        x = jnp.einsum('bhnm,bhmd->bhnd', attn, v)
        return x.transpose(0, 2, 1, 3).reshape(B, Nq, C)

    def _L2_ffn_ref(input_batch, router_w, w_in, b_in, w_out, b_out):
        import jax, jax.numpy as jnp
        import numpy as np
        D, H, E, K = (128, 128, 8, 2)

        def _moe(x, router_w, w_in, b_in, w_out, b_out):
            B, S, Dm = x.shape
            T = B * S
            x2 = x.reshape(T, Dm)
            logits = x2 @ router_w
            probs = jax.nn.softmax(logits, axis=-1)
            top_p, top_e = jax.lax.top_k(probs, K)
            flat_e = top_e.reshape(-1)
            flat_p = top_p.reshape(-1)
            tok = jnp.repeat(jnp.arange(T), K)
            order = jnp.argsort(flat_e)
            se, sp, st = (flat_e[order], flat_p[order], tok[order])
            xd = x2[st]
            N = xd.shape[0]
            h = jnp.zeros((N, H), x.dtype)
            for e in range(E):
                m = (se == e)[:, None]
                h = h + jnp.where(m, jax.nn.gelu(xd @ w_in[e] + b_in[e]), 0.0)
            y = jnp.zeros((N, Dm), x.dtype)
            for e in range(E):
                m = (se == e)[:, None]
                y = y + jnp.where(m, h @ w_out[e] + b_out[e], 0.0)
            y = y * sp[:, None]
            out = jnp.zeros((T, Dm), x.dtype).at[st].add(y)
            return out.reshape(B, S, Dm)
        return _moe(input_batch, router_w, w_in, b_in, w_out, b_out)

    def _L3_xattn_ref(k, v, q, Wk, Wv, bv, Wq, bq, Wo, bo):
        import jax, jax.numpy as jnp
        import numpy as np
        D_MODEL = 128
        B, S = (4, 256)
        kp = jnp.einsum('bsd,ed->bse', k, Wk)
        vp = jnp.einsum('bsd,ed->bse', v, Wv) + bv
        qp = jnp.einsum('bsd,ed->bse', q, Wq) + bq
        scale = 1.0 / jnp.sqrt(jnp.float32(kp.shape[-1]))
        scores = jnp.einsum('bqd,bkd->bqk', qp, kp) * scale
        probs = jax.nn.softmax(scores, axis=-1)
        ctx = jnp.einsum('bqk,bkd->bqd', probs, vp)
        return jnp.einsum('bqd,ed->bqe', ctx, Wo) + bo

    def _L3_ffn_ref(x, ln1_g, ln1_b, Wqkv, Wproj, ln2_g, ln2_b, Wgate, W1, b1, W2, b2):
        import jax, jax.numpy as jnp
        import numpy as np
        import math
        B, T, D, H, E, TOPK, CAPF = (4, 256, 128, 16, 8, 2, 2.0)
        HD = D // H

        def layernorm(x, g, b, eps=1e-05):
            m = jnp.mean(x, -1, keepdims=True)
            v = jnp.mean(jnp.square(x - m), -1, keepdims=True)
            return (x - m) * jax.lax.rsqrt(v + eps) * g + b

        def block_forward(x, ln1_g, ln1_b, Wqkv, Wproj, ln2_g, ln2_b, Wgate, W1, b1, W2, b2):
            Bb, Tt, d = x.shape
            hd = HD
            half = hd // 2
            h = layernorm(x, ln1_g, ln1_b)
            qkv = (h @ Wqkv).reshape(Bb, Tt, H, 3 * hd)
            q, k, v = (qkv[..., :hd], qkv[..., hd:2 * hd], qkv[..., 2 * hd:])
            inv_freq = 1.0 / 10000.0 ** (jnp.arange(0, hd, 2, dtype=jnp.float32) / hd)
            ang = jnp.arange(Tt, dtype=jnp.float32)[:, None] * inv_freq
            sin = jnp.sin(ang)[None, :, None, :].astype(x.dtype)
            cos = jnp.cos(ang)[None, :, None, :].astype(x.dtype)

            def rope(t):
                t1, t2 = (t[..., :half], t[..., half:])
                return jnp.concatenate([t1 * cos - t2 * sin, t1 * sin + t2 * cos], -1)
            q, k = (rope(q), rope(k))
            scores = jnp.einsum('bqhd,bkhd->bhqk', q, k) / math.sqrt(hd)
            causal = jnp.tril(jnp.ones((Tt, Tt), dtype=bool))
            scores = jnp.where(causal, scores, jnp.asarray(-1000000000.0, scores.dtype))
            probs = jax.nn.softmax(scores, axis=-1)
            attn = jnp.einsum('bhqk,bkhd->bqhd', probs, v).reshape(Bb, Tt, d) @ Wproj
            x = x + attn
            h2 = layernorm(x, ln2_g, ln2_b)
            flat = h2.reshape(-1, d)
            N = flat.shape[0]
            capacity = int(math.ceil(CAPF * N / E))
            gates = jax.nn.softmax((flat @ Wgate).astype(jnp.float32), -1).astype(flat.dtype)
            _, top_inds = jax.lax.top_k(gates, TOPK)
            mask = jnp.zeros((N, E), dtype=bool).at[jnp.arange(N)[:, None], top_inds].set(True)
            pos = jnp.cumsum(mask.astype(jnp.int32), axis=0) * mask - 1
            keep = (pos < capacity) & mask
            t_flat = jnp.repeat(jnp.arange(N), TOPK)
            e_flat = top_inds.reshape(-1)
            p = pos[t_flat, e_flat]
            kp = keep[t_flat, e_flat]
            p_eff = jnp.where(kp, p, capacity)
            exp_in = jnp.zeros((E, capacity, d), flat.dtype).at[e_flat, p_eff].set(flat[t_flat], mode='drop')
            hmid = jax.nn.gelu(jnp.einsum('ecd,edf->ecf', exp_in, W1) + b1[:, None, :], approximate=False)
            exp_out = jnp.einsum('ecf,efd->ecd', hmid, W2) + b2[:, None, :]
            gate = gates[t_flat, e_flat] * kp.astype(flat.dtype)
            p_g = jnp.minimum(p_eff, capacity - 1)
            moe = jnp.zeros((N, d), flat.dtype).at[t_flat].add(exp_out[e_flat, p_g] * gate[:, None])
            return x + moe.reshape(Bb, Tt, d)
        return block_forward(x, ln1_g, ln1_b, Wqkv, Wproj, ln2_g, ln2_b, Wgate, W1, b1, W2, b2)
    x = x + jnp.tanh(g_xattn[0]) * _L0_xattn_ref(_layernorm(x, axis=-1), ctx_1024, ctx_1024, L0_xattn_ig_kernel, L0_xattn_ig_bias, L0_xattn_fg_kernel, L0_xattn_fg_bias, L0_xattn_outnorm_weight)
    x = x + jnp.tanh(g_ffn[0]) * _L0_ffn_ref(_layernorm(x, axis=-1), L0_ffn_Wq, L0_ffn_Wk, L0_ffn_Wv, L0_ffn_Ws, L0_ffn_Wd, L0_ffn_Wo)
    x = x + jnp.tanh(g_xattn[1]) * _L1_xattn_ref(_layernorm(x, axis=-1), ctx_1024, ctx_1024, fside_BxSxS2_0, mask_BxSxS2_ik1, L1_xattn_wq_k, L1_xattn_wq_b, L1_xattn_wk_k, L1_xattn_wk_b, L1_xattn_wv_k, L1_xattn_wv_b, L1_xattn_wo_k, L1_xattn_wo_b)
    x = x + jnp.tanh(g_ffn[1]) * _L1_ffn_ref(_layernorm(x, axis=-1), L1_ffn_rW1, L1_ffn_rb1, L1_ffn_ln_g, L1_ffn_ln_b, L1_ffn_rW2, L1_ffn_rb2, L1_ffn_qW, L1_ffn_qb, L1_ffn_kW, L1_ffn_kb, L1_ffn_vW, L1_ffn_vb, L1_ffn_oW, L1_ffn_ob)
    x = x + jnp.tanh(g_xattn[2]) * _L2_xattn_ref(ctx_1024, _layernorm(x, axis=-1), L2_xattn_Wq, L2_xattn_Wk, L2_xattn_Wv, 1, 0, 1)
    x = x + jnp.tanh(g_ffn[2]) * _L2_ffn_ref(_layernorm(x, axis=-1), L2_ffn_router_w, L2_ffn_w_in, L2_ffn_b_in, L2_ffn_w_out, L2_ffn_b_out)
    x = x + jnp.tanh(g_xattn[3]) * _L3_xattn_ref(ctx_1024, ctx_1024, _layernorm(x, axis=-1), L3_xattn_Wk, L3_xattn_Wv, L3_xattn_bv, L3_xattn_Wq, L3_xattn_bq, L3_xattn_Wo, L3_xattn_bo)
    x = x + jnp.tanh(g_ffn[3]) * _L3_ffn_ref(_layernorm(x, axis=-1), L3_ffn_ln1_g, L3_ffn_ln1_b, L3_ffn_Wqkv, L3_ffn_Wproj, L3_ffn_ln2_g, L3_ffn_ln2_b, L3_ffn_Wgate, L3_ffn_W1, L3_ffn_b1, L3_ffn_W2, L3_ffn_b2)
    return x

_drawn_inputs = setup_inputs


def setup_inputs(seed=0):
    import zlib

    import numpy as np

    out = dict(_drawn_inputs(seed))
    spreads = {'L0_xattn_outnorm_weight': (1.0, 0.2),
     'L1_xattn_wq_b': (0.0, 0.768),
     'L1_xattn_wk_b': (0.0, 2.0),
     'L1_xattn_wv_b': (0.0, 0.274),
     'L1_xattn_wo_b': (0.0, 0.1),
     'L1_ffn_rb1': (0.0, 0.429),
     'L1_ffn_ln_g': (1.0, 0.6),
     'L1_ffn_ln_b': (0.0, 0.655),
     'L1_ffn_rb2': (0.0, 0.1),
     'L1_ffn_qb': (0.0, 0.8),
     'L1_ffn_kb': (0.0, 2.0),
     'L1_ffn_vb': (0.0, 0.729),
     'L1_ffn_ob': (0.0, 0.1),
     'L2_ffn_b_in': (0.0, 0.561),
     'L2_ffn_b_out': (0.0, 0.383),
     'L3_xattn_bv': (0.0, 0.1),
     'L3_xattn_bq': (0.0, 0.661),
     'L3_xattn_bo': (0.0, 0.1),
     'L3_ffn_ln1_g': (1.0, 0.6),
     'L3_ffn_ln1_b': (0.0, 0.8),
     'L3_ffn_ln2_g': (1.0, 0.6),
     'L3_ffn_ln2_b': (0.0, 0.8),
     'L3_ffn_b1': (0.0, 0.8),
     'L3_ffn_b2': (0.0, 0.8)}
    factors = {'g_ffn': 30.712,
     'L0_xattn_ig_bias': 64.0,
     'L0_xattn_fg_kernel': 3.572,
     'L0_ffn_Wq': 8.0,
     'L0_ffn_Wk': 8.0,
     'L0_ffn_Wv': 5.073,
     'L0_ffn_Ws': 5.478,
     'L0_ffn_Wd': 5.97,
     'L0_ffn_Wo': 4.978,
     'L1_ffn_qW': 8.0,
     'L1_ffn_kW': 8.0,
     'L1_ffn_vW': 8.0,
     'L1_ffn_oW': 4.957,
     'L2_xattn_Wq': 8.0,
     'L2_xattn_Wk': 8.0,
     'L3_ffn_Wqkv': 8.0,
     'L3_ffn_Wproj': 8.0,
     'L3_ffn_Wgate': 7.565,
     'L3_ffn_W1': 8.0,
     'L3_ffn_W2': 8.0}
    for name, (base, spread) in spreads.items():
        noise = np.random.default_rng([zlib.crc32(name.encode()), seed]).standard_normal(out[name].shape)
        drawn = base * np.exp(spread * noise) if base else spread * noise
        out[name] = jnp.asarray(drawn.astype(out[name].dtype))
    for name, factor in factors.items():
        out[name] = (out[name] * factor).astype(out[name].dtype)
    return out
```

```python
import math
from contextlib import ExitStack

import concourse.bass as bass
import numpy as np
from concourse import mybir
from concourse.alu_op_type import AluOpType as ALU

FP32, BF16, I32 = mybir.dt.float32, mybir.dt.bfloat16, mybir.dt.int32
ACT = mybir.ActivationFunctionType
X_AXIS = mybir.AxisListType.X

B, S, D, P = 8, 256, 128, 128
NT = S // P
E = 8
STAGES = 8
CAPACITY = int(math.ceil(2.0 * B * S / E))
BIG = 1.0e30
NEG_MASK = -1.0e9

WEIGHTS = [
    ("l0_gate", 24), ("l0_bias", 2), ("l0_outnorm", 128), ("gains", 8),
    ("l0_wq", 1024), ("l0_wk", 1024), ("l0_wv", 512), ("l0_wsd", 256), ("l0_wo", 512),
    ("l1_wq", 512), ("l1_wk", 512), ("l1_wv", 128), ("l1_qb", 4), ("l1_kb", 4), ("l1_vb", 128),
    ("l1_wo", 128), ("l1_bo", 128),
    ("l1f_rw1", 64), ("l1f_rb1", 64), ("l1f_lng", 64), ("l1f_lnb", 64), ("l1f_rw2", 8), ("l1f_rb2", 8),
    ("l1f_ow", 1024), ("l1f_vb", 64), ("l1f_ob", 128),
    ("l2_wq", 256), ("l2_wk", 256), ("l2_wv", 128),
    ("l2f_router", 8), ("l2f_win", 1024), ("l2f_bin", 8), ("l2f_wout", 1024), ("l2f_bout", 128),
    ("l3_wk", 128), ("l3_wv", 128), ("l3_wq", 128), ("l3_wo", 128), ("l3_bq", 1), ("l3_bv", 128), ("l3_bo", 128),
    ("l3f_ln", 4), ("l3f_wq", 512), ("l3f_wqs", 512), ("l3f_wk", 512), ("l3f_wks", 512), ("l3f_wv", 128),
    ("l3f_wproj", 128), ("l3f_wgate", 8), ("l3f_w1", 4096), ("l3f_b1", 32), ("l3f_w2", 4096), ("l3f_b2", 128),
]
CONSTS = [
    ("ident", 128), ("ones", 128), ("upto", 128), ("rank", 8), ("sel4", 512), ("cos", 256), ("sin", 256),
    ("kones8", 1), ("kones16", 1), ("zero", 1), ("den8", 32),
]
EXPERT_COLS = 512 + 512 + 128 + 4 + 4


def columns(layout):
    at, out = 0, {}
    for name, width in layout:
        out[name] = (at, width)
        at += width
    return out, at


class Attention:

    def __init__(self, heads, dh, rows, per, scale, heads_before, groups_before, norms_before, masked=False, gated=False,
                 score_banks=3):
        self.heads, self.dh, self.rows, self.per, self.scale = heads, dh, rows, per, scale
        self.groups = heads // per
        self.masked, self.gated, self.score_banks = masked, gated, score_banks
        self.hb, self.gb, self.nb = heads_before, groups_before, norms_before
        self.chunk = min(4, self.groups)
        self.chunks = self.groups // self.chunk
        self.turns = {}
        for c in range(self.chunks):
            last = (c + 1) * self.chunk * per - 1
            for t in range(NT):
                self.turns[last + per + 3 + t] = (c, t)
        self.steps = max(self.turns) + 1

    def turns_before(self, step):
        return sum(1 for s in self.turns if s < step)

    def adds_before(self, step):
        return sum(1 for i in range(step) if i % self.per == 0 and self.per <= i <= self.heads)


def program(nc, x_in, ctx_in, gp_in, mask_in, maskT_in, weights_in, consts_in, causal_in, experts_in, out):
    WC, n_weights = columns(WEIGHTS)
    CC, n_consts = columns(CONSTS)
    scope = ExitStack()
    with scope:
        def sb(name, shape, dt=FP32):
            return scope.enter_context(nc.sbuf_tensor(name, shape, dt))

        W = sb("W", [P, n_weights])
        C = sb("C", [P, n_consts])

        def w(name, rows=P):
            a, n = WC[name]
            return W[0:rows, a:a + n]

        def c(name, rows=P):
            a, n = CC[name]
            return C[0:rows, a:a + n]

        ident = c("ident")
        ident_bf = sb("ident_bf", [P, P], BF16)
        causS = sb("causS", [P, NT, S], BF16)
        causT = sb("causT", [P, NT, S], BF16)
        tanh_gain = sb("tanh_gain", [P, 8])
        minus_half = sb("minus_half", [P, 16])
        out_bias1 = sb("out_bias1", [E, D])
        expert = sb("expert", [P, EXPERT_COLS])

        xs = sb("xs", [P, NT, D])
        ctxs = sb("ctxs", [P, NT, D])
        ctxT = sb("ctxT", [P, S])
        y = sb("y", [P, NT, D])
        yT = sb("yT", [P, S])
        bn = sb("bn", [P, NT, 6])
        mv = sb("mv", [P, NT, 2])
        rstd = sb("rstd", [P, NT])
        tmp = sb("tmp", [P, NT, D])
        acc = sb("acc", [P, NT, D])
        gpT = sb("gpT", [P, NT, S])
        negS = sb("negS", [P, NT, S], BF16)
        negT = sb("negT", [P, NT, S], BF16)

        qk = sb("qk", [P, 8, S])
        qS, kS = qk[:, 0:4, :], qk[:, 4:8, :]
        qk64 = qk[:, :, :].rearrange("p (h a) s -> p h (a s)", a=2)
        negmax = {8: sb("negmax8", [P, 4, NT, P]), 16: sb("negmax16", [P, 2, NT, P]), 64: sb("negmax64", [P, 4, NT, P])}
        V8 = sb("V8", [P, NT, 16, 32])
        V16 = sb("V16", [P, NT, 8, 32])
        V64s = sb("V64s", [P, NT * 16 * 65])
        V64 = V64s[:, :].rearrange("p (t h d) -> p t h d", t=NT, h=16)
        V8x = V64s[:, 0:NT * 16 * 32].rearrange("p (t h d) -> p t h d", t=NT, h=16)
        PTG = sb("PTG", [P, 6, 2 * S])
        PT, PG = PTG[:, 0:3, :], PTG[:, 3:6, :]
        OT = sb("OT", [P, 8, S])
        on = sb("on", [P, NT, 1024])
        onT = sb("onT", [P, S])
        rden = sb("rden", [P, 16])

        l0r = PTG[0:4, :, :].rearrange("p a (b s) -> p (a b) s", b=2)
        gcol = sb("gcol", [P, NT, 4])
        mcol = sb("mcol", [P, NT, 4])
        mix = sb("mix", [P, 4096])
        mixD, mixP = mix[:, 0:2048], mix[:, 2048:4096]
        mask_i = mix[:, 0:512].bitcast(I32).rearrange("p (t s) -> p t s", t=NT)
        maskT_i = mix[:, 512:1024].bitcast(I32).rearrange("p (t s) -> p t s", t=NT)
        Dm = mix[:, 0:1536].rearrange("p (h s) -> p h s", h=4)
        Cm = mix[:, 1536:3072].rearrange("p (h s) -> p h s", h=4)
        Vm = sb("Vm", [P, NT, 4, 33])
        hh = sb("hh", [P, NT, 4, 32])
        bn8 = sb("bn8", [P, 8, 6])
        mv8 = sb("mv8", [P, 8, 2])
        rstd8 = sb("rstd8", [P, 8])
        dn = sb("dn", [P, 4, NT * 4])
        pv = sb("pv", [P, NT, 512])
        gv = sb("gv", [P, 512])
        t2 = OT[:, :, :].rearrange("p (a b) s -> p a (b s)", b=2)
        t2s = sb("t2s", [P, 2, 64])
        gsig = sb("gsig", [P, 512])
        coef = sb("coef", [P, 512])

        gates = sb("gates", [P, NT, E])
        gatesT = sb("gatesT", [E, S])
        gs = sb("gs", [P, 4, NT])
        hT = on[:, :, :].rearrange("p t (f s) -> p t f s", f=4)
        GT = hT[:, 0, :, :]
        carry = sb("carry", [P, E])
        x1 = tmp
        pr = sb("pr", [P, 2, S])
        r1 = pr[:, 1, 0:NT * 64].rearrange("p (t d) -> p t d", t=NT)
        r1T = pr[0:64, 0, :]

        bank = [scope.enter_context(nc.psum_tensor(f"bank{i}", [P, 512], FP32)) for i in range(8)]
        MISC = bank[7]

        setup = {n: scope.enter_context(nc.semaphore(n)) for n in (
            "consts_loaded", "causal_loaded", "weights_loaded", "setup_dve", "setup_pool", "setup_pe", "setup_act",
            "engine_at_end", "cleared", "engine_resumes")}
        done = {n: scope.enter_context(nc.semaphore(n)) for n in (
            "x_loaded", "ctx_loaded", "mask_loaded", "maskT_loaded", "gp_loaded", "expert_loaded", "x_final", "out_stored",
            "dve_step", "dve_expert_step", "pool_step", "act_step",
            "ln_var", "ln_rstd", "ln_y", "ln_turned", "ln_yT",
            "scored", "max_taken", "max_turned", "q_shifted", "scoredT", "exped", "group_weighted", "valued",
            "o_copied", "o_turned", "normed",
            "ctx_turned", "ctxT_ready", "on_turned", "onT_ready", "projected",
            "l0_gates", "l0_absf", "l0_softplus", "l0_rows", "l0_cols_turned", "l0_negm", "l0_expm", "l0_spread", "l0_args",
            "l0_decay", "l0_decay_masked", "l0_qk", "l0_cm", "l0_h", "l0_hstat", "l0_hrstd",
            "l0f_qk", "l0f_qk_ready", "l0f_pv", "l0f_gates", "l0f_gcopied", "l0f_sig", "l0f_pvcopied", "l0f_coef", "l0f_vdve",
            "l0f_vpool", "l0f_coefo", "l0f_gdve", "l0f_gpool", "l0f_gturned", "l0f_gT",
            "filled", "neg_ready", "l1_q", "l1_k", "l1_v", "l1_q_ready", "l1_kv_ready",
            "l1f_r1", "l1f_rvar", "l1f_rrstd", "l1f_r1n", "l1f_r1turned", "l1f_r1T", "l1f_logits", "l1f_rmax", "l1f_rexp",
            "l1f_gates", "l1f_gturned", "l1f_gT", "l1f_bias",
            "ex_q", "ex_k", "ex_v", "ex_q_ready", "ex_kv_ready", "ex_turned", "ex_oT", "ex_projected", "ex_added",
            "l2_q", "l2_kv", "l2_q_ready", "l2_kv_ready",
            "l2f_logits", "l2f_rmax", "l2f_rexp", "l2f_gates", "l2f_gturned", "l2f_gT", "l2f_h", "l2f_gelu", "l2f_o", "l2f_oadd",
            "l3_qkv", "l3_qk_ready", "l3_v_ready", "l3_s", "l3_smax", "l3_exp", "l3_pturned", "l3_pT", "l3_ctx", "l3_ctx_ready", "l3_rden", "l3_out",
            "rope_q", "rope_k", "rope_v", "rope_q_ready", "rope_kv_ready",
            "l3f_logits", "l3f_rmax", "l3f_rexp", "l3f_top", "l3f_count", "l3f_gates", "l3f_gturned", "l3f_gT", "l3f_h", "l3f_gelu", "l3f_o",
            "l3f_oadd")}
        A0 = Attention(16, 64, 128, 1, 64 ** -0.5, 0, 0, 0, score_banks=2)
        A1 = Attention(16, 8, 32, 4, 8 ** -0.5, 16, 16, 8, masked=True, gated=True)

        def expert_attention(e):
            return Attention(16, 8, 32, 4, 8 ** -0.5, e * 16 + 32, e * 4 + 20, e * 2 + 10)

        A2 = Attention(8, 16, 32, 4, 0.25, 32 + 128, 20 + 32, 10 + 16)
        A3 = Attention(16, 8, 32, 4, 8 ** -0.5, 168, 54, 28, masked=True)

        def some(n):
            return not isinstance(n, int) or n > 0

        block = scope.enter_context(nc.Block())

        @block.sync
        def _(sp):
            sp.dma_start(C[:, :], consts_in).then_inc(setup["consts_loaded"], 16)
            sp.dma_start(mixD[:, 0:1024], causal_in).then_inc(setup["causal_loaded"], 16)
            sp.dma_start(W[:, :], weights_in).then_inc(setup["weights_loaded"], 16)
            with sp.Fori(0, B) as b:
                def tokens(ap):
                    return ap[bass.ds(b, 1)].rearrange("a (t p) d -> p (a t) d", p=P)

                sp.dma_start(xs[:, :, :], tokens(x_in)).then_inc(done["x_loaded"], 16)
                sp.dma_start(ctxs[:, :, :], tokens(ctx_in)).then_inc(done["ctx_loaded"], 16)
                if STAGES > 2:
                    sp.dma_start(gpT[:, :, :], tokens(gp_in)).then_inc(done["gp_loaded"], 16)
                    sp.wait_ge(done["l0f_gturned"], 2)
                    sp.dma_start(mask_i, tokens(mask_in)).then_inc(done["mask_loaded"], 16)
                    sp.dma_start(maskT_i, tokens(maskT_in)).then_inc(done["maskT_loaded"], 16)
                if STAGES > 3:
                    sp.dma_start(expert[:, :], experts_in[0]).then_inc(done["expert_loaded"], 16)
                    with sp.Fori(1, E) as e:
                        sp.wait_ge(done["ex_kv_ready"], e)
                        sp.wait_ge(done["ex_q_ready"], e)
                        sp.dma_start(expert[:, :], experts_in[bass.ds(e, 1)].rearrange("a p n -> (a p) n"))\
                            .then_inc(done["expert_loaded"], 16)
                sp.wait_ge(done["x_final"], 1)
                sp.dma_start(out[bass.ds(b, 1)].rearrange("a (t p) d -> p (a t) d", p=P), xs[:, :, :])\
                    .then_inc(done["out_stored"], 16)
                sp.wait_ge(done["out_stored"], 16)
                for n in ("x_loaded", "ctx_loaded"):
                    sp.wait_ge(done[n], 16)
                if STAGES > 2:
                    for n in ("mask_loaded", "maskT_loaded", "gp_loaded"):
                        sp.wait_ge(done[n], 16)
                if STAGES > 3:
                    sp.wait_ge(done["expert_loaded"], 16 * E)
                sp.wait_ge(setup["engine_at_end"], 4)
                for s in done.values():
                    sp.sem_clear(s)
                sp.sem_clear(setup["engine_at_end"])
                sp.sem_inc(setup["cleared"], 1)
                sp.wait_ge(setup["engine_resumes"], 4)
                sp.sem_clear(setup["cleared"])
                sp.sem_clear(setup["engine_resumes"])

        def end_of_batch(eng):
            eng.sem_inc(setup["engine_at_end"], 1)
            eng.wait_ge(setup["cleared"], 1)
            eng.sem_inc(setup["engine_resumes"], 1)

        def q_rows(A, h, n):
            if A.rows == 128:
                return qk64[0:n, h % 4, 0:S]
            j = 32 * (h % 4)
            return qS[j:j + n, h // 4, :]

        def k_rows(A, h, n):
            if A.rows == 128:
                return qk64[0:n, h % 4, S:2 * S]
            j = 32 * (h % 4)
            return kS[j:j + n, h // 4, :]

        def pe_attention(pe, A, V, masks=None, before=None):
            per, dh = A.per, A.dh
            for i in range(A.steps):
                if before is not None:
                    before(i)
                if i < A.heads:
                    if some(A.hb + i - A.score_banks + 1):
                        pe.wait_ge(done["max_taken"], A.hb + i - A.score_banks + 1)
                    for t in range(NT):
                        mm = pe.matmul(bank[i % A.score_banks][:, t * S:(t + 1) * S], q_rows(A, i, dh)[:, t * P:(t + 1) * P],
                                       k_rows(A, i, dh), start=True, stop=masks is None)
                        if masks is not None:
                            mm = pe.matmul(bank[i % A.score_banks][:, t * S:(t + 1) * S], ident_bf[:, :], masks[0][:, t, :],
                                           start=False, stop=True)
                    mm.then_inc(done["scored"], 1)
                if i % per == 0 and per <= i <= A.heads:
                    g = i // per - 1
                    pe.wait_ge(done["max_taken"], A.hb + (g + 1) * per)
                    if some(A.gb + g):
                        pe.wait_ge(done["q_shifted"], A.gb + g)
                    if some(A.nb + A.turns_before(i)):
                        pe.wait_ge(done["normed"], A.nb + A.turns_before(i))
                    M = negmax[dh][:, g % 4, :, :]
                    rows = A.rows if A.rows == 128 else 128
                    for t in range(NT):
                        mm = pe.transpose(MISC[0:rows, t * P:(t + 1) * P], M[:, t, :], ident)
                    mm.then_inc(done["max_turned"], 1)
                h = i - per - 1
                if 0 <= h < A.heads:
                    pe.wait_ge(done["q_shifted"], A.gb + h // per + 1)
                    if some(A.hb + h - 1):
                        pe.wait_ge(done["exped"], A.hb + h - 1)
                    for t in range(NT):
                        mm = pe.matmul(bank[3 + h % 2][:, t * S:(t + 1) * S], k_rows(A, h, dh + 1)[:, t * P:(t + 1) * P],
                                       q_rows(A, h, dh + 1), start=True, stop=masks is None)
                        if masks is not None:
                            mm = pe.matmul(bank[3 + h % 2][:, t * S:(t + 1) * S], ident_bf[:, :], masks[1][:, t, :],
                                           start=False, stop=True)
                    mm.then_inc(done["scoredT"], 1)
                h = i - per - 2
                if 0 <= h < A.heads:
                    g, j = h // per, h % per
                    if j == 0:
                        if some(A.gb + g - 1):
                            pe.wait_ge(done["o_copied"], A.gb + g - 1)
                    if A.gated:
                        pe.wait_ge(done["group_weighted"], h + 1)
                    pe.wait_ge(done["exped"], A.hb + h + 1)
                    if A.rows == 128:
                        o = bank[5 + g % 2][0:dh + 1, 0:S]
                    else:
                        o = bank[5 + g % 2][32 * j:32 * j + 32, 0:S]
                    for t in range(NT):
                        mm = pe.matmul(o, V[:, t, h, :], (PG if A.gated else PT)[:, h % 3, t * S:(t + 1) * S],
                                       start=t == 0, stop=t == NT - 1 and not A.gated)
                    if A.gated:
                        for t in range(NT):
                            mm = pe.matmul(o, c("den8"), PT[:, h % 3, t * S:(t + 1) * S], start=False, stop=t == NT - 1)
                    mm.then_inc(done["valued"], 1)
                if i in A.turns:
                    ch, t = A.turns[i]
                    pe.wait_ge(done["o_copied"], A.gb + (ch + 1) * A.chunk)
                    if some(A.nb + A.turns_before(i)):
                        pe.wait_ge(done["normed"], A.nb + A.turns_before(i))
                    pe.wait_ge(done["q_shifted"], A.gb + A.adds_before(i + 1))
                    n = dh + 1 if A.rows == 128 else 128
                    for s in range(A.chunk):
                        g = ch * A.chunk + s
                        mm = pe.transpose(MISC[:, s * 128:s * 128 + n], OT[0:n, g % 8, t * P:(t + 1) * P], ident[0:n, 0:n])
                    mm.then_inc(done["o_turned"], 1)

        def act_attention(act, A, before=None):
            per = A.per

            def copy_out(g):
                act.wait_ge(done["valued"], A.hb + (g + 1) * per)
                n = A.dh + 1 if A.rows == 128 else 128
                act.activation(OT[0:n, g % 8, :], bank[5 + g % 2][0:n, 0:S], ACT.Copy).then_inc(done["o_copied"], 1)

            for h in range(A.heads):
                if before is not None:
                    before(h)
                act.wait_ge(done["scoredT"], A.hb + h + 1)
                if some(A.hb + h - 2):
                    act.wait_ge(done["valued"], A.hb + h - 2)
                act.activation(PT[:, h % 3, :], bank[3 + h % 2][:, :], ACT.Exp, scale=A.scale).then_inc(done["exped"], 1)
                if h >= 1 and h % per == 0:
                    copy_out(h // per - 1)
            copy_out(A.groups - 1)

        def pool_attention(pool, A):
            for h in range(A.heads):
                pool.wait_ge(done["exped"], A.hb + h + 1)
                if some(A.hb + h - 2):
                    pool.wait_ge(done["valued"], A.hb + h - 2)
                pool.tensor_tensor(PG[:, h % 3, :], PT[:, h % 3, :], gpT[:, :, :].rearrange("p t s -> p (t s)"), ALU.mult)\
                    .then_inc(done["group_weighted"], 1)

        def dve_attention(dve, A, link, gate=None):
            per, dh = A.per, A.dh
            for i in range(A.steps):
                if i < A.heads:
                    dve.wait_ge(done["scored"], A.hb + i + 1)
                    g, j = i // per, i % per
                    dve.tensor_reduce(negmax[dh][:, g % 4, :, j * 32 + dh], bank[i % A.score_banks][:, :].rearrange("p (t s) -> p t s", t=NT),
                                      X_AXIS, ALU.max, negate=True).then_inc(done["max_taken"], 1)
                if i % per == 0 and per <= i <= A.heads:
                    g = i // per - 1
                    dve.wait_ge(done["max_turned"], A.gb + g + 1)
                    if A.rows == 128:
                        dve.tensor_copy(qk64[dh:dh + 1, g % 4, 0:S], MISC[dh:dh + 1, 0:S]).then_inc(done["q_shifted"], 1)
                    else:
                        dve.tensor_tensor(qS[:, g, :], qS[:, g, :], MISC[:, 0:S], ALU.add).then_inc(done["q_shifted"], 1)
                if i in A.turns:
                    ch, t = A.turns[i]
                    dve.wait_ge(done["o_turned"], A.nb + A.turns_before(i) + 1)
                    n = A.chunk * per
                    T = MISC[:, 0:A.chunk * 128].rearrange("p (h c) -> p h c", c=A.rows)
                    r = rden[:, 0:n].unsqueeze(2)
                    link(dve.reciprocal(r, T[:, :, dh:dh + 1]))
                    if gate is not None:
                        link(dve.tensor_scalar(rden[:, 0:n], rden[:, 0:n], gate(t), None, ALU.mult))
                    o = on[:, t, ch * n * dh:(ch + 1) * n * dh].rearrange("p (h d) -> p h d", d=dh)
                    dve.tensor_tensor(o, T[:, :, 0:dh], r.broadcast_to([P, n, dh]), ALU.mult).then_inc(done["normed"], 1)

        @block.tensor
        def _(pe):
            pe.wait_ge(setup["weights_loaded"], 16)
            pe.wait_ge(setup["consts_loaded"], 16)
            pe.wait_ge(setup["setup_dve"], SETUP_DVE)
            for e in range(E):
                mm = pe.matmul(bank[0][0:E, 0:D], w("l1f_vb")[:, e * E:(e + 1) * E], w("l1f_ow")[:, e * D:(e + 1) * D],
                               start=e == 0, stop=e == E - 1)
            mm.then_inc(setup["setup_pe"], 1)

            def turn_ln(n):
                pe.wait_ge(done["ln_y"], n + 1)
                for t in range(NT):
                    mm = pe.transpose(MISC[:, t * P:(t + 1) * P], y[:, t, :], ident)
                mm.then_inc(done["ln_turned"], 1)

            def turn_on(n):
                for t in range(NT):
                    mm = pe.transpose(bank[0][:, t * P:(t + 1) * P], on[:, t, 0:D], ident)
                mm.then_inc(done["on_turned"], 1)
                pe.wait_ge(done["onT_ready"], n + 1)

            with pe.Fori(0, B) as b:
                pe.wait_ge(done["ctx_loaded"], 16)
                for t in range(NT):
                    mm = pe.transpose(bank[6][:, t * P:(t + 1) * P], ctxs[:, t, :], ident)
                mm.then_inc(done["ctx_turned"], 1)

                turn_ln(0)
                pe.wait_ge(done["ctxT_ready"], 1)
                pe.wait_ge(done["ln_yT"], 1)
                for which in range(2):
                    for part, rhs in enumerate((yT, ctxT, ctxT)):
                        mm = pe.matmul(bank[4][0:4, which * S:(which + 1) * S],
                                       w("l0_gate")[:, part * 8 + which * 4:part * 8 + which * 4 + 4], rhs[:, :],
                                       start=part == 0, stop=part == 2)
                mm.then_inc(done["l0_gates"], 1)
                for h in range(4):
                    r = slice(32 * h, 32 * h + 32)
                    pe.matmul(bank[h][:, 0:S], ctxT[r, 0:P], yT[r, :], start=True, stop=True)
                    mm = pe.matmul(bank[h][:, S:S + P], ctxT[r, P:S], yT[r, P:S], start=True, stop=True)
                mm.then_inc(done["l0_qk"], 1)
                pe.wait_ge(done["l0_rows"], 1)
                for k, row in enumerate((8, 10)):
                    for t in range(NT):
                        mm = pe.transpose(bank[5][:, (k * NT + t) * 4:(k * NT + t) * 4 + 4], l0r[0:4, row, t * P:(t + 1) * P],
                                          ident[0:4, 0:4])
                mm.then_inc(done["l0_cols_turned"], 1)
                for h in range(4):
                    mm = pe.matmul(bank[6 + h // 2][:, (h % 2) * S:(h % 2 + 1) * S], c("sel4", 4)[:, h * P:(h + 1) * P],
                                   l0r[0:4, 9, :], start=True, stop=True)
                mm.then_inc(done["l0_spread"], 1)
                pe.wait_ge(done["l0_cm"], 4)
                for t in range(NT):
                    for h in range(4):
                        o = bank[4 + t][:, h * 33:h * 33 + 33]
                        if t == 0:
                            mm = pe.matmul(o, Cm[:, h, 0:P], Vm[:, 0, h, :], start=True, stop=True)
                        else:
                            pe.matmul(o, Cm[:, h, P:S], Vm[:, 0, h, :], start=True, stop=False)
                            mm = pe.matmul(o, Cm[:, h, S:S + P], Vm[:, 1, h, :], start=False, stop=True)
                    mm.then_inc(done["l0_h"], 1)

                if STAGES > 1:
                    turn_ln(1)
                    pe.wait_ge(done["ln_yT"], 2)
                    for t in range(NT):
                        mm = pe.matmul(bank[0][:, t * 256:(t + 1) * 256], yT[:, t * P:(t + 1) * P], w("l0_wsd"), start=True, stop=True)
                    mm.then_inc(done["l0f_gates"], 1)
                    for t in range(NT):
                        mm = pe.matmul(bank[1 + t][:, :], yT[:, t * P:(t + 1) * P], w("l0_wv"), start=True, stop=True)
                        mm.then_inc(done["l0f_pv"], 1)
                    pe.wait_ge(done["l0f_gcopied"], 1)
                    pe.wait_ge(done["l0f_pvcopied"], 2)

                    def project_qk(h):
                        if some(h):
                            pe.wait_ge(done["l0f_qk_ready"], h)
                        for part, wt in enumerate((w("l0_wq"), w("l0_wk"))):
                            mm = pe.matmul(bank[2][0:64, part * S:(part + 1) * S], wt[:, h * 64:(h + 1) * 64], yT[:, :],
                                           start=True, stop=True)
                        mm.then_inc(done["l0f_qk"], 1)

                    def before_step(i):
                        if i == 0:
                            project_qk(0)
                        if i + 1 < 16:
                            project_qk(i + 1)
                        if i < 16:
                            pe.wait_ge(done["l0f_qk_ready"], i + 1)
                        if i == 2:
                            pe.wait_ge(done["filled"], 2)
                        if i == 3:
                            pe.wait_ge(done["l0f_vdve"], 4)
                            pe.wait_ge(done["l0f_vpool"], 4)

                    pe_attention(pe, A0, V64, before=before_step)
                    for t in range(NT):
                        pe.wait_ge(done[("l0f_gdve", "l0f_gpool")[t]], 4)
                        for q in range(4):
                            mm = pe.transpose(bank[t][:, q * P:(q + 1) * P], pv[:, t, q * P:(q + 1) * P], ident)
                        mm.then_inc(done["l0f_gturned"], 1)
                    pe.wait_ge(done["l0f_gT"], 2)
                    for t in range(NT):
                        for q in range(4):
                            mm = pe.matmul(bank[2][:, t * P:(t + 1) * P], GT[:, q, t * P:(t + 1) * P], w("l0_wo")[:, q * D:(q + 1) * D],
                                           start=q == 0, stop=q == 3)
                    mm.then_inc(done["projected"], 1)

                if STAGES > 2:
                    turn_ln(2)
                    for g in range(4):
                        if g == 0:
                            for gg in range(4):
                                mm = pe.matmul(bank[3 + gg // 2][:, (gg % 2) * S:(gg % 2 + 1) * S], w("l1_wk")[:, gg * P:(gg + 1) * P],
                                               ctxT[:, :], start=True, stop=True)
                            mm.then_inc(done["l1_k"], 1)
                            for t in range(NT):
                                mm = pe.matmul(bank[5][:, t * D:(t + 1) * D], ctxT[:, t * P:(t + 1) * P], w("l1_wv"),
                                               start=True, stop=True)
                            mm.then_inc(done["l1_v"], 1)
                            pe.wait_ge(done["ln_yT"], 3)
                        mm = pe.matmul(bank[g // 2][:, (g % 2) * S:(g % 2 + 1) * S], w("l1_wq")[:, g * P:(g + 1) * P], yT[:, :],
                                       start=True, stop=True)
                    mm.then_inc(done["l1_q"], 1)
                    pe.wait_ge(done["l1_q_ready"], 1)
                    pe.wait_ge(done["l1_kv_ready"], 1)
                    pe.wait_ge(done["neg_ready"], 1)
                    pe_attention(pe, A1, V8x, masks=(negS, negT))
                    pe.wait_ge(done["normed"], 10)
                    turn_on(0)
                    for t in range(NT):
                        mm = pe.matmul(bank[1][:, t * P:(t + 1) * P], onT[:, t * P:(t + 1) * P], w("l1_wo"), start=True, stop=True)
                    mm.then_inc(done["projected"], 1)

                if STAGES > 3:
                    turn_ln(3)
                    pe.wait_ge(done["ln_yT"], 4)
                    for t in range(NT):
                        mm = pe.matmul(bank[2][:, t * 64:(t + 1) * 64], yT[:, t * P:(t + 1) * P], w("l1f_rw1"), start=True, stop=True)
                    mm.then_inc(done["l1f_r1"], 1)
                    pe.wait_ge(done["l1f_r1n"], 1)
                    for t in range(NT):
                        mm = pe.transpose(bank[3][0:64, t * P:(t + 1) * P], r1[:, t, :], ident)
                    mm.then_inc(done["l1f_r1turned"], 1)
                    pe.wait_ge(done["l1f_r1T"], 1)
                    for t in range(NT):
                        mm = pe.matmul(bank[2][:, 128 + t * E:128 + (t + 1) * E], r1T[:, t * P:(t + 1) * P], w("l1f_rw2", 64),
                                       start=True, stop=True)
                    mm.then_inc(done["l1f_logits"], 1)
                    pe.wait_ge(done["l1f_gates"], 1)
                    for t in range(NT):
                        mm = pe.transpose(bank[3][0:E, t * P:(t + 1) * P], gates[:, t, :], ident)
                    mm.then_inc(done["l1f_gturned"], 1)
                    pe.wait_ge(done["l1f_gT"], 1)
                    with pe.Fori(0, E) as e:
                        pe.wait_ge(done["expert_loaded"], e * 16 + 16)
                        for g in range(4):
                            mm = pe.matmul(bank[g // 2][:, (g % 2) * S:(g % 2 + 1) * S], expert[:, g * P:(g + 1) * P], yT[:, :],
                                           start=True, stop=True)
                        mm.then_inc(done["ex_q"], 1)
                        for g in range(4):
                            mm = pe.matmul(bank[2 + g // 2][:, (g % 2) * S:(g % 2 + 1) * S], expert[:, 512 + g * P:512 + (g + 1) * P],
                                           yT[:, :], start=True, stop=True)
                        mm.then_inc(done["ex_k"], 1)
                        for t in range(NT):
                            mm = pe.matmul(bank[4][:, t * D:(t + 1) * D], yT[:, t * P:(t + 1) * P], expert[:, 1024:1152],
                                           start=True, stop=True)
                        mm.then_inc(done["ex_v"], 1)
                        pe.wait_ge(done["ex_q_ready"], e + 1)
                        pe.wait_ge(done["ex_kv_ready"], e + 1)
                        pe_attention(pe, expert_attention(e), V8)
                        pe.wait_ge(done["normed"], e * 2 + 12)
                        for t in range(NT):
                            mm = pe.transpose(bank[5][:, t * P:(t + 1) * P], on[:, t, 0:D], ident)
                        mm.then_inc(done["ex_turned"], 1)
                        pe.wait_ge(done["ex_oT"], e + 1)
                        for t in range(NT):
                            mm = pe.matmul(bank[6][:, t * P:(t + 1) * P], onT[:, t * P:(t + 1) * P],
                                           W[:, bass.ds(e * D + WC["l1f_ow"][0], D)], start=True, stop=True)
                        mm.then_inc(done["ex_projected"], 1)
                        pe.wait_ge(done["ex_added"], e + 2)
                    for t in range(NT):
                        mm = pe.matmul(bank[6][:, t * P:(t + 1) * P], gatesT[:, t * P:(t + 1) * P], out_bias1[:, :],
                                       start=True, stop=True)
                    mm.then_inc(done["l1f_bias"], 1)

                if STAGES > 4:
                    turn_ln(4)
                    for g in range(2):
                        mm = pe.matmul(bank[1][:, g * S:(g + 1) * S], w("l2_wk")[:, g * P:(g + 1) * P], ctxT[:, :], start=True, stop=True)
                    for t in range(NT):
                        mm = pe.matmul(bank[2][:, t * D:(t + 1) * D], ctxT[:, t * P:(t + 1) * P], w("l2_wv"), start=True, stop=True)
                    mm.then_inc(done["l2_kv"], 1)
                    pe.wait_ge(done["ln_yT"], 5)
                    for g in range(2):
                        mm = pe.matmul(bank[0][:, g * S:(g + 1) * S], w("l2_wq")[:, g * P:(g + 1) * P], yT[:, :], start=True, stop=True)
                    mm.then_inc(done["l2_q"], 1)
                    pe.wait_ge(done["l2_q_ready"], 1)
                    pe.wait_ge(done["l2_kv_ready"], 1)
                    pe_attention(pe, A2, V16)

                if STAGES > 5:
                    turn_ln(5)
                    pe.wait_ge(done["ln_yT"], 6)
                    for t in range(NT):
                        mm = pe.matmul(bank[6][:, t * E:(t + 1) * E], yT[:, t * P:(t + 1) * P], w("l2f_router"), start=True, stop=True)
                    mm.then_inc(done["l2f_logits"], 1)
                    for e in range(E + 1):
                        if e < E:
                            if some(e - 1):
                                pe.wait_ge(done["l2f_gelu"], e - 1)
                            pe.matmul(bank[e % 2][:, 0:S], w("l2f_win")[:, e * P:(e + 1) * P], yT[:, :], start=True, stop=True)\
                                .then_inc(done["l2f_h"], 1)
                        if e >= 1:
                            k = e - 1
                            pe.wait_ge(done["l2f_gelu"], k + 1)
                            if some(k - 1):
                                pe.wait_ge(done["l2f_oadd"], k - 1)
                            for t in range(NT):
                                mm = pe.matmul(bank[2 + k % 2][:, t * P:(t + 1) * P], hT[:, k % 2, 0, t * P:(t + 1) * P],
                                               w("l2f_wout")[:, k * D:(k + 1) * D], start=True, stop=True)
                            mm.then_inc(done["l2f_o"], 1)
                    pe.wait_ge(done["l2f_gates"], 1)
                    for t in range(NT):
                        mm = pe.transpose(bank[4][0:E, t * P:(t + 1) * P], gates[:, t, :], ident)
                    mm.then_inc(done["l2f_gturned"], 1)
                    pe.wait_ge(done["l2f_gT"], 1)
                    for t in range(NT):
                        mm = pe.matmul(bank[5][:, t * P:(t + 1) * P], gatesT[:, t * P:(t + 1) * P], w("l2f_bout", E), start=True, stop=True)
                    mm.then_inc(done["projected"], 1)

                if STAGES > 6:
                    turn_ln(6)
                    pe.matmul(bank[1][:, 0:S], w("l3_wk"), ctxT[:, :], start=True, stop=True)
                    for t in range(NT):
                        mm = pe.matmul(bank[2][:, t * D:(t + 1) * D], ctxT[:, t * P:(t + 1) * P], w("l3_wv"), start=True, stop=True)
                    pe.wait_ge(done["ln_yT"], 7)
                    pe.matmul(bank[0][:, 0:S], w("l3_wq"), yT[:, :], start=True, stop=True).then_inc(done["l3_qkv"], 1)
                    pe.wait_ge(done["l3_qk_ready"], 2)
                    pe.wait_ge(done["l3_v_ready"], 1)
                    for t in range(NT):
                        mm = pe.matmul(bank[3][:, t * S:(t + 1) * S], qS[:, 0, t * P:(t + 1) * P], kS[:, 0, :], start=True, stop=True)
                    mm.then_inc(done["l3_s"], 1)
                    pe.wait_ge(done["l3_exp"], 2)
                    for t in range(NT):
                        for k in range(NT):
                            mm = pe.transpose(bank[4][:, k * S + t * P:k * S + (t + 1) * P], pr[:, t, k * P:(k + 1) * P], ident)
                    mm.then_inc(done["l3_pturned"], 1)
                    pe.wait_ge(done["l3_pT"], 1)
                    for k in range(NT):
                        mm = pe.matmul(bank[5][:, 0:S], acc[:, k, :], PT[:, 0, k * S:(k + 1) * S], start=k == 0, stop=k == NT - 1)
                    mm.then_inc(done["l3_ctx"], 1)
                    pe.wait_ge(done["l3_ctx_ready"], 1)
                    for t in range(NT):
                        mm = pe.matmul(bank[6][:, t * P:(t + 1) * P], onT[:, t * P:(t + 1) * P], w("l3_wo"), start=True, stop=True)
                    mm.then_inc(done["l3_out"], 1)

                if STAGES > 7:
                    turn_ln(7)
                    pe.wait_ge(done["ln_yT"], 8)
                    for part, name in enumerate(("l3f_wq", "l3f_wqs")):
                        for g in range(4):
                            mm = pe.matmul(bank[2 * part + g // 2][:, (g % 2) * S:(g % 2 + 1) * S], w(name)[:, g * P:(g + 1) * P], yT[:, :],
                                           start=True, stop=True)
                    mm.then_inc(done["rope_q"], 1)
                    for t in range(NT):
                        mm = pe.matmul(bank[6][:, t * D:(t + 1) * D], yT[:, t * P:(t + 1) * P], w("l3f_wv"), start=True, stop=True)
                    mm.then_inc(done["rope_v"], 1)
                    pe.wait_ge(done["rope_q_ready"], 1)
                    for part, name in enumerate(("l3f_wk", "l3f_wks")):
                        for g in range(4):
                            mm = pe.matmul(bank[2 * part + g // 2][:, (g % 2) * S:(g % 2 + 1) * S], w(name)[:, g * P:(g + 1) * P], yT[:, :],
                                           start=True, stop=True)
                    mm.then_inc(done["rope_k"], 1)
                    pe.wait_ge(done["rope_kv_ready"], 1)
                    pe_attention(pe, A3, V8, masks=(causS, causT))
                    pe.wait_ge(done["normed"], 30)
                    turn_on(1)
                    for t in range(NT):
                        mm = pe.matmul(bank[1][:, t * P:(t + 1) * P], onT[:, t * P:(t + 1) * P], w("l3f_wproj"), start=True, stop=True)
                    mm.then_inc(done["projected"], 1)
                    turn_ln(8)
                    pe.wait_ge(done["ln_yT"], 9)
                    for t in range(NT):
                        mm = pe.matmul(bank[6][:, t * E:(t + 1) * E], yT[:, t * P:(t + 1) * P], w("l3f_wgate"), start=True, stop=True)
                    mm.then_inc(done["l3f_logits"], 1)
                    pe.wait_ge(done["l3f_top"], 1)
                    pe.matmul(bank[7][:, 0:E], c("upto"), coef[:, 0:E], start=True, stop=True)
                    pe.matmul(bank[7][:, E:2 * E], c("ones"), coef[:, 0:E], start=True, stop=False)
                    pe.matmul(bank[7][:, E:2 * E], c("upto"), coef[:, E:2 * E], start=False, stop=True)
                    pe.matmul(bank[7][:, 2 * E:3 * E], c("ones"), coef[:, 0:E], start=True, stop=False)
                    pe.matmul(bank[7][:, 2 * E:3 * E], c("ones"), coef[:, E:2 * E], start=False, stop=True)\
                        .then_inc(done["l3f_count"], 1)
                    for e in range(E + 1):
                        if e < E:
                            if some(4 * (e - 1)):
                                pe.wait_ge(done["l3f_gelu"], 4 * (e - 1))
                            for f in range(4):
                                pe.matmul(bank[2 * (e % 2) + f // 2][:, (f % 2) * S:(f % 2 + 1) * S],
                                          w("l3f_w1")[:, (e * 4 + f) * P:(e * 4 + f + 1) * P], yT[:, :],
                                          start=True, stop=True).then_inc(done["l3f_h"], 1)
                        if e >= 1:
                            k = e - 1
                            pe.wait_ge(done["l3f_gelu"], 4 * (k + 1))
                            if some(k - 1):
                                pe.wait_ge(done["l3f_oadd"], k - 1)
                            for t in range(NT):
                                for f in range(4):
                                    mm = pe.matmul(bank[4 + k % 2][:, t * P:(t + 1) * P], hT[:, k % 2, f, t * P:(t + 1) * P],
                                                   w("l3f_w2")[:, (k * 4 + f) * D:(k * 4 + f + 1) * D], start=f == 0, stop=f == 3)
                            mm.then_inc(done["l3f_o"], 1)
                    pe.wait_ge(done["l3f_gates"], 1)
                    for t in range(NT):
                        mm = pe.transpose(bank[6][0:E, t * P:(t + 1) * P], gates[:, t, :], ident)
                    mm.then_inc(done["l3f_gturned"], 1)
                    pe.wait_ge(done["l3f_gT"], 1)
                    for t in range(NT):
                        mm = pe.matmul(bank[0][:, t * P:(t + 1) * P], gatesT[:, t * P:(t + 1) * P], w("l3f_b2", E), start=True, stop=True)
                    mm.then_inc(done["projected"], 1)
                end_of_batch(pe)

        @block.scalar
        def _(act):
            act.wait_ge(setup["weights_loaded"], 16)
            act.wait_ge(setup["consts_loaded"], 16)
            act.activation(tanh_gain[:, :], w("gains"), ACT.Tanh).then_inc(setup["setup_act"], 1)
            with act.Fori(0, B) as b:
                def copy_ln(n, scale=None, bias=None):
                    act.wait_ge(done["ln_turned"], n + 1)
                    if scale is None:
                        act.activation(yT[:, :], MISC[:, 0:S], ACT.Copy).then_inc(done["ln_yT"], 1)
                    else:
                        act.activation(yT[:, :], MISC[:, 0:S], ACT.Identity, bias=bias, scale=scale).then_inc(done["ln_yT"], 1)

                def copy_on(n):
                    act.wait_ge(done["on_turned"], n + 1)
                    act.activation(onT[:, :], bank[0][:, 0:S], ACT.Copy).then_inc(done["onT_ready"], 1)

                act.wait_ge(done["ctx_turned"], 1)
                act.activation(ctxT[:, :], bank[6][:, 0:S], ACT.Copy).then_inc(done["ctxT_ready"], 1)
                copy_ln(0)
                act.wait_ge(done["l0_absf"], 1)
                act.activation(l0r[0:4, 3, :], l0r[0:4, 2, :], ACT.Exp, scale=-1.0).then_inc(done["act_step"], 1)
                act.wait_ge(done["act_step"], 1)
                act.activation(l0r[0:4, 4, :], l0r[0:4, 3, :], ACT.Ln, bias=1.0).then_inc(done["l0_softplus"], 1)
                act.wait_ge(done["l0_negm"], 1)
                act.activation(dn[:, 0, :], mcol[:, :, :].rearrange("p t h -> p (t h)"), ACT.Exp).then_inc(done["l0_expm"], 1)
                act.wait_ge(done["l0_args"], 1)
                act.activation(Dm[:, :, :], Dm[:, :, :], ACT.Exp).then_inc(done["l0_decay"], 1)

                if STAGES > 1:
                    copy_ln(1)
                    act.wait_ge(done["l0f_gcopied"], 1)
                    act.activation(gsig[:, :], gv[:, :], ACT.Exp, scale=-1.0).then_inc(done["l0f_sig"], 1)
                    for t in range(NT):
                        act.wait_ge(done["l0f_pv"], t + 1)
                        act.activation(pv[:, t, :], bank[1 + t][:, :], ACT.Copy).then_inc(done["l0f_pvcopied"], 1)

                    def copy_qk(first, last):
                        for h in range(first, min(last, 16)):
                            act.wait_ge(done["l0f_qk"], h + 1)
                            act.activation(qk64[0:64, h % 4, :], bank[2][0:64, :], ACT.Copy).then_inc(done["l0f_qk_ready"], 1)

                    act_attention(act, A0, before=lambda h: copy_qk(h + 3 if h else 0, h + 4))
                    for t in range(NT):
                        act.wait_ge(done["l0f_gturned"], t + 1)
                        act.activation(GT[:, :, t * P:(t + 1) * P], bank[t][:, :].rearrange("p (q s) -> p q s", q=4), ACT.Copy)\
                            .then_inc(done["l0f_gT"], 1)

                if STAGES > 2:
                    copy_ln(2)
                    act.wait_ge(done["l1_q"], 1)
                    for g in range(4):
                        a = act.activation(qS[:, g, :], bank[g // 2][:, (g % 2) * S:(g % 2 + 1) * S], ACT.Identity,
                                           bias=w("l1_qb")[:, g:g + 1])
                    a.then_inc(done["l1_q_ready"], 1)
                    act_attention(act, A1)
                    copy_on(0)

                if STAGES > 3:
                    copy_ln(3)
                    act.wait_ge(done["l1f_r1turned"], 1)
                    act.activation(r1T, bank[3][0:64, 0:S], ACT.Copy).then_inc(done["l1f_r1T"], 1)
                    act.wait_ge(done["l1f_rmax"], 1)
                    act.activation(gv[:, 0:NT * E], gv[:, 0:NT * E], ACT.Exp).then_inc(done["l1f_rexp"], 1)
                    act.wait_ge(done["l1f_gturned"], 1)
                    act.activation(gatesT[:, :], bank[3][0:E, 0:S], ACT.Copy).then_inc(done["l1f_gT"], 1)
                    with act.Fori(0, E) as e:
                        act.wait_ge(done["ex_q"], e + 1)
                        for g in range(4):
                            a = act.activation(qS[:, g, :], bank[g // 2][:, (g % 2) * S:(g % 2 + 1) * S], ACT.Identity,
                                               bias=expert[:, 1152 + g:1153 + g])
                        a.then_inc(done["ex_q_ready"], 1)
                        act_attention(act, expert_attention(e))
                        act.wait_ge(done["ex_turned"], e + 1)
                        act.activation(onT[:, :], bank[5][:, 0:S], ACT.Copy).then_inc(done["ex_oT"], 1)

                if STAGES > 4:
                    copy_ln(4)
                    act.wait_ge(done["l2_q"], 1)
                    act.activation(qS[:, 0:2, :], bank[0][:, :].rearrange("p (g s) -> p g s", g=2), ACT.Copy).then_inc(done["l2_q_ready"], 1)
                    act_attention(act, A2)

                if STAGES > 5:
                    copy_ln(5)
                    act.wait_ge(done["l2f_rmax"], 1)
                    act.activation(gv[:, 0:NT * E], gv[:, 0:NT * E], ACT.Exp).then_inc(done["l2f_rexp"], 1)
                    for e in range(E):
                        act.wait_ge(done["l2f_h"], e + 1)
                        if some(e - 1):
                            act.wait_ge(done["l2f_o"], e - 1)
                        act.activation(hT[:, e % 2, 0, :], bank[e % 2][:, 0:S], ACT.Gelu_apprx_tanh, bias=w("l2f_bin")[:, e:e + 1])\
                            .then_inc(done["l2f_gelu"], 1)
                    act.wait_ge(done["l2f_gturned"], 1)
                    act.activation(gatesT[:, :], bank[4][0:E, 0:S], ACT.Copy).then_inc(done["l2f_gT"], 1)

                if STAGES > 6:
                    copy_ln(6)
                    act.wait_ge(done["l3_qkv"], 1)
                    act.activation(qS[:, 0, :], bank[0][:, 0:S], ACT.Identity, bias=w("l3_bq")).then_inc(done["l3_qk_ready"], 1)
                    act.activation(kS[:, 0, :], bank[1][:, 0:S], ACT.Copy).then_inc(done["l3_qk_ready"], 1)
                    act.wait_ge(done["l3_smax"], 1)
                    for t in range(NT):
                        act.activation(pr[:, t, :], bank[3][:, t * S:(t + 1) * S], ACT.Exp, scale=D ** -0.5, bias=gs[:, 1, t:t + 1],
                                       accum_out=gs[:, 2, t:t + 1]).then_inc(done["l3_exp"], 1)
                    act.wait_ge(done["l3_pturned"], 1)
                    act.activation(PT[:, 0, :], bank[4][:, :], ACT.Copy).then_inc(done["l3_pT"], 1)
                    act.wait_ge(done["l3_ctx"], 1)
                    act.activation(onT[:, :], bank[5][:, 0:S], ACT.Copy).then_inc(done["l3_ctx_ready"], 1)

                if STAGES > 7:
                    copy_ln(7, w("l3f_ln")[:, 0:1], w("l3f_ln")[:, 1:2])
                    act_attention(act, A3)
                    copy_on(1)
                    copy_ln(8, w("l3f_ln")[:, 2:3], w("l3f_ln")[:, 3:4])
                    act.wait_ge(done["l3f_rmax"], 1)
                    act.activation(gv[:, 0:NT * E], gv[:, 0:NT * E], ACT.Exp).then_inc(done["l3f_rexp"], 1)
                    for e in range(E):
                        if some(e - 1):
                            act.wait_ge(done["l3f_o"], e - 1)
                        for f in range(4):
                            act.wait_ge(done["l3f_h"], 4 * e + f + 1)
                            if f % 2 == 0:
                                act.wait_ge(done["l3f_h"], 4 * e + f + 2)
                            act.activation(hT[:, e % 2, f, :], bank[2 * (e % 2) + f // 2][:, (f % 2) * S:(f % 2 + 1) * S], ACT.Gelu,
                                           bias=w("l3f_b1")[:, e * 4 + f:e * 4 + f + 1]).then_inc(done["l3f_gelu"], 1)
                    act.wait_ge(done["l3f_gturned"], 1)
                    act.activation(gatesT[:, :], bank[6][0:E, 0:S], ACT.Copy).then_inc(done["l3f_gT"], 1)
                end_of_batch(act)

        @block.gpsimd
        def _(pool):
            pool.memset(minus_half[:, :], -0.5).then_inc(setup["setup_pool"], 1)
            pool.wait_ge(setup["setup_pool"], 1)
            with pool.Fori(0, B) as b:
                steps = [0]

                def link(ins):
                    steps[0] += 1
                    ins.then_inc(done["pool_step"], 1)
                    pool.wait_ge(done["pool_step"], steps[0])

                def inv_sqrt(out, var, eps, n):
                    link(pool.tensor_scalar(out, var, eps, None, ALU.add))
                    return pool.tensor_tensor(out, out, minus_half[:, 0:n], ALU.pow)

                def ln_rstd(n, eps=1e-5):
                    pool.wait_ge(done["ln_var"], n + 1)
                    inv_sqrt(rstd[:, :], mv[:, :, 1], eps, NT).then_inc(done["ln_rstd"], 1)

                pool.wait_ge(done["x_loaded"], 16)
                pool.memset(V64[:, :, :, 64:65], 1.0).then_inc(done["filled"], 1)
                pool.wait_ge(done["filled"], 1)
                pool.memset(qk64[64:65, :, S:2 * S], 1.0).then_inc(done["filled"], 1)
                pool.wait_ge(done["filled"], 2)
                ln_rstd(0)
                pool.wait_ge(done["l0_decay"], 1)
                for a in (0, S):
                    pool.tensor_tensor(Dm[:, :, a:a + P], Dm[:, :, a:a + P], c("upto").unsqueeze(1).broadcast_to([P, 4, P]), ALU.mult)\
                        .then_inc(done["l0_decay_masked"], 1)
                pool.wait_ge(done["l0_hstat"], 1)
                inv_sqrt(rstd8[:, :], mv8[:, :, 1], 1e-6, 8).then_inc(done["l0_hrstd"], 1)

                def pool_mix(coef_of, values, dst, signal, n_in):
                    n_out = 32 // n_in
                    m = mixP.rearrange("p (o i d) -> p o i d", i=n_in, d=64)
                    link(pool.tensor_tensor(m, coef_of, values, ALU.mult))
                    k = n_in // 2
                    while k > 1:
                        link(pool.tensor_tensor(m[:, :, 0:k, :], m[:, :, 0:k, :], m[:, :, k:2 * k, :], ALU.add))
                        k //= 2
                    link(pool.tensor_tensor(dst, m[:, :, 0, :], m[:, :, 1, :], ALU.add))
                    pool.sem_inc(done[signal], 1)

                if STAGES > 1:
                    ln_rstd(1)
                    pool.wait_ge(done["l0f_coef"], 1)
                    pool.wait_ge(done["l0f_pvcopied"], 2)
                    co = coef[:, :].rearrange("p (t k h e) -> p t k h e", t=NT, k=2, h=16)
                    for part in range(4):
                        hs = slice(4 * part, 4 * part + 4)
                        pool_mix(co[:, 1, 0, hs, :].unsqueeze(3).broadcast_to([P, 4, 8, 64]),
                                 pv[:, 1, :].rearrange("p (e d) -> p e d", e=8).unsqueeze(1).broadcast_to([P, 4, 8, 64]),
                                 V64[:, 1, hs, 0:64], "l0f_vpool", 8)
                    pool.wait_ge(done["l0f_vdve"], 4)
                    pool.wait_ge(done["normed"], 8)
                    for part in range(4):
                        es = slice(2 * part, 2 * part + 2)
                        pool_mix(co[:, 1, 1, :, es].rearrange("p h e -> p e h").unsqueeze(3).broadcast_to([P, 2, 16, 64]),
                                 on[:, 1, :].rearrange("p (h d) -> p h d", h=16).unsqueeze(1).broadcast_to([P, 2, 16, 64]),
                                 pv[:, 1, :].rearrange("p (e d) -> p e d", e=8)[:, es, :], "l0f_gpool", 16)
                if STAGES > 2:
                    pool.memset(V8x, 0.0).then_inc(done["filled"], 1)
                    ln_rstd(2)
                    pool.wait_ge(done["gp_loaded"], 16)
                    pool_attention(pool, A1)
                if STAGES > 3:
                    ln_rstd(3)
                    pool.wait_ge(done["l1f_rvar"], 1)
                    inv_sqrt(rstd[:, :], mv[:, :, 1], 1e-5, NT).then_inc(done["l1f_rrstd"], 1)
                if STAGES > 4:
                    ln_rstd(4)
                if STAGES > 5:
                    ln_rstd(5)
                if STAGES > 6:
                    ln_rstd(6)
                if STAGES > 7:
                    ln_rstd(7)
                    ln_rstd(8)
                    ln_rstd(9)
                end_of_batch(pool)

        @block.vector
        def _(dve):
            n_setup = [0]

            def slink(ins):
                n_setup[0] += 1
                ins.then_inc(setup["setup_dve"], 1)

            dve.wait_ge(setup["consts_loaded"], 16)
            slink(dve.tensor_copy(ident_bf[:, :], ident))
            dve.wait_ge(setup["causal_loaded"], 16)
            slink(dve.tensor_copy(causS[:, :, :], mixD[:, 0:512].rearrange("p (t s) -> p t s", t=NT)))
            slink(dve.tensor_copy(causT[:, :, :], mixD[:, 512:1024].rearrange("p (t s) -> p t s", t=NT)))
            for k in (8, 16, 64):
                slink(dve.memset(negmax[k][:, :, :, :], 0.0))
            for V, k in ((V8, 8), (V16, 16)):
                slink(dve.memset(V[:, :, :, :], 0.0))
                dve.wait_ge(setup["setup_dve"], n_setup[0])
                slink(dve.memset(V[:, :, :, k:k + 1], 1.0))
            slink(dve.memset(Vm[:, :, :, 32:33], 1.0))
            slink(dve.memset(carry[:, :], 0.0))
            assert n_setup[0] == SETUP_DVE, n_setup[0]
            dve.wait_ge(setup["setup_dve"], n_setup[0])
            dve.wait_ge(setup["setup_pe"], 1)
            dve.wait_ge(setup["weights_loaded"], 16)
            dve.wait_ge(setup["setup_act"], 1)
            dve.tensor_tensor(out_bias1[:, :], bank[0][0:E, 0:D], w("l1f_ob", E), ALU.add).then_inc(setup["setup_dve"], 1)
            dve.wait_ge(setup["setup_dve"], n_setup[0] + 1)

            with dve.Fori(0, B) as b:
                steps = [0]

                def link(ins):
                    steps[0] += 1
                    ins.then_inc(done["dve_step"], 1)
                    dve.wait_ge(done["dve_step"], steps[0])

                def layernorm(n, src, dst=y):
                    for t in range(NT):
                        ins = dve.bn_stats(bn[:, t, :], src[:, t, :])
                        if t == 0:
                            ins.then_inc(done["dve_step"], 1)
                            steps[0] += 1
                        else:
                            link(ins)
                    for t in range(NT):
                        ins = dve.bn_aggr(mv[:, t, :], bn[:, t, :])
                    ins.then_inc(done["ln_var"], 1)
                    dve.wait_ge(done["ln_rstd"], n + 1)
                    dve.wait_ge(done["ln_var"], n + 1)
                    for t in range(NT):
                        ins = dve.tensor_scalar(dst[:, t, :], src[:, t, :], mv[:, t, 0:1], rstd[:, t:t + 1], ALU.subtract, ALU.mult)
                        if t == 0:
                            ins.then_inc(done["dve_step"], 1)
                            steps[0] += 1
                    return ins

                def add_to_x(src, k):
                    link(dve.scalar_tensor_tensor(xs[:, :, :], src, tanh_gain[:, k:k + 1], xs[:, :, :], ALU.mult, ALU.add))

                def top2(v, n, mask):
                    v3 = v.rearrange("p (n e) -> p n e", e=8)
                    A_, B_, C_, D_ = (t2[:, k, 0:8 * n].rearrange("p (n e) -> p n e", e=8) for k in range(4))
                    m, k1 = t2s[:, 0, 0:n].unsqueeze(2), t2s[:, 1, 0:n].unsqueeze(2)
                    rank = c("rank").unsqueeze(1).broadcast_to([P, n, 8])
                    mask3 = mask.rearrange("p (n e) -> p n e", e=8)
                    src = v3
                    for r, hot in enumerate((A_, B_)):
                        link(dve.tensor_reduce(m, src, X_AXIS, ALU.max))
                        link(dve.tensor_tensor(C_, src, m.broadcast_to([P, n, 8]), ALU.is_ge))
                        link(dve.tensor_tensor(C_, C_, rank, ALU.mult))
                        link(dve.tensor_reduce(k1, C_, X_AXIS, ALU.max))
                        link(dve.tensor_tensor(hot, C_, k1.broadcast_to([P, n, 8]), ALU.is_equal))
                        if r == 0:
                            link(dve.scalar_tensor_tensor(D_, hot, -BIG, v3, ALU.mult, ALU.add))
                            src = D_
                    link(dve.tensor_tensor(mask3, A_, B_, ALU.add))

                def routing(name, logits, bias=None):
                    dve.wait_ge(done[f"{name}_logits"], 1)
                    L = gv[:, 0:NT * E]
                    L3 = L.rearrange("p (t e) -> p t e", e=E)
                    if bias is None:
                        link(dve.tensor_copy(L, logits))
                    else:
                        link(dve.tensor_tensor(L3, logits.rearrange("p (t e) -> p t e", e=E), bias.unsqueeze(1).broadcast_to([P, NT, E]), ALU.add))
                    top2(L, NT, coef[:, 0:NT * E])
                    link(dve.tensor_reduce(gs[:, 0, :].unsqueeze(2), L3, X_AXIS, ALU.max))
                    dve.tensor_tensor(L3, L3, gs[:, 0, :].unsqueeze(2).broadcast_to([P, NT, E]), ALU.subtract)\
                        .then_inc(done[f"{name}_rmax"], 1)
                    dve.wait_ge(done[f"{name}_rexp"], 1)
                    return L3

                dve.wait_ge(done["x_loaded"], 16)
                layernorm(0, xs).then_inc(done["ln_y"], 1)
                dve.wait_ge(done["ctx_loaded"], 16)
                link(dve.tensor_copy(Vm[:, :, :, 0:32], ctxs[:, :, :].rearrange("p t (h d) -> p t h d", h=4)))
                dve.wait_ge(done["l0_gates"], 1)
                R = l0r[0:4, :, :]
                link(dve.tensor_scalar(R[:, 0, :], bank[4][0:4, 0:S], w("l0_bias", 4)[:, 0:1], None, ALU.add))
                link(dve.tensor_scalar(R[:, 1, :], bank[4][0:4, S:2 * S], w("l0_bias", 4)[:, 1:2], None, ALU.add))
                dve.scalar_tensor_tensor(R[:, 2, :], R[:, 1, :], -1.0, R[:, 1, :], ALU.mult, ALU.max).then_inc(done["l0_absf"], 1)
                dve.wait_ge(done["l0_softplus"], 1)
                link(dve.scalar_tensor_tensor(R[:, 5, :], R[:, 1, :], 0.0, R[:, 4, :], ALU.min, ALU.subtract))
                link(dve.tensor_tensor_scan(R[:, 6, :], c("ones", 4)[:, 0:1].broadcast_to([4, S]), R[:, 5, :], 0.0, ALU.mult, ALU.add))
                link(dve.tensor_tensor(R[:, 8, :], R[:, 0, :], R[:, 6, :], ALU.subtract))
                link(dve.tensor_tensor_scan(R[:, 7, :], c("ones", 4)[:, 0:1].broadcast_to([4, S]), R[:, 8, :], -3.0e38, ALU.mult, ALU.max))
                link(dve.tensor_scalar(R[:, 9, :], R[:, 7, :], -1.0, None, ALU.mult))
                dve.tensor_tensor(R[:, 10, :], R[:, 9, :], R[:, 6, :], ALU.subtract).then_inc(done["l0_rows"], 1)
                dve.wait_ge(done["l0_cols_turned"], 1)
                link(dve.tensor_copy(gcol[:, :, :], bank[5][:, 0:8].rearrange("p (t h) -> p t h", t=NT)))
                dve.tensor_copy(mcol[:, :, :], bank[5][:, 8:16].rearrange("p (t h) -> p t h", t=NT)).then_inc(done["l0_negm"], 1)
                dve.wait_ge(done["l0_spread"], 1)
                for h in range(4):
                    src = bank[6 + h // 2][:, (h % 2) * S:(h % 2 + 1) * S]
                    dve.tensor_scalar(Dm[:, h, 0:S], src, gcol[:, 0, h:h + 1], 0.0, ALU.add, ALU.min)
                    ins = dve.tensor_scalar(Dm[:, h, S:S + P], src[:, P:S], gcol[:, 1, h:h + 1], 0.0, ALU.add, ALU.min)
                ins.then_inc(done["l0_args"], 1)
                dve.wait_ge(done["l0_qk"], 1)
                dve.wait_ge(done["l0_decay"], 1)
                dve.wait_ge(done["l0_decay_masked"], 2)
                for h in range(4):
                    dve.scalar_tensor_tensor(Cm[:, h, :], bank[h][:, 0:384], 32 ** -0.5, Dm[:, h, :], ALU.mult, ALU.mult)\
                        .then_inc(done["l0_cm"], 1)
                dve.wait_ge(done["l0_expm"], 1)
                for t in range(NT):
                    dve.wait_ge(done["l0_h"], t + 1)
                    T = bank[4 + t][:, 0:132].rearrange("p (h c) -> p h c", c=33)
                    d = dn[:, 1, 4 * t:4 * t + 4]
                    link(dve.tensor_copy(d.unsqueeze(2), T[:, :, 32:33]))
                    link(dve.scalar_tensor_tensor(dn[:, 2, 0:4], d, -1.0, d, ALU.mult, ALU.max))
                    link(dve.tensor_tensor(dn[:, 2, 0:4], dn[:, 2, 0:4], dn[:, 0, 4 * t:4 * t + 4], ALU.max))
                    link(dve.tensor_scalar(dn[:, 2, 0:4], dn[:, 2, 0:4], 1e-6, None, ALU.add))
                    link(dve.reciprocal(dn[:, 3, 0:4], dn[:, 2, 0:4]))
                    link(dve.tensor_tensor(hh[:, t, :, :], T[:, :, 0:32], dn[:, 3, 0:4].unsqueeze(2).broadcast_to([P, 4, 32]), ALU.mult))
                H = hh[:, :, :, :].rearrange("p t h d -> p (t h) d")
                for k in range(8):
                    ins = dve.bn_stats(bn8[:, k, :], H[:, k, :])
                link(ins)
                for k in range(8):
                    ins = dve.bn_aggr(mv8[:, k, :], bn8[:, k, :])
                ins.then_inc(done["l0_hstat"], 1)
                dve.wait_ge(done["l0_hrstd"], 1)
                dve.wait_ge(done["l0_hstat"], 1)
                link(dve.tensor_tensor(H, H, mv8[:, :, 0:1].broadcast_to([P, 8, 32]), ALU.subtract))
                link(dve.tensor_tensor(H, H, rstd8[:, :].unsqueeze(2).broadcast_to([P, 8, 32]), ALU.mult))
                H2 = hh[:, :, :, :].rearrange("p t h d -> p t (h d)")
                link(dve.tensor_tensor(H2, H2, w("l0_outnorm").unsqueeze(1).broadcast_to([P, NT, D]), ALU.mult))
                add_to_x(H2, 0)

                def dve_mix(coef_of, values, dst, signal, n_in):
                    m = mixD.rearrange("p (o i d) -> p o i d", i=n_in, d=64)
                    link(dve.tensor_tensor(m, coef_of, values, ALU.mult))
                    dve.tensor_reduce(dst.unsqueeze(3), m.rearrange("p o i d -> p o d i"), X_AXIS, ALU.add).then_inc(done[signal], 1)

                if STAGES > 1:
                    layernorm(1, xs).then_inc(done["ln_y"], 1)
                    dve.wait_ge(done["l0f_gates"], 1)
                    dve.tensor_copy(gv[:, :], bank[0][:, :]).then_inc(done["l0f_gcopied"], 1)
                    dve.wait_ge(done["l0f_gcopied"], 1)
                    top2(gv[:, :], 64, coef[:, :])
                    dve.wait_ge(done["l0f_sig"], 1)
                    link(dve.tensor_scalar(gsig[:, :], gsig[:, :], 1.0, None, ALU.add))
                    link(dve.reciprocal(gsig[:, :], gsig[:, :]))
                    for t in range(NT):
                        a = coef[:, t * 256:t * 256 + 128]
                        ins = dve.tensor_tensor(a, a, gsig[:, t * 256:t * 256 + 128], ALU.mult)
                    ins.then_inc(done["l0f_coef"], 1)
                    dve.wait_ge(done["l0f_coef"], 1)
                    dve.wait_ge(done["l0f_pvcopied"], 2)
                    co = coef[:, :].rearrange("p (t k h e) -> p t k h e", t=NT, k=2, h=16)
                    for part in range(4):
                        hs = slice(4 * part, 4 * part + 4)
                        if some(part):
                            dve.wait_ge(done["l0f_vdve"], part)
                        dve_mix(co[:, 0, 0, hs, :].unsqueeze(3).broadcast_to([P, 4, 8, 64]),
                                pv[:, 0, :].rearrange("p (e d) -> p e d", e=8).unsqueeze(1).broadcast_to([P, 4, 8, 64]),
                                V64[:, 0, hs, 0:64], "l0f_vdve", 8)
                    dve_attention(dve, A0, link)
                    dve.wait_ge(done["normed"], 8)
                    dve.wait_ge(done["l0f_vdve"], 4)
                    for part in range(4):
                        es = slice(2 * part, 2 * part + 2)
                        if some(part):
                            dve.wait_ge(done["l0f_gdve"], part)
                        dve_mix(co[:, 0, 1, :, es].rearrange("p h e -> p e h").unsqueeze(3).broadcast_to([P, 2, 16, 64]),
                                on[:, 0, :].rearrange("p (h d) -> p h d", h=16).unsqueeze(1).broadcast_to([P, 2, 16, 64]),
                                pv[:, 0, :].rearrange("p (e d) -> p e d", e=8)[:, es, :], "l0f_gdve", 16)
                    dve.wait_ge(done["projected"], 1)
                    add_to_x(bank[2][:, 0:S].rearrange("p (t d) -> p t d", t=NT), 1)

                if STAGES > 2:
                    layernorm(2, xs).then_inc(done["ln_y"], 1)
                    dve.wait_ge(done["mask_loaded"], 16)
                    dve.wait_ge(done["maskT_loaded"], 16)
                    for src, dst in ((mask_i, negS), (maskT_i, negT)):
                        ins = dve.tensor_scalar(dst[:, :, :], src, 1.0, -NEG_MASK * 8 ** 0.5, ALU.subtract, ALU.mult)
                    ins.then_inc(done["neg_ready"], 1)
                    dve.wait_ge(done["l1_k"], 1)
                    for g in range(4):
                        dve.tensor_scalar(kS[:, g, :], bank[3 + g // 2][:, (g % 2) * S:(g % 2 + 1) * S], w("l1_kb")[:, g:g + 1], None, ALU.add)
                    dve.wait_ge(done["l1_v"], 1)
                    dve.wait_ge(done["filled"], 3)
                    for t in range(NT):
                        ins = dve.tensor_tensor(V8x[:, t, :, 0:8], bank[5][:, t * D:(t + 1) * D].rearrange("p (h d) -> p h d", d=8),
                                                w("l1_vb").rearrange("p (h d) -> p h d", d=8), ALU.add)
                    ins.then_inc(done["l1_kv_ready"], 1)
                    dve_attention(dve, A1, link)
                    dve.wait_ge(done["projected"], 2)
                    link(dve.tensor_tensor(tmp[:, :, :], bank[1][:, 0:S].rearrange("p (t d) -> p t d", t=NT),
                                           w("l1_bo").unsqueeze(1).broadcast_to([P, NT, D]), ALU.add))
                    add_to_x(tmp[:, :, :], 2)

                if STAGES > 3:
                    layernorm(3, xs).then_inc(done["ln_y"], 1)
                    dve.memset(acc[:, :, :], 0.0).then_inc(done["ex_added"], 1)
                    dve.wait_ge(done["l1f_r1"], 1)
                    link(dve.tensor_tensor(r1, bank[2][:, 0:128].rearrange("p (t d) -> p t d", t=NT),
                                           w("l1f_rb1").unsqueeze(1).broadcast_to([P, NT, 64]), ALU.add))
                    for t in range(NT):
                        link(dve.bn_stats(bn[:, t, :], r1[:, t, :]))
                    for t in range(NT):
                        ins = dve.bn_aggr(mv[:, t, :], bn[:, t, :])
                    ins.then_inc(done["l1f_rvar"], 1)
                    dve.wait_ge(done["l1f_rrstd"], 1)
                    dve.wait_ge(done["l1f_rvar"], 1)
                    for t in range(NT):
                        link(dve.tensor_scalar(r1[:, t, :], r1[:, t, :], mv[:, t, 0:1], rstd[:, t:t + 1], ALU.subtract, ALU.mult))
                    link(dve.tensor_tensor(r1, r1, w("l1f_lng").unsqueeze(1).broadcast_to([P, NT, 64]), ALU.mult))
                    link(dve.tensor_tensor(r1, r1, w("l1f_lnb").unsqueeze(1).broadcast_to([P, NT, 64]), ALU.add))
                    dve.tensor_scalar(r1, r1, 0.0, None, ALU.max).then_inc(done["l1f_r1n"], 1)
                    L3 = routing("l1f", bank[2][:, 128:128 + NT * E], w("l1f_rb2"))
                    M3 = coef[:, 0:NT * E].rearrange("p (t e) -> p t e", e=E)
                    link(dve.tensor_tensor(gates[:, :, :], L3, M3, ALU.mult))
                    link(dve.tensor_reduce(gs[:, 1, :].unsqueeze(2), gates[:, :, :], X_AXIS, ALU.add))
                    link(dve.reciprocal(gs[:, 2, :], gs[:, 1, :]))
                    dve.tensor_tensor(gates[:, :, :], gates[:, :, :], gs[:, 2, :].unsqueeze(2).broadcast_to([P, NT, E]), ALU.mult)\
                        .then_inc(done["l1f_gates"], 1)
                    dve.wait_ge(done["l1f_gates"], 1)
                    with dve.Fori(0, E) as e:
                        per_expert = 4
                        inner = [0]

                        def link_e(ins):
                            inner[0] += 1
                            ins.then_inc(done["dve_expert_step"], 1)
                            dve.wait_ge(done["dve_expert_step"], e * per_expert + inner[0])

                        dve.wait_ge(done["ex_k"], e + 1)
                        for g in range(4):
                            dve.tensor_scalar(kS[:, g, :], bank[2 + g // 2][:, (g % 2) * S:(g % 2 + 1) * S], expert[:, 1156 + g:1157 + g],
                                              None, ALU.add)
                        dve.wait_ge(done["ex_v"], e + 1)
                        dve.tensor_copy(V8[:, :, :, 0:8], bank[4][:, 0:S].rearrange("p (t h d) -> p t h d", t=NT, d=8))\
                            .then_inc(done["ex_kv_ready"], 1)
                        dve_attention(dve, expert_attention(e), link_e,
                                      gate=lambda t: gates[:, t, bass.ds(e, 1)])
                        dve.wait_ge(done["ex_projected"], e + 1)
                        dve.wait_ge(done["ex_added"], e + 1)
                        dve.tensor_tensor(acc[:, :, :], acc[:, :, :], bank[6][:, 0:S].rearrange("p (t d) -> p t d", t=NT), ALU.add)\
                            .then_inc(done["ex_added"], 1)
                        assert inner[0] == per_expert, inner[0]
                    dve.wait_ge(done["ex_added"], E + 1)
                    dve.wait_ge(done["l1f_bias"], 1)
                    link(dve.tensor_tensor(acc[:, :, :], acc[:, :, :], bank[6][:, 0:S].rearrange("p (t d) -> p t d", t=NT), ALU.add))
                    add_to_x(acc[:, :, :], 3)

                if STAGES > 4:
                    layernorm(4, xs).then_inc(done["ln_y"], 1)
                    dve.wait_ge(done["l2_kv"], 1)
                    dve.tensor_scalar(kS[:, 0:2, :], bank[1][:, :].rearrange("p (g s) -> p g s", g=2), c("kones16"), None, ALU.add)
                    dve.tensor_copy(V16[:, :, :, 0:16], bank[2][:, 0:S].rearrange("p (t h d) -> p t h d", t=NT, d=16))\
                        .then_inc(done["l2_kv_ready"], 1)
                    dve_attention(dve, A2, link)
                    dve.wait_ge(done["normed"], A2.nb + 2)
                    add_to_x(on[:, :, 0:D], 4)

                if STAGES > 5:
                    layernorm(5, xs).then_inc(done["ln_y"], 1)
                    L3 = routing("l2f", bank[6][:, 0:NT * E])
                    M3 = coef[:, 0:NT * E].rearrange("p (t e) -> p t e", e=E)
                    link(dve.tensor_reduce(gs[:, 1, :].unsqueeze(2), L3, X_AXIS, ALU.add))
                    link(dve.reciprocal(gs[:, 2, :], gs[:, 1, :]))
                    link(dve.tensor_tensor(gates[:, :, :], L3, M3, ALU.mult))
                    dve.tensor_tensor(gates[:, :, :], gates[:, :, :], gs[:, 2, :].unsqueeze(2).broadcast_to([P, NT, E]), ALU.mult)\
                        .then_inc(done["l2f_gates"], 1)
                    dve.wait_ge(done["l2f_gates"], 1)
                    link(dve.memset(acc[:, :, :], 0.0))
                    for e in range(E):
                        dve.wait_ge(done["l2f_o"], e + 1)
                        if some(e):
                            dve.wait_ge(done["l2f_oadd"], e)
                        for t in range(NT):
                            ins = dve.scalar_tensor_tensor(acc[:, t, :], bank[2 + e % 2][:, t * P:(t + 1) * P], gates[:, t, e:e + 1],
                                                           acc[:, t, :], ALU.mult, ALU.add)
                        ins.then_inc(done["l2f_oadd"], 1)
                    dve.wait_ge(done["l2f_oadd"], E)
                    dve.wait_ge(done["projected"], 3)
                    link(dve.tensor_tensor(acc[:, :, :], acc[:, :, :], bank[5][:, 0:S].rearrange("p (t d) -> p t d", t=NT), ALU.add))
                    add_to_x(acc[:, :, :], 5)

                if STAGES > 6:
                    layernorm(6, xs).then_inc(done["ln_y"], 1)
                    dve.wait_ge(done["l3_qkv"], 1)
                    dve.tensor_tensor(acc[:, :, :], bank[2][:, 0:S].rearrange("p (t d) -> p t d", t=NT),
                                      w("l3_bv").unsqueeze(1).broadcast_to([P, NT, D]), ALU.add).then_inc(done["l3_v_ready"], 1)
                    dve.wait_ge(done["l3_s"], 1)
                    link(dve.tensor_reduce(gs[:, 0, :].unsqueeze(2), bank[3][:, :].rearrange("p (t s) -> p t s", t=NT), X_AXIS, ALU.max))
                    dve.tensor_scalar(gs[:, 1, :], gs[:, 0, :], -D ** -0.5, None, ALU.mult).then_inc(done["l3_smax"], 1)
                    dve.wait_ge(done["l3_exp"], 2)
                    link(dve.reciprocal(gs[:, 3, :], gs[:, 2, :]))
                    dve.wait_ge(done["l3_out"], 1)
                    for t in range(NT):
                        link(dve.scalar_tensor_tensor(tmp[:, t, :], bank[6][:, t * P:(t + 1) * P], gs[:, 3, t:t + 1], w("l3_bo"),
                                                      ALU.mult, ALU.add))
                    add_to_x(tmp[:, :, :], 6)

                if STAGES > 7:
                    link(layernorm(7, xs, x1))
                    layernorm(8, x1).then_inc(done["ln_y"], 1)
                    for name, dst, extra in (("rope_q", qS, "zero"), ("rope_k", kS, "kones8")):
                        dve.wait_ge(done[name], 1)
                        for g in range(4):
                            cols = slice((g % 2) * S, (g % 2 + 1) * S)
                            link(dve.tensor_tensor(pr[:, 0, :], bank[g // 2][:, cols], c("cos"), ALU.mult))
                            link(dve.tensor_tensor(pr[:, 1, :], bank[2 + g // 2][:, cols], c("sin"), ALU.mult))
                            ins = dve.scalar_tensor_tensor(dst[:, g, :], pr[:, 0, :], c(extra), pr[:, 1, :], ALU.add, ALU.add)
                            if g < 3:
                                link(ins)
                        if name == "rope_q":
                            ins.then_inc(done["rope_q_ready"], 1)
                            dve.wait_ge(done["rope_q_ready"], 1)
                            dve.wait_ge(done["rope_v"], 1)
                            link(dve.tensor_copy(V8[:, :, :, 0:8], bank[6][:, 0:S].rearrange("p (t h d) -> p t h d", t=NT, d=8)))
                        else:
                            ins.then_inc(done["rope_kv_ready"], 1)
                    dve_attention(dve, A3, link)
                    dve.wait_ge(done["projected"], 4)
                    link(dve.tensor_tensor(x1[:, :, :], x1[:, :, :], bank[1][:, 0:S].rearrange("p (t d) -> p t d", t=NT), ALU.add))
                    layernorm(9, x1).then_inc(done["ln_y"], 1)
                    L3 = routing("l3f", bank[6][:, 0:NT * E])
                    M3 = coef[:, 0:NT * E].rearrange("p (t e) -> p t e", e=E)
                    dve.sem_inc(done["l3f_top"], 1)
                    link(dve.tensor_reduce(gs[:, 1, :].unsqueeze(2), L3, X_AXIS, ALU.add))
                    link(dve.reciprocal(gs[:, 2, :], gs[:, 1, :]))
                    link(dve.tensor_tensor(gates[:, :, :], L3, gs[:, 2, :].unsqueeze(2).broadcast_to([P, NT, E]), ALU.mult))
                    dve.wait_ge(done["l3f_count"], 1)
                    K3 = gsig[:, 0:NT * E].rearrange("p (t e) -> p t e", e=E)
                    link(dve.tensor_tensor(K3, bank[7][:, 0:2 * E].rearrange("p (t e) -> p t e", e=E),
                                           carry[:, :].unsqueeze(1).broadcast_to([P, NT, E]), ALU.add))
                    link(dve.tensor_scalar(K3, K3, float(CAPACITY) + 0.5, None, ALU.is_lt))
                    link(dve.tensor_tensor(carry[:, :], carry[:, :], bank[7][:, 2 * E:3 * E], ALU.add))
                    link(dve.tensor_tensor(K3, K3, M3, ALU.mult))
                    dve.tensor_tensor(gates[:, :, :], gates[:, :, :], K3, ALU.mult).then_inc(done["l3f_gates"], 1)
                    dve.wait_ge(done["l3f_gates"], 1)
                    for e in range(E):
                        dve.wait_ge(done["l3f_o"], e + 1)
                        if some(e):
                            dve.wait_ge(done["l3f_oadd"], e)
                        for t in range(NT):
                            ins = dve.scalar_tensor_tensor(x1[:, t, :], bank[4 + e % 2][:, t * P:(t + 1) * P], gates[:, t, e:e + 1],
                                                           x1[:, t, :], ALU.mult, ALU.add)
                        ins.then_inc(done["l3f_oadd"], 1)
                    dve.wait_ge(done["l3f_oadd"], E)
                    dve.wait_ge(done["projected"], 5)
                    link(dve.tensor_tensor(x1[:, :, :], x1[:, :, :], bank[0][:, 0:S].rearrange("p (t d) -> p t d", t=NT), ALU.add))
                    add_to_x(x1[:, :, :], 7)
                dve.sem_inc(done["x_final"], 1)
                end_of_batch(dve)


SETUP_DVE = 12


def kernel(**inputs):
    import numpy as _np
    import concourse.bacc as _bacc
    from concourse import mybir as _mybir
    from concourse.bass_utils import run_bass_kernel_spmd as _run

    f32 = _np.float32
    I = {k: _np.asarray(v) for k, v in inputs.items()}

    def spread(cols, dh):
        rows, n = cols.shape
        out = _np.zeros((rows, n // dh, 32), f32)
        out[:, :, :dh] = cols.reshape(rows, n // dh, dh)
        return out.reshape(rows, -1)

    def spread_bias(vec, dh, one):
        out = _np.zeros((vec.size // dh, 32), f32)
        out[:, :dh] = vec.reshape(-1, dh)
        out[:, dh] = one
        return _np.ascontiguousarray(out.reshape(-1, 128).T)

    def rows(vec):
        return _np.broadcast_to(vec.reshape(1, -1), (128, vec.size))

    def experts_to_cols(a):
        return a.transpose(1, 0, 2).reshape(a.shape[1], -1)

    gate = _np.concatenate([I["L0_xattn_ig_kernel"].reshape(3, 128, 4), I["L0_xattn_fg_kernel"].reshape(3, 128, 4)], axis=2)
    gains = _np.stack([I["g_xattn"], I["g_ffn"]], axis=1).reshape(-1)
    qkv = I["L3_ffn_Wqkv"].reshape(128, 16, 24)
    swap = [4, 5, 6, 7, 0, 1, 2, 3]
    q, k, v = (qkv[:, :, a:a + 8] for a in (0, 8, 16))
    vb_cols = _np.zeros((128, 8, 8), f32)
    for e in range(8):
        vb_cols[:, e, e] = I["L1_ffn_vb"][e]
    W = {
        "l0_gate": experts_to_cols(gate), "l0_bias": _np.stack([I["L0_xattn_ig_bias"], I["L0_xattn_fg_bias"]], axis=1),
        "l0_outnorm": rows(I["L0_xattn_outnorm_weight"]), "gains": rows(gains),
        "l0_wq": I["L0_ffn_Wq"].transpose(2, 0, 1).reshape(128, -1), "l0_wk": I["L0_ffn_Wk"].transpose(2, 0, 1).reshape(128, -1),
        "l0_wv": I["L0_ffn_Wv"].transpose(2, 0, 1).reshape(128, -1),
        "l0_wsd": _np.concatenate([I["L0_ffn_Ws"].transpose(2, 0, 1).reshape(128, -1),
                                   I["L0_ffn_Wd"].transpose(2, 0, 1).reshape(128, -1)], axis=1),
        "l0_wo": I["L0_ffn_Wo"].transpose(0, 2, 1).reshape(4, 128, 128).transpose(1, 0, 2).reshape(128, -1),
        "l1_wq": spread(I["L1_xattn_wq_k"], 8), "l1_wk": spread(I["L1_xattn_wk_k"], 8), "l1_wv": I["L1_xattn_wv_k"],
        "l1_qb": spread_bias(I["L1_xattn_wq_b"], 8, 0.0), "l1_kb": spread_bias(I["L1_xattn_wk_b"], 8, 1.0),
        "l1_vb": rows(I["L1_xattn_wv_b"]), "l1_wo": I["L1_xattn_wo_k"], "l1_bo": rows(I["L1_xattn_wo_b"]),
        "l1f_rw1": I["L1_ffn_rW1"].T, "l1f_rb1": rows(I["L1_ffn_rb1"]), "l1f_lng": rows(I["L1_ffn_ln_g"]),
        "l1f_lnb": rows(I["L1_ffn_ln_b"]), "l1f_rw2": I["L1_ffn_rW2"].T, "l1f_rb2": rows(I["L1_ffn_rb2"]),
        "l1f_ow": experts_to_cols(I["L1_ffn_oW"].transpose(0, 2, 1)), "l1f_vb": vb_cols.reshape(128, 64), "l1f_ob": I["L1_ffn_ob"],
        "l2_wq": spread(I["L2_xattn_Wq"].T, 16), "l2_wk": spread(I["L2_xattn_Wk"].T, 16), "l2_wv": I["L2_xattn_Wv"].T,
        "l2f_router": I["L2_ffn_router_w"], "l2f_win": experts_to_cols(I["L2_ffn_w_in"]), "l2f_bin": I["L2_ffn_b_in"].T,
        "l2f_wout": experts_to_cols(I["L2_ffn_w_out"]), "l2f_bout": I["L2_ffn_b_out"],
        "l3_wk": I["L3_xattn_Wk"].T, "l3_wv": I["L3_xattn_Wv"].T, "l3_wq": I["L3_xattn_Wq"].T, "l3_wo": I["L3_xattn_Wo"].T,
        "l3_bq": I["L3_xattn_bq"].reshape(128, 1), "l3_bv": rows(I["L3_xattn_bv"]), "l3_bo": rows(I["L3_xattn_bo"]),
        "l3f_ln": _np.stack([I["L3_ffn_ln1_g"], I["L3_ffn_ln1_b"], I["L3_ffn_ln2_g"], I["L3_ffn_ln2_b"]], axis=1),
        "l3f_wq": spread(q.reshape(128, -1), 8), "l3f_wqs": spread(q[:, :, swap].reshape(128, -1), 8),
        "l3f_wk": spread(k.reshape(128, -1), 8), "l3f_wks": spread(k[:, :, swap].reshape(128, -1), 8),
        "l3f_wv": v.reshape(128, -1), "l3f_wproj": I["L3_ffn_Wproj"], "l3f_wgate": I["L3_ffn_Wgate"],
        "l3f_w1": experts_to_cols(I["L3_ffn_W1"]), "l3f_b1": I["L3_ffn_b1"].reshape(32, 128).T,
        "l3f_w2": experts_to_cols(I["L3_ffn_W2"].reshape(32, 128, 128)), "l3f_b2": I["L3_ffn_b2"],
    }
    at, n = columns(WEIGHTS)
    weights = _np.zeros((128, n), f32)
    for name, (a, width) in at.items():
        weights[:W[name].shape[0], a:a + width] = W[name]

    idx = _np.arange(128)
    ang = _np.arange(256, dtype=f32)[:, None] * (1.0 / 10000.0 ** (_np.arange(0, 8, 2, dtype=f32) / f32(8))).astype(f32)
    cos, sin = _np.zeros((4, 32, 256), f32), _np.zeros((4, 32, 256), f32)
    cos[:, 0:8] = _np.concatenate([_np.cos(ang), _np.cos(ang)], axis=1).T
    sin[:, 0:8] = _np.concatenate([-_np.sin(ang), _np.sin(ang)], axis=1).T
    later = _np.arange(256)
    neg = _np.where(later[:, None] >= later[None, :], 0.0, -1.0e9 * 8 ** 0.5).astype(f32)
    sel = _np.zeros((128, 4, 128), f32)
    for h in range(4):
        sel[h, h] = 1.0
    ones_row = {8: _np.zeros((128, 1), f32), 16: _np.zeros((128, 1), f32)}
    for d, a in ones_row.items():
        a[d::32] = 1.0
    den8 = _np.zeros((128, 32), f32)
    den8[:, 8] = 1.0
    C = {
        "ident": _np.eye(128, dtype=f32), "ones": _np.ones((128, 128), f32), "upto": (idx[:, None] <= idx[None, :]).astype(f32),
        "rank": _np.broadcast_to(_np.arange(8, 0, -1, dtype=f32), (128, 8)), "sel4": sel.reshape(128, -1),
        "cos": cos.reshape(128, 256), "sin": sin.reshape(128, 256), "kones8": ones_row[8], "kones16": ones_row[16],
        "zero": _np.zeros((128, 1), f32), "den8": den8,
    }
    causal = _np.concatenate([neg.reshape(2, 128, 256).transpose(1, 0, 2).reshape(128, -1),
                              neg.T.reshape(2, 128, 256).transpose(1, 0, 2).reshape(128, -1)], axis=1)
    at, n = columns(CONSTS)
    consts = _np.zeros((128, n), f32)
    for name, (a, width) in at.items():
        consts[:, a:a + width] = C[name]

    experts = _np.stack([_np.concatenate([
        spread(I["L1_ffn_qW"][e].T, 8), spread(I["L1_ffn_kW"][e].T, 8), I["L1_ffn_vW"][e].T,
        spread_bias(I["L1_ffn_qb"][e], 8, 0.0), spread_bias(I["L1_ffn_kb"][e], 8, 1.0)], axis=1) for e in range(8)])

    mask = I["mask_BxSxS2_ik1"]
    arrays = {
        "x": I["x"], "ctx": I["ctx_1024"], "group_prob_T": I["fside_BxSxS2_0"].transpose(0, 2, 1),
        "mask": mask, "mask_T": mask.transpose(0, 2, 1), "weights": weights, "consts": consts, "causal": causal, "experts": experts,
    }
    nc = _bacc.Bacc("TRN2", target_bir_lowering=False, num_devices=1)
    args = []
    for name in arrays:
        arrays[name] = a = _np.ascontiguousarray(arrays[name])
        args.append(nc.dram_tensor(name, a.shape, _mybir.dt.from_np(a.dtype), kind="ExternalInput").ap())
    args.append(nc.dram_tensor("out", (8, 256, 128), _mybir.dt.float32, kind="ExternalOutput").ap())
    program(nc, *args)
    r = _run(nc, [arrays], core_ids=[0])
    return r.results[0]["out"]
```

```python
import math
from contextlib import ExitStack

import concourse.bass as bass
import numpy as np
from concourse import mybir
from concourse.alu_op_type import AluOpType as ALU

FP32, BF16, I32 = mybir.dt.float32, mybir.dt.bfloat16, mybir.dt.int32
ACT = mybir.ActivationFunctionType
X_AXIS = mybir.AxisListType.X

B, S, D, P = 8, 256, 128, 128
NT = S // P
E = 8
STAGES = 8
CAPACITY = int(math.ceil(2.0 * B * S / E))
BIG = 1.0e30
NEG_MASK = -1.0e9

WEIGHTS = [
    ("l0_gate", 24), ("l0_bias", 2), ("l0_outnorm", 128), ("gains", 8),
    ("l0_wq", 1024), ("l0_wk", 1024), ("l0_wv", 512), ("l0_wsd", 256), ("l0_wo", 512),
    ("l1_wq", 512), ("l1_wk", 512), ("l1_wv", 128), ("l1_qb", 4), ("l1_kb", 4), ("l1_vb", 128),
    ("l1_wo", 128), ("l1_bo", 128),
    ("l1f_rw1", 64), ("l1f_rb1", 64), ("l1f_lng", 64), ("l1f_lnb", 64), ("l1f_rw2", 8), ("l1f_rb2", 8),
    ("l1f_ow", 1024), ("l1f_vb", 64), ("l1f_ob", 128),
    ("l2_wq", 256), ("l2_wk", 256), ("l2_wv", 128),
    ("l2f_router", 8), ("l2f_win", 1024), ("l2f_bin", 8), ("l2f_wout", 1024), ("l2f_bout", 128),
    ("l3_wk", 128), ("l3_wv", 128), ("l3_wq", 128), ("l3_wo", 128), ("l3_bq", 1), ("l3_bv", 128), ("l3_bo", 128),
    ("l3f_ln", 4), ("l3f_wq", 512), ("l3f_wqs", 512), ("l3f_wk", 512), ("l3f_wks", 512), ("l3f_wv", 128),
    ("l3f_wproj", 128), ("l3f_wgate", 8), ("l3f_w1", 4096), ("l3f_b1", 32), ("l3f_w2", 4096), ("l3f_b2", 128),
]
CONSTS = [
    ("ident", 128), ("ones", 128), ("upto", 128), ("rank", 8), ("sel4", 512), ("cos", 256), ("sin", 256),
    ("kones8", 1), ("kones16", 1), ("kones_stack", 1), ("zero", 1), ("den8", 32),
]
EXPERT_COLS = 3 * 128 + 2


def columns(layout):
    at, out = 0, {}
    for name, width in layout:
        out[name] = (at, width)
        at += width
    return out, at


class Attention:

    def __init__(self, heads, dh, rows, per, scale, heads_before, groups_before, norms_before, masked=False, gated=False,
                 score_banks=3):
        self.heads, self.dh, self.rows, self.per, self.scale = heads, dh, rows, per, scale
        self.groups = heads // per
        self.masked, self.gated, self.score_banks = masked, gated, score_banks
        self.hb, self.gb, self.nb = heads_before, groups_before, norms_before
        self.chunk = min(4, self.groups)
        self.chunks = self.groups // self.chunk
        self.turns = {}
        for c in range(self.chunks):
            last = (c + 1) * self.chunk * per - 1
            for t in range(NT):
                self.turns[last + per + 3 + t] = (c, t)
        self.steps = max(self.turns) + 1

    def turns_before(self, step):
        return sum(1 for s in self.turns if s < step)

    def adds_before(self, step):
        return sum(1 for i in range(step) if i % self.per == 0 and self.per <= i <= self.heads)


def program(nc, x_in, ctx_in, gp_in, mask_in, maskT_in, weights_in, consts_in, causal_in, sel_in, experts_in, out):
    WC, n_weights = columns(WEIGHTS)
    CC, n_consts = columns(CONSTS)
    scope = ExitStack()
    with scope:
        def sb(name, shape, dt=FP32):
            return scope.enter_context(nc.sbuf_tensor(name, shape, dt))

        W = sb("W", [P, n_weights])
        C = sb("C", [P, n_consts])

        def w(name, rows=P):
            a, n = WC[name]
            return W[0:rows, a:a + n]

        def c(name, rows=P):
            a, n = CC[name]
            return C[0:rows, a:a + n]

        ident = c("ident")
        ident_bf = sb("ident_bf", [P, P], BF16)
        causS = sb("causS", [P, NT, S], BF16)
        causT = sb("causT", [P, NT, S], BF16)
        tanh_gain = sb("tanh_gain", [P, 8])
        minus_half = sb("minus_half", [P, 16])
        out_bias1 = sb("out_bias1", [E, D])
        expert = sb("expert", [P, EXPERT_COLS])
        sel = sb("sel_sb", [P, 8, 2, 3, P], BF16)
        kone = sb("kone", [P, 2])

        xs = sb("xs", [P, NT, D])
        ctxs = sb("ctxs", [P, NT, D])
        ctxT = sb("ctxT", [P, S])
        y = sb("y", [P, NT, D])
        yT = sb("yT", [P, S])
        bn = sb("bn", [P, NT, 6])
        mv = sb("mv", [P, NT, 2])
        rstd = sb("rstd", [P, NT])
        tmp = sb("tmp", [P, NT, D])
        acc = sb("acc", [P, NT, D])

        mix = sb("mix", [P, 4096])
        qk = sb("qk", [P, 8, S])
        qS, kS = qk[:, 0:4, :], qk[:, 4:8, :]
        qk64 = qk[:, :, :].rearrange("p (h a) s -> p h (a s)", a=2)
        negmax = {8: sb("negmax8", [P, 4, NT, P]), 16: sb("negmax16", [P, 2, NT, P]), 64: sb("negmax64", [P, 4, NT, P])}
        F = mix[:, 0:512].rearrange("p (a s) -> p a s", a=2)
        rest = mix[:, 512:1024].rearrange("p (a s) -> p a s", a=2)
        stack = mix[:, 1024:3072].bitcast(BF16).rearrange("p (t a s) -> p t a s", t=8, a=2)
        parts = mix[:, 3072:3840].bitcast(BF16).rearrange("p (c a s) -> p c a s", c=3, a=2)
        Vn = mix[:, 3840:4096].rearrange("p (t h d) -> p t h d", t=NT, d=8)
        negmax_bf = sb("negmax_bf", [P, 2, NT, P], BF16)
        V8 = sb("V8", [P, NT, 16, 32])
        V16 = sb("V16", [P, NT, 8, 32])
        V64s = sb("V64s", [P, NT * 16 * 65])
        V64 = V64s[:, :].rearrange("p (t h d) -> p t h d", t=NT, h=16)
        V8x = V64s[:, 0:NT * 16 * 32].rearrange("p (t h d) -> p t h d", t=NT, h=16)
        negS = V64s[:, 1024:1280].bitcast(BF16).rearrange("p (t s) -> p t s", t=NT)
        negT = V64s[:, 1280:1536].bitcast(BF16).rearrange("p (t s) -> p t s", t=NT)
        gpT = V64s[:, 1536:2048].rearrange("p (t s) -> p t s", t=NT)
        PTG = sb("PTG", [P, 6, 2 * S])
        PX = PTG[:, 0:4, :]
        PT, PG = PTG[:, 0:3, :], PTG[:, 3:6, :]
        OT = sb("OT", [P, 8, S])
        on = sb("on", [P, NT, 1024])
        onT = sb("onT", [P, S])
        rden = sb("rden", [P, 16])

        l0r = PTG[0:4, :, :].rearrange("p a (b s) -> p (a b) s", b=2)
        gcol = sb("gcol", [P, NT, 4])
        mcol = sb("mcol", [P, NT, 4])
        mixD, mixP = mix[:, 0:2048], mix[:, 2048:4096]
        mask_i = mix[:, 0:512].bitcast(I32).rearrange("p (t s) -> p t s", t=NT)
        maskT_i = mix[:, 512:1024].bitcast(I32).rearrange("p (t s) -> p t s", t=NT)
        Dm = mix[:, 0:1536].rearrange("p (h s) -> p h s", h=4)
        Cm = mix[:, 1536:3072].rearrange("p (h s) -> p h s", h=4)
        Vm = sb("Vm", [P, NT, 4, 33])
        hh = sb("hh", [P, NT, 4, 32])
        bn8 = sb("bn8", [P, 8, 6])
        mv8 = sb("mv8", [P, 8, 2])
        rstd8 = sb("rstd8", [P, 8])
        dn = sb("dn", [P, 4, NT * 4])
        pv = sb("pv", [P, NT, 512])
        gv = sb("gv", [P, 512])
        t2 = OT[:, :, :].rearrange("p (a b) s -> p a (b s)", b=2)
        t2s = sb("t2s", [P, 2, 64])
        gsig = sb("gsig", [P, 512])
        coef = sb("coef", [P, 512])

        gates = sb("gates", [P, NT, E])
        gatesT = y[0:E, :, :].rearrange("p t d -> p (t d)")
        gs = sb("gs", [P, 4, NT])
        hT = on[:, :, :].rearrange("p t (f s) -> p t f s", f=4)
        GT = hT[:, 0, :, :]
        carry = sb("carry", [P, E])
        x1 = tmp
        pr = sb("pr", [P, 2, S])
        r1 = pr[:, 1, 0:NT * 64].rearrange("p (t d) -> p t d", t=NT)
        r1T = pr[0:64, 0, :]

        bank = [scope.enter_context(nc.psum_tensor(f"bank{i}", [P, 512], FP32)) for i in range(8)]
        MISC = bank[7]

        setup = {n: scope.enter_context(nc.semaphore(n)) for n in (
            "consts_loaded", "causal_loaded", "sel_loaded", "weights_loaded", "setup_dve", "setup_pool", "setup_pe", "setup_act",
            "engine_at_end", "cleared", "engine_resumes")}
        done = {n: scope.enter_context(nc.semaphore(n)) for n in (
            "x_loaded", "ctx_loaded", "mask_loaded", "maskT_loaded", "gp_loaded", "expert_loaded", "x_final", "out_stored",
            "dve_step", "dve_expert_step", "pool_step", "pool_expert_step", "act_step",
            "ln_var", "ln_rstd", "ln_y", "ln_turned", "ln_yT",
            "scored", "max_taken", "max_turned", "q_shifted", "scoredT", "exped", "group_weighted", "valued",
            "o_copied", "o_turned", "normed",
            "ctx_turned", "ctxT_ready", "on_turned", "onT_ready", "projected",
            "l0_gates", "l0_absf", "l0_softplus", "l0_rows", "l0_cols_turned", "l0_negm", "l0_expm", "l0_spread", "l0_args",
            "l0_decay", "l0_decay_masked", "l0_qk", "l0_cm", "l0_h", "l0_hstat", "l0_hrstd",
            "l0f_qk", "l0f_qk_ready", "l0f_pv", "l0f_gates", "l0f_gcopied", "l0f_sig", "l0f_pvcopied", "l0f_coef", "l0f_vdve",
            "l0f_vpool", "l0f_gdve", "l0f_gpool", "l0f_gturned", "l0f_gT",
            "filled", "neg_ready", "l1_q", "l1_k", "l1_v", "l1_q_ready", "l1_kv_ready",
            "l1f_r1", "l1f_rvar", "l1f_rrstd", "l1f_r1n", "l1f_r1turned", "l1f_r1T", "router_logits", "router_shifted", "router_exped", "gates_ready", "gates_turned", "gatesT_ready", "l1f_bias",
            "ex_qk_projected", "ex_F_ready", "ex_split", "ex_spread", "ex_stacked_act", "ex_stacked_dve", "ex_v_projected",
            "ex_v_ready", "ex_v_placed", "ex_scored", "ex_max_taken", "ex_max_turned", "ex_shifted", "ex_scoredT", "ex_exped",
            "ex_valued", "ex_o_copied", "ex_o_turned", "ex_normed", "ex_on_turned", "ex_onT_ready", "ex_projected", "ex_added",
            "l2_q", "l2_kv", "l2_q_ready", "l2_kv_ready",
            "l2f_h", "l2f_gelu", "l2f_o", "l2f_oadd",
            "l3_qkv", "l3_qk_ready", "l3_v_ready", "l3_s", "l3_smax", "l3_exp", "l3_pturned", "l3_pT", "l3_ctx", "l3_ctx_ready", "l3_out",
            "rope_q", "rope_k", "rope_v", "rope_q_ready", "rope_kv_ready",
            "l3f_top", "l3f_count", "l3f_h", "l3f_gelu", "l3f_o",
            "l3f_oadd")}
        A0 = Attention(16, 64, 128, 1, 64 ** -0.5, 0, 0, 0, score_banks=2)
        A1 = Attention(16, 8, 32, 4, 8 ** -0.5, 16, 16, 8, masked=True, gated=True)

        A2 = Attention(8, 16, 32, 4, 0.25, 32, 20, 10)
        A3 = Attention(16, 8, 32, 4, 8 ** -0.5, 40, 22, 12, masked=True)

        def some(n):
            return not isinstance(n, int) or n > 0

        block = scope.enter_context(nc.Block())

        @block.sync
        def _(sp):
            sp.dma_start(C[:, :], consts_in).then_inc(setup["consts_loaded"], 16)
            sp.dma_start(mixD[:, 0:1024], causal_in).then_inc(setup["causal_loaded"], 16)
            sp.dma_start(sel[:, :, :, :, :], sel_in).then_inc(setup["sel_loaded"], 16)
            sp.dma_start(W[:, :], weights_in).then_inc(setup["weights_loaded"], 16)
            with sp.Fori(0, B) as b:
                def tokens(ap):
                    return ap[bass.ds(b, 1)].rearrange("a (t p) d -> p (a t) d", p=P)

                sp.dma_start(xs[:, :, :], tokens(x_in)).then_inc(done["x_loaded"], 16)
                sp.dma_start(ctxs[:, :, :], tokens(ctx_in)).then_inc(done["ctx_loaded"], 16)
                if STAGES > 2:
                    sp.wait_ge(done["l0f_gturned"], 2)
                    sp.dma_start(gpT, tokens(gp_in)).then_inc(done["gp_loaded"], 16)
                    sp.dma_start(mask_i, tokens(mask_in)).then_inc(done["mask_loaded"], 16)
                    sp.dma_start(maskT_i, tokens(maskT_in)).then_inc(done["maskT_loaded"], 16)
                if STAGES > 3:
                    sp.dma_start(expert[:, :], experts_in[0]).then_inc(done["expert_loaded"], 16)
                    with sp.Fori(1, E) as e:
                        sp.wait_ge(done["ex_v_projected"], e)
                        sp.wait_ge(done["ex_F_ready"], e)
                        sp.dma_start(expert[:, :], experts_in[bass.ds(e, 1)].rearrange("a p n -> (a p) n"))\
                            .then_inc(done["expert_loaded"], 16)
                sp.wait_ge(done["x_final"], 1)
                sp.dma_start(out[bass.ds(b, 1)].rearrange("a (t p) d -> p (a t) d", p=P), xs[:, :, :])\
                    .then_inc(done["out_stored"], 16)
                sp.wait_ge(done["out_stored"], 16)
                for n in ("x_loaded", "ctx_loaded"):
                    sp.wait_ge(done[n], 16)
                if STAGES > 2:
                    for n in ("mask_loaded", "maskT_loaded", "gp_loaded"):
                        sp.wait_ge(done[n], 16)
                if STAGES > 3:
                    sp.wait_ge(done["expert_loaded"], 16 * E)
                sp.wait_ge(setup["engine_at_end"], 4)
                for s in done.values():
                    sp.sem_clear(s)
                sp.sem_clear(setup["engine_at_end"])
                sp.sem_inc(setup["cleared"], 1)
                sp.wait_ge(setup["engine_resumes"], 4)
                sp.sem_clear(setup["cleared"])
                sp.sem_clear(setup["engine_resumes"])

        def end_of_batch(eng):
            eng.sem_inc(setup["engine_at_end"], 1)
            eng.wait_ge(setup["cleared"], 1)
            eng.sem_inc(setup["engine_resumes"], 1)

        def q_rows(A, h, n):
            if A.rows == 128:
                return qk64[0:n, h % 4, 0:S]
            j = 32 * (h % 4)
            return qS[j:j + n, h // 4, :]

        def k_rows(A, h, n):
            if A.rows == 128:
                return qk64[0:n, h % 4, S:2 * S]
            j = 32 * (h % 4)
            return kS[j:j + n, h // 4, :]

        def pe_attention(pe, A, V, masks=None, before=None):
            per, dh = A.per, A.dh
            for i in range(A.steps):
                if before is not None:
                    before(i)
                if i < A.heads:
                    if some(A.hb + i - A.score_banks + 1):
                        pe.wait_ge(done["max_taken"], A.hb + i - A.score_banks + 1)
                    for t in range(NT):
                        mm = pe.matmul(bank[i % A.score_banks][:, t * S:(t + 1) * S], q_rows(A, i, dh)[:, t * P:(t + 1) * P],
                                       k_rows(A, i, dh), start=True, stop=masks is None)
                        if masks is not None:
                            mm = pe.matmul(bank[i % A.score_banks][:, t * S:(t + 1) * S], ident_bf[:, :], masks[0][:, t, :],
                                           start=False, stop=True)
                    mm.then_inc(done["scored"], 1)
                if i % per == 0 and per <= i <= A.heads:
                    g = i // per - 1
                    pe.wait_ge(done["max_taken"], A.hb + (g + 1) * per)
                    if some(A.gb + g):
                        pe.wait_ge(done["q_shifted"], A.gb + g)
                    if some(A.nb + A.turns_before(i)):
                        pe.wait_ge(done["normed"], A.nb + A.turns_before(i))
                    M = negmax[dh][:, g % 4, :, :]
                    rows = A.rows if A.rows == 128 else 128
                    for t in range(NT):
                        mm = pe.transpose(MISC[0:rows, t * P:(t + 1) * P], M[:, t, :], ident)
                    mm.then_inc(done["max_turned"], 1)
                h = i - per - 1
                if 0 <= h < A.heads:
                    pe.wait_ge(done["q_shifted"], A.gb + h // per + 1)
                    if some(A.hb + h - 1):
                        pe.wait_ge(done["exped"], A.hb + h - 1)
                    for t in range(NT):
                        mm = pe.matmul(bank[3 + h % 2][:, t * S:(t + 1) * S], k_rows(A, h, dh + 1)[:, t * P:(t + 1) * P],
                                       q_rows(A, h, dh + 1), start=True, stop=masks is None)
                        if masks is not None:
                            mm = pe.matmul(bank[3 + h % 2][:, t * S:(t + 1) * S], ident_bf[:, :], masks[1][:, t, :],
                                           start=False, stop=True)
                    mm.then_inc(done["scoredT"], 1)
                h = i - per - 2
                if 0 <= h < A.heads:
                    g, j = h // per, h % per
                    if j == 0:
                        if some(A.gb + g - 1):
                            pe.wait_ge(done["o_copied"], A.gb + g - 1)
                    if A.gated:
                        pe.wait_ge(done["group_weighted"], h + 1)
                    pe.wait_ge(done["exped"], A.hb + h + 1)
                    if A.rows == 128:
                        o = bank[5 + g % 2][0:dh + 1, 0:S]
                    else:
                        o = bank[5 + g % 2][32 * j:32 * j + 32, 0:S]
                    for t in range(NT):
                        mm = pe.matmul(o, V[:, t, h, :], (PG if A.gated else PT)[:, h % 3, t * S:(t + 1) * S],
                                       start=t == 0, stop=t == NT - 1 and not A.gated)
                    if A.gated:
                        for t in range(NT):
                            mm = pe.matmul(o, c("den8"), PT[:, h % 3, t * S:(t + 1) * S], start=False, stop=t == NT - 1)
                    mm.then_inc(done["valued"], 1)
                if i in A.turns:
                    ch, t = A.turns[i]
                    pe.wait_ge(done["o_copied"], A.gb + (ch + 1) * A.chunk)
                    if some(A.nb + A.turns_before(i)):
                        pe.wait_ge(done["normed"], A.nb + A.turns_before(i))
                    pe.wait_ge(done["q_shifted"], A.gb + A.adds_before(i + 1))
                    n = dh + 1 if A.rows == 128 else 128
                    for s in range(A.chunk):
                        g = ch * A.chunk + s
                        mm = pe.transpose(MISC[:, s * 128:s * 128 + n], OT[0:n, g % 8, t * P:(t + 1) * P], ident[0:n, 0:n])
                    mm.then_inc(done["o_turned"], 1)

        def act_attention(act, A, before=None):
            per = A.per

            def copy_out(g):
                act.wait_ge(done["valued"], A.hb + (g + 1) * per)
                n = A.dh + 1 if A.rows == 128 else 128
                act.activation(OT[0:n, g % 8, :], bank[5 + g % 2][0:n, 0:S], ACT.Copy).then_inc(done["o_copied"], 1)

            for h in range(A.heads):
                if before is not None:
                    before(h)
                act.wait_ge(done["scoredT"], A.hb + h + 1)
                if some(A.hb + h - 2):
                    act.wait_ge(done["valued"], A.hb + h - 2)
                act.activation(PT[:, h % 3, :], bank[3 + h % 2][:, :], ACT.Exp, scale=A.scale).then_inc(done["exped"], 1)
                if h >= 1 and h % per == 0:
                    copy_out(h // per - 1)
            copy_out(A.groups - 1)

        def pool_attention(pool, A):
            for h in range(A.heads):
                pool.wait_ge(done["exped"], A.hb + h + 1)
                if some(A.hb + h - 2):
                    pool.wait_ge(done["valued"], A.hb + h - 2)
                pool.tensor_tensor(PG[:, h % 3, :], PT[:, h % 3, :], gpT.rearrange("p t s -> p (t s)"), ALU.mult)\
                    .then_inc(done["group_weighted"], 1)

        def dve_attention(dve, A, link):
            per, dh = A.per, A.dh
            for i in range(A.steps):
                if i < A.heads:
                    dve.wait_ge(done["scored"], A.hb + i + 1)
                    g, j = i // per, i % per
                    dve.tensor_reduce(negmax[dh][:, g % 4, :, j * 32 + dh], bank[i % A.score_banks][:, :].rearrange("p (t s) -> p t s", t=NT),
                                      X_AXIS, ALU.max, negate=True).then_inc(done["max_taken"], 1)
                if i % per == 0 and per <= i <= A.heads:
                    g = i // per - 1
                    dve.wait_ge(done["max_turned"], A.gb + g + 1)
                    if A.rows == 128:
                        dve.tensor_copy(qk64[dh:dh + 1, g % 4, 0:S], MISC[dh:dh + 1, 0:S]).then_inc(done["q_shifted"], 1)
                    else:
                        dve.tensor_tensor(qS[:, g, :], qS[:, g, :], MISC[:, 0:S], ALU.add).then_inc(done["q_shifted"], 1)
                if i in A.turns:
                    ch, t = A.turns[i]
                    dve.wait_ge(done["o_turned"], A.nb + A.turns_before(i) + 1)
                    n = A.chunk * per
                    T = MISC[:, 0:A.chunk * 128].rearrange("p (h c) -> p h c", c=A.rows)
                    r = rden[:, 0:n].unsqueeze(2)
                    link(dve.reciprocal(r, T[:, :, dh:dh + 1]))
                    o = on[:, t, ch * n * dh:(ch + 1) * n * dh].rearrange("p (h d) -> p h d", d=dh)
                    dve.tensor_tensor(o, T[:, :, 0:dh], r.broadcast_to([P, n, dh]), ALU.mult).then_inc(done["normed"], 1)

        SPREAD_AT = {1: 2, 2: 3, 4: 4, 5: 5, 7: 6, 8: 7}
        SPREAD_NEXT_AT = {13: 0, 15: 1}
        KQ = 48

        def body_pe(pe, e, prev, own, nxt):
            def spread(T, tile):
                for a in range(2):
                    for part in range(3):
                        mm = pe.matmul(bank[2][:, a * S:(a + 1) * S], sel[:, tile, a, part, :], parts[:, part, a, :],
                                       start=part == 0, stop=part == 2)
                mm.then_inc(done["ex_spread"], 1)

            for i in range(16):
                if own:
                    tile, row = i // 2, 64 * (i % 2)
                    if i % 4 == 0:
                        pe.wait_ge(done["ex_stacked_act"], e * 4 + i // 4 + 1)
                    elif i % 2 == 0:
                        pe.wait_ge(done["ex_stacked_dve"], e * 4 + i // 4 + 1)
                    if some(e * 16 + i - 1):
                        pe.wait_ge(done["ex_max_taken"], e * 16 + i - 1)
                    for t in range(NT):
                        mm = pe.matmul(bank[i % 2][:, t * S:(t + 1) * S], stack[row:row + KQ, tile, 0, t * P:(t + 1) * P],
                                       stack[row:row + KQ, tile, 1, :], start=True, stop=True)
                    mm.then_inc(done["ex_scored"], 1)
                if i % 2 == 0 and (own if i >= 2 else prev):
                    pe.wait_ge(done["ex_max_taken"], e * 16 + i)
                    if some(e * 8 + i // 2 - 1):
                        pe.wait_ge(done["ex_shifted"], e * 8 + i // 2 - 1)
                    if prev and i in (6, 8):
                        pe.wait_ge(done["ex_normed"], e * 2 + (i - 6) // 2 - 1)
                    if prev and i == 10:
                        pe.wait_ge(done["ex_onT_ready"], e)
                    if prev and i == 12:
                        pe.wait_ge(done["ex_added"], e + 1)
                    for t in range(NT):
                        mm = pe.transpose(MISC[:, :].bitcast(BF16)[:, t * P:(t + 1) * P],
                                          negmax_bf[:, (i // 2 - 1) % 2, t, :], ident_bf[:, :])
                    mm.then_inc(done["ex_max_turned"], 1)
                if prev and i in (5, 7, 9, 11):
                    pe.wait_ge(done["ex_shifted"], e * 8 + (i // 2 if own else 0))
                    if i in (5, 7):
                        t = (i - 5) // 2
                        pe.wait_ge(done["ex_o_copied"], e * 4)
                        if i == 7:
                            pe.wait_ge(done["ex_normed"], e * 2 - 1)
                        for g in range(4):
                            mm = pe.transpose(MISC[:, g * P:(g + 1) * P], OT[:, g, t * P:(t + 1) * P], ident)
                        mm.then_inc(done["ex_o_turned"], 1)
                    if i == 9:
                        pe.wait_ge(done["ex_normed"], e * 2)
                        for t in range(NT):
                            mm = pe.transpose(MISC[:, t * P:(t + 1) * P], on[:, t, 0:D], ident)
                        mm.then_inc(done["ex_on_turned"], 1)
                    if i == 11:
                        pe.wait_ge(done["ex_onT_ready"], e)
                        for t in range(NT):
                            mm = pe.matmul(MISC[:, t * P:(t + 1) * P], onT[:, t * P:(t + 1) * P],
                                           W[:, bass.ds(e * D + (WC["l1f_ow"][0] - D), D)], start=True, stop=True)
                        mm.then_inc(done["ex_projected"], 1)
                if own and i in SPREAD_AT:
                    tile = SPREAD_AT[i]
                    if tile == 6 and nxt:
                        pe.wait_ge(done["ex_F_ready"], e + 2)
                    elif tile % 2 == 0:
                        pe.wait_ge(done["ex_stacked_dve"], e * 4 + tile // 2)
                    else:
                        pe.wait_ge(done["ex_stacked_act"], e * 4 + tile // 2 + 1)
                    spread(e, tile)
                if nxt and i == 6:
                    pe.wait_ge(done["expert_loaded"], e * 16 + 32)
                    if own:
                        pe.wait_ge(done["ex_stacked_dve"], e * 4 + 3)
                    for a in range(2):
                        mm = pe.matmul(bank[2][:, a * S:(a + 1) * S], expert[:, a * P:(a + 1) * P], yT[:, :], start=True, stop=True)
                    mm.then_inc(done["ex_qk_projected"], 1)
                if nxt and i in SPREAD_NEXT_AT:
                    tile = SPREAD_NEXT_AT[i]
                    pe.wait_ge(done["ex_split"], e + 2)
                    if tile == 0:
                        if own:
                            pe.wait_ge(done["ex_stacked_dve"], e * 4 + 4)
                        else:
                            pe.wait_ge(done["ex_F_ready"], e + 2)
                    else:
                        pe.wait_ge(done["ex_v_ready"], e + 2)
                    spread(e + 1, tile)
                if nxt and i == 14:
                    pe.wait_ge(done["ex_stacked_act"], e * 4 + 5)
                    for t in range(NT):
                        mm = pe.matmul(bank[2][:, t * D:(t + 1) * D], yT[:, t * P:(t + 1) * P], expert[:, 256:384], start=True, stop=True)
                    mm.then_inc(done["ex_v_projected"], 1)
                if own if i >= 3 else prev:
                    h = (i - 3) % 16
                    tile, row = h // 2, 64 * (h % 2)
                    pe.wait_ge(done["ex_shifted"], e * 8 + (i - 3) // 2 + 1)
                    if some(e * 16 + i - 4):
                        pe.wait_ge(done["ex_exped"], e * 16 + i - 4)
                    for t in range(NT):
                        mm = pe.matmul(bank[3 + h % 2][:, t * S:(t + 1) * S], stack[row:row + KQ + 1, tile, 1, t * P:(t + 1) * P],
                                       stack[row:row + KQ + 1, tile, 0, :], start=True, stop=True)
                    mm.then_inc(done["ex_scoredT"], 1)
                if own if i >= 4 else prev:
                    h = (i - 4) % 16
                    g, j = h // 4, h % 4
                    if j == 0:
                        if some(e * 4 + i // 4 - 2):
                            pe.wait_ge(done["ex_o_copied"], e * 4 + i // 4 - 2)
                        pe.wait_ge(done["ex_v_placed"], e * 2 + (2 if g == 3 else 1) - (0 if i >= 4 else 2))
                    pe.wait_ge(done["ex_exped"], e * 16 + i - 3)
                    for t in range(NT):
                        mm = pe.matmul(bank[5 + g % 2][32 * j:32 * j + 32, 0:S], V8[:, t, h, :], PX[:, h % 4, t * S:(t + 1) * S],
                                       start=t == 0, stop=t == NT - 1)
                    mm.then_inc(done["ex_valued"], 1)

        def body_act(act, e, prev, own, nxt):
            def stack_tile(e_, tile):
                act.activation(stack[:, tile, 0, :], bank[2][:, 0:S], ACT.Copy)
                act.activation(stack[:, tile, 1, :], bank[2][:, S:2 * S], ACT.Identity, bias=c("kones_stack"))\
                    .then_inc(done["ex_stacked_act"], 1)

            for i in range(16):
                if own and i in SPREAD_AT and SPREAD_AT[i] % 2 == 0:
                    act.wait_ge(done["ex_spread"], e * 8 + SPREAD_AT[i] + 1)
                    stack_tile(e, SPREAD_AT[i])
                if nxt and i == 6:
                    act.wait_ge(done["ex_qk_projected"], e + 2)
                    if own:
                        act.wait_ge(done["ex_split"], e + 1)
                    for a in range(2):
                        ins = act.activation(F[:, a, :], bank[2][:, a * S:(a + 1) * S], ACT.Identity, bias=expert[:, 384 + a:385 + a])
                    ins.then_inc(done["ex_F_ready"], 1)
                if nxt and i == 13:
                    act.wait_ge(done["ex_spread"], e * 8 + 9)
                    stack_tile(e + 1, 0)
                if own if i >= 3 else prev:
                    h = (i - 3) % 16
                    act.wait_ge(done["ex_scoredT"], e * 16 + i - 2)
                    if some(e * 16 + i - 6):
                        act.wait_ge(done["ex_valued"], e * 16 + i - 6)
                    act.activation(PX[:, h % 4, :], bank[3 + h % 2][:, :], ACT.Exp, scale=8 ** -0.5).then_inc(done["ex_exped"], 1)
                if i % 4 == 3 and (own if i >= 7 else prev):
                    g = (i - 7) // 4 % 4
                    act.wait_ge(done["ex_valued"], e * 16 + i - 3)
                    if g == 0 and some(e * 2 - 2) and prev:
                        act.wait_ge(done["ex_o_turned"], e * 2)
                    act.activation(OT[:, g, :], bank[5 + g % 2][:, 0:S], ACT.Copy).then_inc(done["ex_o_copied"], 1)
                if prev and i == 9:
                    act.wait_ge(done["ex_on_turned"], e)
                    act.activation(onT[:, :], MISC[:, 0:S], ACT.Copy).then_inc(done["ex_onT_ready"], 1)

        def body_dve(dve, e, prev, own, nxt):
            n_linked = [0]

            def link(ins):
                n_linked[0] += 1
                ins.then_inc(done["dve_expert_step"], 1)
                dve.wait_ge(done["dve_expert_step"], e * 4 + n_linked[0] - 4)

            for i in range(16):
                if own:
                    dve.wait_ge(done["ex_scored"], e * 16 + i + 1)
                    if i % 2 == 0 and some(e * 8 + i // 2 - 1):
                        dve.wait_ge(done["ex_max_turned"], e * 8 + i // 2 - 1)
                    dve.tensor_reduce(negmax_bf[:, (i // 2) % 2, :, (i % 2) * 64 + KQ], bank[i % 2][:, :].rearrange("p (t s) -> p t s", t=NT),
                                      X_AXIS, ALU.max, negate=True).then_inc(done["ex_max_taken"], 1)
                if i % 2 == 0 and (own if i >= 2 else prev):
                    tile = (i // 2 - 1) % 8
                    dve.wait_ge(done["ex_max_turned"], e * 8 + i // 2)
                    dve.tensor_tensor(stack[:, tile, 0, :], stack[:, tile, 0, :], MISC[:, :].bitcast(BF16)[:, 0:S], ALU.add)\
                        .then_inc(done["ex_shifted"], 1)
                if prev and i in (5, 7):
                    t = (i - 5) // 2
                    dve.wait_ge(done["ex_o_turned"], e * 2 + t - 1)
                    T = MISC[:, :].rearrange("p (h c) -> p h c", c=32)
                    r = rden[:, 0:16].unsqueeze(2)
                    link(dve.reciprocal(r, T[:, :, 8:9]))
                    link(dve.tensor_scalar(rden[:, 0:16], rden[:, 0:16], gates[:, t, bass.ds(e - 1, 1)], None, ALU.mult))
                    dve.tensor_tensor(on[:, t, 0:D].rearrange("p (h d) -> p h d", d=8), T[:, :, 0:8], r.broadcast_to([P, 16, 8]), ALU.mult)\
                        .then_inc(done["ex_normed"], 1)
                if prev and i == 11:
                    dve.wait_ge(done["ex_projected"], e)
                    dve.wait_ge(done["ex_added"], e)
                    dve.tensor_tensor(acc[:, :, :], acc[:, :, :], MISC[:, 0:S].rearrange("p (t d) -> p t d", t=NT), ALU.add)\
                        .then_inc(done["ex_added"], 1)
                if own and i in SPREAD_AT and SPREAD_AT[i] % 2 == 1:
                    tile = SPREAD_AT[i]
                    dve.wait_ge(done["ex_spread"], e * 8 + tile + 1)
                    dve.tensor_tensor(stack[:, tile, :, :], bank[2][:, :].rearrange("p (a s) -> p a s", a=2), kone1, ALU.add)\
                        .then_inc(done["ex_stacked_dve"], 1)
                if nxt and i == 14:
                    dve.wait_ge(done["ex_v_projected"], e + 2)
                    if own:
                        dve.wait_ge(done["ex_v_placed"], e * 2 + 2)
                    dve.tensor_copy(Vn, bank[2][:, 0:S].rearrange("p (t h d) -> p t h d", t=NT, d=8)).then_inc(done["ex_v_ready"], 1)
                if nxt and i == 15:
                    dve.wait_ge(done["ex_spread"], e * 8 + 10)
                    dve.tensor_tensor(stack[:, 1, :, :], bank[2][:, :].rearrange("p (a s) -> p a s", a=2), kone1, ALU.add)\
                        .then_inc(done["ex_stacked_dve"], 1)

        kone1 = kone[:, :].unsqueeze(2).broadcast_to([P, 2, S])

        def body_pool(pool, e, own):
            pool.wait_ge(done["ex_F_ready"], e + 2)
            if own:
                pool.wait_ge(done["ex_spread"], e * 8 + 8)
            base = e * 3 + 3
            one = c("ones")[:, 0:2]
            pool.tensor_tensor(parts[:, 0, :, :], F, one.unsqueeze(2).broadcast_to([P, 2, S]), ALU.mult).then_inc(done["pool_expert_step"], 1)
            pool.wait_ge(done["pool_expert_step"], base + 1)
            pool.tensor_tensor(rest, F, parts[:, 0, :, :], ALU.subtract).then_inc(done["pool_expert_step"], 1)
            pool.wait_ge(done["pool_expert_step"], base + 2)
            pool.tensor_tensor(parts[:, 1, :, :], rest, one.unsqueeze(2).broadcast_to([P, 2, S]), ALU.mult).then_inc(done["pool_expert_step"], 1)
            pool.wait_ge(done["pool_expert_step"], base + 3)
            pool.tensor_tensor(parts[:, 2, :, :], rest, parts[:, 1, :, :], ALU.subtract).then_inc(done["ex_split"], 1)
            pool.wait_ge(done["ex_v_ready"], e + 2)
            if own:
                pool.wait_ge(done["ex_valued"], e * 16 + 12)
            pool.tensor_tensor(V8[:, :, 0:12, 0:8], Vn[:, :, 0:12, :], one.unsqueeze(2).unsqueeze(3).broadcast_to([P, NT, 12, 8]), ALU.mult).then_inc(done["ex_v_placed"], 1)
            if own:
                pool.wait_ge(done["ex_valued"], e * 16 + 16)
            pool.tensor_tensor(V8[:, :, 12:16, 0:8], Vn[:, :, 12:16, :], one.unsqueeze(2).unsqueeze(3).broadcast_to([P, NT, 4, 8]), ALU.mult).then_inc(done["ex_v_placed"], 1)

        @block.tensor
        def _(pe):
            pe.wait_ge(setup["weights_loaded"], 16)
            pe.wait_ge(setup["consts_loaded"], 16)
            pe.wait_ge(setup["sel_loaded"], 16)
            pe.wait_ge(setup["setup_dve"], SETUP_DVE)
            for e in range(E):
                mm = pe.matmul(bank[0][0:E, 0:D], w("l1f_vb")[:, e * E:(e + 1) * E], w("l1f_ow")[:, e * D:(e + 1) * D],
                               start=e == 0, stop=e == E - 1)
            mm.then_inc(setup["setup_pe"], 1)

            def turn_ln(n):
                pe.wait_ge(done["ln_y"], n + 1)
                for t in range(NT):
                    mm = pe.transpose(MISC[:, t * P:(t + 1) * P], y[:, t, :], ident)
                mm.then_inc(done["ln_turned"], 1)

            def turn_on(n):
                for t in range(NT):
                    mm = pe.transpose(bank[0][:, t * P:(t + 1) * P], on[:, t, 0:D], ident)
                mm.then_inc(done["on_turned"], 1)
                pe.wait_ge(done["onT_ready"], n + 1)

            with pe.Fori(0, B) as b:
                pe.wait_ge(done["ctx_loaded"], 16)
                for t in range(NT):
                    mm = pe.transpose(bank[6][:, t * P:(t + 1) * P], ctxs[:, t, :], ident)
                mm.then_inc(done["ctx_turned"], 1)

                turn_ln(0)
                pe.wait_ge(done["ctxT_ready"], 1)
                pe.wait_ge(done["ln_yT"], 1)
                for which in range(2):
                    for part, rhs in enumerate((yT, ctxT, ctxT)):
                        mm = pe.matmul(bank[4][0:4, which * S:(which + 1) * S],
                                       w("l0_gate")[:, part * 8 + which * 4:part * 8 + which * 4 + 4], rhs[:, :],
                                       start=part == 0, stop=part == 2)
                mm.then_inc(done["l0_gates"], 1)
                for h in range(4):
                    r = slice(32 * h, 32 * h + 32)
                    pe.matmul(bank[h][:, 0:S], ctxT[r, 0:P], yT[r, :], start=True, stop=True)
                    mm = pe.matmul(bank[h][:, S:S + P], ctxT[r, P:S], yT[r, P:S], start=True, stop=True)
                mm.then_inc(done["l0_qk"], 1)
                pe.wait_ge(done["l0_rows"], 1)
                for k, row in enumerate((8, 10)):
                    for t in range(NT):
                        mm = pe.transpose(bank[5][:, (k * NT + t) * 4:(k * NT + t) * 4 + 4], l0r[0:4, row, t * P:(t + 1) * P],
                                          ident[0:4, 0:4])
                mm.then_inc(done["l0_cols_turned"], 1)
                for h in range(4):
                    mm = pe.matmul(bank[6 + h // 2][:, (h % 2) * S:(h % 2 + 1) * S], c("sel4", 4)[:, h * P:(h + 1) * P],
                                   l0r[0:4, 9, :], start=True, stop=True)
                mm.then_inc(done["l0_spread"], 1)
                pe.wait_ge(done["l0_cm"], 4)
                for t in range(NT):
                    for h in range(4):
                        o = bank[4 + t][:, h * 33:h * 33 + 33]
                        if t == 0:
                            mm = pe.matmul(o, Cm[:, h, 0:P], Vm[:, 0, h, :], start=True, stop=True)
                        else:
                            pe.matmul(o, Cm[:, h, P:S], Vm[:, 0, h, :], start=True, stop=False)
                            mm = pe.matmul(o, Cm[:, h, S:S + P], Vm[:, 1, h, :], start=False, stop=True)
                    mm.then_inc(done["l0_h"], 1)

                if STAGES > 1:
                    turn_ln(1)
                    pe.wait_ge(done["ln_yT"], 2)
                    for t in range(NT):
                        mm = pe.matmul(bank[0][:, t * 256:(t + 1) * 256], yT[:, t * P:(t + 1) * P], w("l0_wsd"), start=True, stop=True)
                    mm.then_inc(done["l0f_gates"], 1)
                    for t in range(NT):
                        mm = pe.matmul(bank[1 + t][:, :], yT[:, t * P:(t + 1) * P], w("l0_wv"), start=True, stop=True)
                        mm.then_inc(done["l0f_pv"], 1)
                    pe.wait_ge(done["l0f_gcopied"], 1)
                    pe.wait_ge(done["l0f_pvcopied"], 2)

                    def project_qk(h):
                        if some(h):
                            pe.wait_ge(done["l0f_qk_ready"], h)
                        for part, wt in enumerate((w("l0_wq"), w("l0_wk"))):
                            mm = pe.matmul(bank[2][0:64, part * S:(part + 1) * S], wt[:, h * 64:(h + 1) * 64], yT[:, :],
                                           start=True, stop=True)
                        mm.then_inc(done["l0f_qk"], 1)

                    def before_step(i):
                        if i == 0:
                            project_qk(0)
                        if i + 1 < 16:
                            project_qk(i + 1)
                        if i < 16:
                            pe.wait_ge(done["l0f_qk_ready"], i + 1)
                        if i == 2:
                            pe.wait_ge(done["filled"], 2)
                        if i == 3:
                            pe.wait_ge(done["l0f_vdve"], 4)
                            pe.wait_ge(done["l0f_vpool"], 4)

                    pe_attention(pe, A0, V64, before=before_step)
                    for t in range(NT):
                        pe.wait_ge(done[("l0f_gdve", "l0f_gpool")[t]], 4)
                        for q in range(4):
                            mm = pe.transpose(bank[t][:, q * P:(q + 1) * P], pv[:, t, q * P:(q + 1) * P], ident)
                        mm.then_inc(done["l0f_gturned"], 1)
                    pe.wait_ge(done["l0f_gT"], 2)
                    for t in range(NT):
                        for q in range(4):
                            mm = pe.matmul(bank[2][:, t * P:(t + 1) * P], GT[:, q, t * P:(t + 1) * P], w("l0_wo")[:, q * D:(q + 1) * D],
                                           start=q == 0, stop=q == 3)
                    mm.then_inc(done["projected"], 1)

                if STAGES > 2:
                    turn_ln(2)
                    for g in range(4):
                        if g == 0:
                            for gg in range(4):
                                mm = pe.matmul(bank[3 + gg // 2][:, (gg % 2) * S:(gg % 2 + 1) * S], w("l1_wk")[:, gg * P:(gg + 1) * P],
                                               ctxT[:, :], start=True, stop=True)
                            mm.then_inc(done["l1_k"], 1)
                            for t in range(NT):
                                mm = pe.matmul(bank[5][:, t * D:(t + 1) * D], ctxT[:, t * P:(t + 1) * P], w("l1_wv"),
                                               start=True, stop=True)
                            mm.then_inc(done["l1_v"], 1)
                            pe.wait_ge(done["ln_yT"], 3)
                        mm = pe.matmul(bank[g // 2][:, (g % 2) * S:(g % 2 + 1) * S], w("l1_wq")[:, g * P:(g + 1) * P], yT[:, :],
                                       start=True, stop=True)
                    mm.then_inc(done["l1_q"], 1)
                    pe.wait_ge(done["l1_q_ready"], 1)
                    pe.wait_ge(done["l1_kv_ready"], 1)
                    pe.wait_ge(done["neg_ready"], 1)
                    pe_attention(pe, A1, V8x, masks=(negS, negT))
                    pe.wait_ge(done["normed"], 10)
                    turn_on(0)
                    for t in range(NT):
                        mm = pe.matmul(bank[1][:, t * P:(t + 1) * P], onT[:, t * P:(t + 1) * P], w("l1_wo"), start=True, stop=True)
                    mm.then_inc(done["projected"], 1)

                if STAGES > 3:
                    turn_ln(3)
                    pe.wait_ge(done["ln_yT"], 4)
                    for t in range(NT):
                        mm = pe.matmul(bank[2][:, t * 64:(t + 1) * 64], yT[:, t * P:(t + 1) * P], w("l1f_rw1"), start=True, stop=True)
                    mm.then_inc(done["l1f_r1"], 1)
                    pe.wait_ge(done["l1f_r1n"], 1)
                    for t in range(NT):
                        mm = pe.transpose(bank[3][0:64, t * P:(t + 1) * P], r1[:, t, :], ident)
                    mm.then_inc(done["l1f_r1turned"], 1)
                    pe.wait_ge(done["l1f_r1T"], 1)
                    for t in range(NT):
                        mm = pe.matmul(bank[2][:, 128 + t * E:128 + (t + 1) * E], r1T[:, t * P:(t + 1) * P], w("l1f_rw2", 64),
                                       start=True, stop=True)
                    mm.then_inc(done["router_logits"], 1)
                    pe.wait_ge(done["gates_ready"], 1)
                    for t in range(NT):
                        mm = pe.transpose(bank[3][0:E, t * P:(t + 1) * P], gates[:, t, :], ident)
                    mm.then_inc(done["gates_turned"], 1)
                    pe.wait_ge(done["gatesT_ready"], 1)
                    body_pe(pe, -1, False, False, True)
                    body_pe(pe, 0, False, True, True)
                    with pe.Fori(1, E - 1) as e:
                        body_pe(pe, e, True, True, True)
                    body_pe(pe, E - 1, True, True, False)
                    body_pe(pe, E, True, False, False)
                    for t in range(NT):
                        mm = pe.matmul(bank[6][:, t * P:(t + 1) * P], gatesT[:, t * P:(t + 1) * P], out_bias1[:, :],
                                       start=True, stop=True)
                    mm.then_inc(done["l1f_bias"], 1)

                if STAGES > 4:
                    turn_ln(4)
                    for g in range(2):
                        mm = pe.matmul(bank[1][:, g * S:(g + 1) * S], w("l2_wk")[:, g * P:(g + 1) * P], ctxT[:, :], start=True, stop=True)
                    for t in range(NT):
                        mm = pe.matmul(bank[2][:, t * D:(t + 1) * D], ctxT[:, t * P:(t + 1) * P], w("l2_wv"), start=True, stop=True)
                    mm.then_inc(done["l2_kv"], 1)
                    pe.wait_ge(done["ln_yT"], 5)
                    for g in range(2):
                        mm = pe.matmul(bank[0][:, g * S:(g + 1) * S], w("l2_wq")[:, g * P:(g + 1) * P], yT[:, :], start=True, stop=True)
                    mm.then_inc(done["l2_q"], 1)
                    pe.wait_ge(done["l2_q_ready"], 1)
                    pe.wait_ge(done["l2_kv_ready"], 1)
                    pe_attention(pe, A2, V16)

                if STAGES > 5:
                    turn_ln(5)
                    pe.wait_ge(done["ln_yT"], 6)
                    for t in range(NT):
                        mm = pe.matmul(bank[6][:, t * E:(t + 1) * E], yT[:, t * P:(t + 1) * P], w("l2f_router"), start=True, stop=True)
                    mm.then_inc(done["router_logits"], 1)
                    for e in range(E + 1):
                        if e < E:
                            if some(e - 1):
                                pe.wait_ge(done["l2f_gelu"], e - 1)
                            pe.matmul(bank[e % 2][:, 0:S], w("l2f_win")[:, e * P:(e + 1) * P], yT[:, :], start=True, stop=True)\
                                .then_inc(done["l2f_h"], 1)
                        if e >= 1:
                            k = e - 1
                            pe.wait_ge(done["l2f_gelu"], k + 1)
                            if some(k - 1):
                                pe.wait_ge(done["l2f_oadd"], k - 1)
                            for t in range(NT):
                                mm = pe.matmul(bank[2 + k % 2][:, t * P:(t + 1) * P], hT[:, k % 2, 0, t * P:(t + 1) * P],
                                               w("l2f_wout")[:, k * D:(k + 1) * D], start=True, stop=True)
                            mm.then_inc(done["l2f_o"], 1)
                    pe.wait_ge(done["gates_ready"], 2)
                    for t in range(NT):
                        mm = pe.transpose(bank[4][0:E, t * P:(t + 1) * P], gates[:, t, :], ident)
                    mm.then_inc(done["gates_turned"], 1)
                    pe.wait_ge(done["gatesT_ready"], 2)
                    for t in range(NT):
                        mm = pe.matmul(bank[5][:, t * P:(t + 1) * P], gatesT[:, t * P:(t + 1) * P], w("l2f_bout", E), start=True, stop=True)
                    mm.then_inc(done["projected"], 1)

                if STAGES > 6:
                    turn_ln(6)
                    pe.matmul(bank[1][:, 0:S], w("l3_wk"), ctxT[:, :], start=True, stop=True)
                    for t in range(NT):
                        mm = pe.matmul(bank[2][:, t * D:(t + 1) * D], ctxT[:, t * P:(t + 1) * P], w("l3_wv"), start=True, stop=True)
                    pe.wait_ge(done["ln_yT"], 7)
                    pe.matmul(bank[0][:, 0:S], w("l3_wq"), yT[:, :], start=True, stop=True).then_inc(done["l3_qkv"], 1)
                    pe.wait_ge(done["l3_qk_ready"], 2)
                    pe.wait_ge(done["l3_v_ready"], 1)
                    for t in range(NT):
                        mm = pe.matmul(bank[3][:, t * S:(t + 1) * S], qS[:, 0, t * P:(t + 1) * P], kS[:, 0, :], start=True, stop=True)
                    mm.then_inc(done["l3_s"], 1)
                    pe.wait_ge(done["l3_exp"], 2)
                    for t in range(NT):
                        for k in range(NT):
                            mm = pe.transpose(bank[4][:, k * S + t * P:k * S + (t + 1) * P], pr[:, t, k * P:(k + 1) * P], ident)
                    mm.then_inc(done["l3_pturned"], 1)
                    pe.wait_ge(done["l3_pT"], 1)
                    for k in range(NT):
                        mm = pe.matmul(bank[5][:, 0:S], acc[:, k, :], PT[:, 0, k * S:(k + 1) * S], start=k == 0, stop=k == NT - 1)
                    mm.then_inc(done["l3_ctx"], 1)
                    pe.wait_ge(done["l3_ctx_ready"], 1)
                    for t in range(NT):
                        mm = pe.matmul(bank[6][:, t * P:(t + 1) * P], onT[:, t * P:(t + 1) * P], w("l3_wo"), start=True, stop=True)
                    mm.then_inc(done["l3_out"], 1)

                if STAGES > 7:
                    turn_ln(7)
                    pe.wait_ge(done["ln_yT"], 8)
                    for part, name in enumerate(("l3f_wq", "l3f_wqs")):
                        for g in range(4):
                            mm = pe.matmul(bank[2 * part + g // 2][:, (g % 2) * S:(g % 2 + 1) * S], w(name)[:, g * P:(g + 1) * P], yT[:, :],
                                           start=True, stop=True)
                    mm.then_inc(done["rope_q"], 1)
                    for t in range(NT):
                        mm = pe.matmul(bank[6][:, t * D:(t + 1) * D], yT[:, t * P:(t + 1) * P], w("l3f_wv"), start=True, stop=True)
                    mm.then_inc(done["rope_v"], 1)
                    pe.wait_ge(done["rope_q_ready"], 1)
                    for part, name in enumerate(("l3f_wk", "l3f_wks")):
                        for g in range(4):
                            mm = pe.matmul(bank[2 * part + g // 2][:, (g % 2) * S:(g % 2 + 1) * S], w(name)[:, g * P:(g + 1) * P], yT[:, :],
                                           start=True, stop=True)
                    mm.then_inc(done["rope_k"], 1)
                    pe.wait_ge(done["rope_kv_ready"], 1)
                    pe_attention(pe, A3, V8, masks=(causS, causT))
                    pe.wait_ge(done["normed"], 14)
                    turn_on(1)
                    for t in range(NT):
                        mm = pe.matmul(bank[1][:, t * P:(t + 1) * P], onT[:, t * P:(t + 1) * P], w("l3f_wproj"), start=True, stop=True)
                    mm.then_inc(done["projected"], 1)
                    turn_ln(8)
                    pe.wait_ge(done["ln_yT"], 9)
                    for t in range(NT):
                        mm = pe.matmul(bank[6][:, t * E:(t + 1) * E], yT[:, t * P:(t + 1) * P], w("l3f_wgate"), start=True, stop=True)
                    mm.then_inc(done["router_logits"], 1)
                    pe.wait_ge(done["l3f_top"], 1)
                    pe.matmul(bank[7][:, 0:E], c("upto"), coef[:, 0:E], start=True, stop=True)
                    pe.matmul(bank[7][:, E:2 * E], c("ones"), coef[:, 0:E], start=True, stop=False)
                    pe.matmul(bank[7][:, E:2 * E], c("upto"), coef[:, E:2 * E], start=False, stop=True)
                    pe.matmul(bank[7][:, 2 * E:3 * E], c("ones"), coef[:, 0:E], start=True, stop=False)
                    pe.matmul(bank[7][:, 2 * E:3 * E], c("ones"), coef[:, E:2 * E], start=False, stop=True)\
                        .then_inc(done["l3f_count"], 1)
                    for e in range(E + 1):
                        if e < E:
                            if some(4 * (e - 1)):
                                pe.wait_ge(done["l3f_gelu"], 4 * (e - 1))
                            for f in range(4):
                                pe.matmul(bank[2 * (e % 2) + f // 2][:, (f % 2) * S:(f % 2 + 1) * S],
                                          w("l3f_w1")[:, (e * 4 + f) * P:(e * 4 + f + 1) * P], yT[:, :],
                                          start=True, stop=True).then_inc(done["l3f_h"], 1)
                        if e >= 1:
                            k = e - 1
                            pe.wait_ge(done["l3f_gelu"], 4 * (k + 1))
                            if some(k - 1):
                                pe.wait_ge(done["l3f_oadd"], k - 1)
                            for t in range(NT):
                                for f in range(4):
                                    mm = pe.matmul(bank[4 + k % 2][:, t * P:(t + 1) * P], hT[:, k % 2, f, t * P:(t + 1) * P],
                                                   w("l3f_w2")[:, (k * 4 + f) * D:(k * 4 + f + 1) * D], start=f == 0, stop=f == 3)
                            mm.then_inc(done["l3f_o"], 1)
                    pe.wait_ge(done["gates_ready"], 3)
                    for t in range(NT):
                        mm = pe.transpose(bank[6][0:E, t * P:(t + 1) * P], gates[:, t, :], ident)
                    mm.then_inc(done["gates_turned"], 1)
                    pe.wait_ge(done["gatesT_ready"], 3)
                    for t in range(NT):
                        mm = pe.matmul(bank[0][:, t * P:(t + 1) * P], gatesT[:, t * P:(t + 1) * P], w("l3f_b2", E), start=True, stop=True)
                    mm.then_inc(done["projected"], 1)
                end_of_batch(pe)

        @block.scalar
        def _(act):
            act.wait_ge(setup["weights_loaded"], 16)
            act.wait_ge(setup["consts_loaded"], 16)
            act.activation(tanh_gain[:, :], w("gains"), ACT.Tanh).then_inc(setup["setup_act"], 1)
            with act.Fori(0, B) as b:
                def copy_ln(n, scale=None, bias=None):
                    act.wait_ge(done["ln_turned"], n + 1)
                    if scale is None:
                        act.activation(yT[:, :], MISC[:, 0:S], ACT.Copy).then_inc(done["ln_yT"], 1)
                    else:
                        act.activation(yT[:, :], MISC[:, 0:S], ACT.Identity, bias=bias, scale=scale).then_inc(done["ln_yT"], 1)

                def copy_on(n):
                    act.wait_ge(done["on_turned"], n + 1)
                    act.activation(onT[:, :], bank[0][:, 0:S], ACT.Copy).then_inc(done["onT_ready"], 1)

                act.wait_ge(done["ctx_turned"], 1)
                act.activation(ctxT[:, :], bank[6][:, 0:S], ACT.Copy).then_inc(done["ctxT_ready"], 1)
                copy_ln(0)
                act.wait_ge(done["l0_absf"], 1)
                act.activation(l0r[0:4, 3, :], l0r[0:4, 2, :], ACT.Exp, scale=-1.0).then_inc(done["act_step"], 1)
                act.wait_ge(done["act_step"], 1)
                act.activation(l0r[0:4, 4, :], l0r[0:4, 3, :], ACT.Ln, bias=1.0).then_inc(done["l0_softplus"], 1)
                act.wait_ge(done["l0_negm"], 1)
                act.activation(dn[:, 0, :], mcol[:, :, :].rearrange("p t h -> p (t h)"), ACT.Exp).then_inc(done["l0_expm"], 1)
                act.wait_ge(done["l0_args"], 1)
                act.activation(Dm[:, :, :], Dm[:, :, :], ACT.Exp).then_inc(done["l0_decay"], 1)

                if STAGES > 1:
                    copy_ln(1)
                    act.wait_ge(done["l0f_gcopied"], 1)
                    act.activation(gsig[:, :], gv[:, :], ACT.Exp, scale=-1.0).then_inc(done["l0f_sig"], 1)
                    for t in range(NT):
                        act.wait_ge(done["l0f_pv"], t + 1)
                        act.activation(pv[:, t, :], bank[1 + t][:, :], ACT.Copy).then_inc(done["l0f_pvcopied"], 1)

                    def copy_qk(first, last):
                        for h in range(first, min(last, 16)):
                            act.wait_ge(done["l0f_qk"], h + 1)
                            act.activation(qk64[0:64, h % 4, :], bank[2][0:64, :], ACT.Copy).then_inc(done["l0f_qk_ready"], 1)

                    act_attention(act, A0, before=lambda h: copy_qk(h + 3 if h else 0, h + 4))
                    for t in range(NT):
                        act.wait_ge(done["l0f_gturned"], t + 1)
                        act.activation(GT[:, :, t * P:(t + 1) * P], bank[t][:, :].rearrange("p (q s) -> p q s", q=4), ACT.Copy)\
                            .then_inc(done["l0f_gT"], 1)

                if STAGES > 2:
                    copy_ln(2)
                    act.wait_ge(done["l1_q"], 1)
                    for g in range(4):
                        a = act.activation(qS[:, g, :], bank[g // 2][:, (g % 2) * S:(g % 2 + 1) * S], ACT.Identity,
                                           bias=w("l1_qb")[:, g:g + 1])
                    a.then_inc(done["l1_q_ready"], 1)
                    act_attention(act, A1)
                    copy_on(0)

                if STAGES > 3:
                    copy_ln(3)
                    act.wait_ge(done["l1f_r1turned"], 1)
                    act.activation(r1T, bank[3][0:64, 0:S], ACT.Copy).then_inc(done["l1f_r1T"], 1)
                    act.wait_ge(done["router_shifted"], 1)
                    act.activation(gv[:, 0:NT * E], gv[:, 0:NT * E], ACT.Exp).then_inc(done["router_exped"], 1)
                    act.wait_ge(done["gates_turned"], 1)
                    act.activation(gatesT, bank[3][0:E, 0:S], ACT.Copy).then_inc(done["gatesT_ready"], 1)
                    body_act(act, -1, False, False, True)
                    body_act(act, 0, False, True, True)
                    with act.Fori(1, E - 1) as e:
                        body_act(act, e, True, True, True)
                    body_act(act, E - 1, True, True, False)
                    body_act(act, E, True, False, False)

                if STAGES > 4:
                    copy_ln(4)
                    act.wait_ge(done["l2_q"], 1)
                    act.activation(qS[:, 0:2, :], bank[0][:, :].rearrange("p (g s) -> p g s", g=2), ACT.Copy).then_inc(done["l2_q_ready"], 1)
                    act_attention(act, A2)

                if STAGES > 5:
                    copy_ln(5)
                    act.wait_ge(done["router_shifted"], 2)
                    act.activation(gv[:, 0:NT * E], gv[:, 0:NT * E], ACT.Exp).then_inc(done["router_exped"], 1)
                    for e in range(E):
                        act.wait_ge(done["l2f_h"], e + 1)
                        if some(e - 1):
                            act.wait_ge(done["l2f_o"], e - 1)
                        act.activation(hT[:, e % 2, 0, :], bank[e % 2][:, 0:S], ACT.Gelu_apprx_tanh, bias=w("l2f_bin")[:, e:e + 1])\
                            .then_inc(done["l2f_gelu"], 1)
                    act.wait_ge(done["gates_turned"], 2)
                    act.activation(gatesT, bank[4][0:E, 0:S], ACT.Copy).then_inc(done["gatesT_ready"], 1)

                if STAGES > 6:
                    copy_ln(6)
                    act.wait_ge(done["l3_qkv"], 1)
                    act.activation(qS[:, 0, :], bank[0][:, 0:S], ACT.Identity, bias=w("l3_bq")).then_inc(done["l3_qk_ready"], 1)
                    act.activation(kS[:, 0, :], bank[1][:, 0:S], ACT.Copy).then_inc(done["l3_qk_ready"], 1)
                    act.wait_ge(done["l3_smax"], 1)
                    for t in range(NT):
                        act.activation(pr[:, t, :], bank[3][:, t * S:(t + 1) * S], ACT.Exp, scale=D ** -0.5, bias=gs[:, 1, t:t + 1],
                                       accum_out=gs[:, 2, t:t + 1]).then_inc(done["l3_exp"], 1)
                    act.wait_ge(done["l3_pturned"], 1)
                    act.activation(PT[:, 0, :], bank[4][:, :], ACT.Copy).then_inc(done["l3_pT"], 1)
                    act.wait_ge(done["l3_ctx"], 1)
                    act.activation(onT[:, :], bank[5][:, 0:S], ACT.Copy).then_inc(done["l3_ctx_ready"], 1)

                if STAGES > 7:
                    copy_ln(7, w("l3f_ln")[:, 0:1], w("l3f_ln")[:, 1:2])
                    act_attention(act, A3)
                    copy_on(1)
                    copy_ln(8, w("l3f_ln")[:, 2:3], w("l3f_ln")[:, 3:4])
                    act.wait_ge(done["router_shifted"], 3)
                    act.activation(gv[:, 0:NT * E], gv[:, 0:NT * E], ACT.Exp).then_inc(done["router_exped"], 1)
                    for e in range(E):
                        if some(e - 1):
                            act.wait_ge(done["l3f_o"], e - 1)
                        for f in range(4):
                            act.wait_ge(done["l3f_h"], 4 * e + f + 1)
                            if f % 2 == 0:
                                act.wait_ge(done["l3f_h"], 4 * e + f + 2)
                            act.activation(hT[:, e % 2, f, :], bank[2 * (e % 2) + f // 2][:, (f % 2) * S:(f % 2 + 1) * S], ACT.Gelu,
                                           bias=w("l3f_b1")[:, e * 4 + f:e * 4 + f + 1]).then_inc(done["l3f_gelu"], 1)
                    act.wait_ge(done["gates_turned"], 3)
                    act.activation(gatesT, bank[6][0:E, 0:S], ACT.Copy).then_inc(done["gatesT_ready"], 1)
                end_of_batch(act)

        @block.gpsimd
        def _(pool):
            pool.memset(minus_half[:, :], -0.5).then_inc(setup["setup_pool"], 1)
            pool.wait_ge(setup["setup_pool"], 1)
            with pool.Fori(0, B) as b:
                steps = [0]

                def link(ins):
                    steps[0] += 1
                    ins.then_inc(done["pool_step"], 1)
                    pool.wait_ge(done["pool_step"], steps[0])

                def inv_sqrt(out, var, eps, n):
                    link(pool.tensor_scalar(out, var, eps, None, ALU.add))
                    return pool.tensor_tensor(out, out, minus_half[:, 0:n], ALU.pow)

                def ln_rstd(n, eps=1e-5):
                    pool.wait_ge(done["ln_var"], n + 1)
                    inv_sqrt(rstd[:, :], mv[:, :, 1], eps, NT).then_inc(done["ln_rstd"], 1)

                pool.wait_ge(done["x_loaded"], 16)
                pool.memset(V64[:, :, :, 64:65], 1.0).then_inc(done["filled"], 1)
                pool.wait_ge(done["filled"], 1)
                pool.memset(qk64[64:65, :, S:2 * S], 1.0).then_inc(done["filled"], 1)
                pool.wait_ge(done["filled"], 2)
                ln_rstd(0)
                pool.wait_ge(done["l0_decay"], 1)
                for a in (0, S):
                    pool.tensor_tensor(Dm[:, :, a:a + P], Dm[:, :, a:a + P], c("upto").unsqueeze(1).broadcast_to([P, 4, P]), ALU.mult)\
                        .then_inc(done["l0_decay_masked"], 1)
                pool.wait_ge(done["l0_hstat"], 1)
                inv_sqrt(rstd8[:, :], mv8[:, :, 1], 1e-6, 8).then_inc(done["l0_hrstd"], 1)

                def pool_mix(coef_of, values, dst, signal, n_in):
                    n_out = 32 // n_in
                    m = mixP.rearrange("p (o i d) -> p o i d", i=n_in, d=64)
                    link(pool.tensor_tensor(m, coef_of, values, ALU.mult))
                    k = n_in // 2
                    while k > 1:
                        link(pool.tensor_tensor(m[:, :, 0:k, :], m[:, :, 0:k, :], m[:, :, k:2 * k, :], ALU.add))
                        k //= 2
                    link(pool.tensor_tensor(dst, m[:, :, 0, :], m[:, :, 1, :], ALU.add))
                    pool.sem_inc(done[signal], 1)

                if STAGES > 1:
                    ln_rstd(1)
                    pool.wait_ge(done["l0f_coef"], 1)
                    pool.wait_ge(done["l0f_pvcopied"], 2)
                    co = coef[:, :].rearrange("p (t k h e) -> p t k h e", t=NT, k=2, h=16)
                    for part in range(4):
                        hs = slice(4 * part, 4 * part + 4)
                        pool_mix(co[:, 1, 0, hs, :].unsqueeze(3).broadcast_to([P, 4, 8, 64]),
                                 pv[:, 1, :].rearrange("p (e d) -> p e d", e=8).unsqueeze(1).broadcast_to([P, 4, 8, 64]),
                                 V64[:, 1, hs, 0:64], "l0f_vpool", 8)
                    pool.wait_ge(done["l0f_vdve"], 4)
                    pool.wait_ge(done["normed"], 8)
                    for part in range(4):
                        es = slice(2 * part, 2 * part + 2)
                        pool_mix(co[:, 1, 1, :, es].rearrange("p h e -> p e h").unsqueeze(3).broadcast_to([P, 2, 16, 64]),
                                 on[:, 1, :].rearrange("p (h d) -> p h d", h=16).unsqueeze(1).broadcast_to([P, 2, 16, 64]),
                                 pv[:, 1, :].rearrange("p (e d) -> p e d", e=8)[:, es, :], "l0f_gpool", 16)
                if STAGES > 2:
                    pool.memset(V8x, 0.0).then_inc(done["filled"], 1)
                    ln_rstd(2)
                    pool.wait_ge(done["gp_loaded"], 16)
                    pool_attention(pool, A1)
                if STAGES > 3:
                    ln_rstd(3)
                    pool.wait_ge(done["l1f_rvar"], 1)
                    inv_sqrt(rstd[:, :], mv[:, :, 1], 1e-5, NT).then_inc(done["l1f_rrstd"], 1)
                    body_pool(pool, -1, False)
                    body_pool(pool, 0, True)
                    with pool.Fori(1, E - 1) as e:
                        body_pool(pool, e, True)
                if STAGES > 4:
                    ln_rstd(4)
                if STAGES > 5:
                    ln_rstd(5)
                if STAGES > 6:
                    ln_rstd(6)
                if STAGES > 7:
                    ln_rstd(7)
                    ln_rstd(8)
                    ln_rstd(9)
                end_of_batch(pool)

        @block.vector
        def _(dve):
            n_setup = [0]

            def slink(ins):
                n_setup[0] += 1
                ins.then_inc(setup["setup_dve"], 1)

            dve.wait_ge(setup["consts_loaded"], 16)
            slink(dve.tensor_copy(ident_bf[:, :], ident))
            dve.wait_ge(setup["causal_loaded"], 16)
            slink(dve.tensor_copy(causS[:, :, :], mixD[:, 0:512].rearrange("p (t s) -> p t s", t=NT)))
            slink(dve.tensor_copy(causT[:, :, :], mixD[:, 512:1024].rearrange("p (t s) -> p t s", t=NT)))
            for k in (8, 16, 64):
                slink(dve.memset(negmax[k][:, :, :, :], 0.0))
            for V, k in ((V8, 8), (V16, 16)):
                slink(dve.memset(V[:, :, :, :], 0.0))
                dve.wait_ge(setup["setup_dve"], n_setup[0])
                slink(dve.memset(V[:, :, :, k:k + 1], 1.0))
            slink(dve.memset(Vm[:, :, :, 32:33], 1.0))
            slink(dve.memset(carry[:, :], 0.0))
            slink(dve.memset(negmax_bf[:, :, :, :], 0.0))
            slink(dve.memset(kone[:, 0:1], 0.0))
            slink(dve.tensor_copy(kone[:, 1:2], c("kones_stack")))
            assert n_setup[0] == SETUP_DVE, n_setup[0]
            dve.wait_ge(setup["setup_dve"], n_setup[0])
            dve.wait_ge(setup["setup_pe"], 1)
            dve.wait_ge(setup["weights_loaded"], 16)
            dve.wait_ge(setup["setup_act"], 1)
            dve.tensor_tensor(out_bias1[:, :], bank[0][0:E, 0:D], w("l1f_ob", E), ALU.add).then_inc(setup["setup_dve"], 1)
            dve.wait_ge(setup["setup_dve"], n_setup[0] + 1)

            with dve.Fori(0, B) as b:
                steps = [0]

                def link(ins):
                    steps[0] += 1
                    ins.then_inc(done["dve_step"], 1)
                    dve.wait_ge(done["dve_step"], steps[0])

                def layernorm(n, src, dst=y):
                    for t in range(NT):
                        ins = dve.bn_stats(bn[:, t, :], src[:, t, :])
                        if t == 0:
                            ins.then_inc(done["dve_step"], 1)
                            steps[0] += 1
                        else:
                            link(ins)
                    for t in range(NT):
                        ins = dve.bn_aggr(mv[:, t, :], bn[:, t, :])
                    ins.then_inc(done["ln_var"], 1)
                    dve.wait_ge(done["ln_rstd"], n + 1)
                    dve.wait_ge(done["ln_var"], n + 1)
                    for t in range(NT):
                        ins = dve.tensor_scalar(dst[:, t, :], src[:, t, :], mv[:, t, 0:1], rstd[:, t:t + 1], ALU.subtract, ALU.mult)
                        if t == 0:
                            ins.then_inc(done["dve_step"], 1)
                            steps[0] += 1
                    return ins

                def add_to_x(src, k):
                    link(dve.scalar_tensor_tensor(xs[:, :, :], src, tanh_gain[:, k:k + 1], xs[:, :, :], ALU.mult, ALU.add))

                def top2(v, n, mask):
                    v3 = v.rearrange("p (n e) -> p n e", e=8)
                    A_, B_, C_, D_ = (t2[:, k, 0:8 * n].rearrange("p (n e) -> p n e", e=8) for k in range(4))
                    m, k1 = t2s[:, 0, 0:n].unsqueeze(2), t2s[:, 1, 0:n].unsqueeze(2)
                    rank = c("rank").unsqueeze(1).broadcast_to([P, n, 8])
                    mask3 = mask.rearrange("p (n e) -> p n e", e=8)
                    src = v3
                    for r, hot in enumerate((A_, B_)):
                        link(dve.tensor_reduce(m, src, X_AXIS, ALU.max))
                        link(dve.tensor_tensor(C_, src, m.broadcast_to([P, n, 8]), ALU.is_ge))
                        link(dve.tensor_tensor(C_, C_, rank, ALU.mult))
                        link(dve.tensor_reduce(k1, C_, X_AXIS, ALU.max))
                        link(dve.tensor_tensor(hot, C_, k1.broadcast_to([P, n, 8]), ALU.is_equal))
                        if r == 0:
                            link(dve.scalar_tensor_tensor(D_, hot, -BIG, v3, ALU.mult, ALU.add))
                            src = D_
                    link(dve.tensor_tensor(mask3, A_, B_, ALU.add))

                def routing(n, logits, bias=None):
                    dve.wait_ge(done["router_logits"], n)
                    L = gv[:, 0:NT * E]
                    L3 = L.rearrange("p (t e) -> p t e", e=E)
                    if bias is None:
                        link(dve.tensor_copy(L, logits))
                    else:
                        link(dve.tensor_tensor(L3, logits.rearrange("p (t e) -> p t e", e=E), bias.unsqueeze(1).broadcast_to([P, NT, E]), ALU.add))
                    top2(L, NT, coef[:, 0:NT * E])
                    link(dve.tensor_reduce(gs[:, 0, :].unsqueeze(2), L3, X_AXIS, ALU.max))
                    dve.tensor_tensor(L3, L3, gs[:, 0, :].unsqueeze(2).broadcast_to([P, NT, E]), ALU.subtract)\
                        .then_inc(done["router_shifted"], 1)
                    dve.wait_ge(done["router_exped"], n)
                    return L3

                dve.wait_ge(done["x_loaded"], 16)
                layernorm(0, xs).then_inc(done["ln_y"], 1)
                dve.wait_ge(done["ctx_loaded"], 16)
                link(dve.tensor_copy(Vm[:, :, :, 0:32], ctxs[:, :, :].rearrange("p t (h d) -> p t h d", h=4)))
                dve.wait_ge(done["l0_gates"], 1)
                R = l0r[0:4, :, :]
                link(dve.tensor_scalar(R[:, 0, :], bank[4][0:4, 0:S], w("l0_bias", 4)[:, 0:1], None, ALU.add))
                link(dve.tensor_scalar(R[:, 1, :], bank[4][0:4, S:2 * S], w("l0_bias", 4)[:, 1:2], None, ALU.add))
                dve.scalar_tensor_tensor(R[:, 2, :], R[:, 1, :], -1.0, R[:, 1, :], ALU.mult, ALU.max).then_inc(done["l0_absf"], 1)
                dve.wait_ge(done["l0_softplus"], 1)
                link(dve.scalar_tensor_tensor(R[:, 5, :], R[:, 1, :], 0.0, R[:, 4, :], ALU.min, ALU.subtract))
                link(dve.tensor_tensor_scan(R[:, 6, :], c("ones", 4)[:, 0:1].broadcast_to([4, S]), R[:, 5, :], 0.0, ALU.mult, ALU.add))
                link(dve.tensor_tensor(R[:, 8, :], R[:, 0, :], R[:, 6, :], ALU.subtract))
                link(dve.tensor_tensor_scan(R[:, 7, :], c("ones", 4)[:, 0:1].broadcast_to([4, S]), R[:, 8, :], -3.0e38, ALU.mult, ALU.max))
                link(dve.tensor_scalar(R[:, 9, :], R[:, 7, :], -1.0, None, ALU.mult))
                dve.tensor_tensor(R[:, 10, :], R[:, 9, :], R[:, 6, :], ALU.subtract).then_inc(done["l0_rows"], 1)
                dve.wait_ge(done["l0_cols_turned"], 1)
                link(dve.tensor_copy(gcol[:, :, :], bank[5][:, 0:8].rearrange("p (t h) -> p t h", t=NT)))
                dve.tensor_copy(mcol[:, :, :], bank[5][:, 8:16].rearrange("p (t h) -> p t h", t=NT)).then_inc(done["l0_negm"], 1)
                dve.wait_ge(done["l0_spread"], 1)
                for h in range(4):
                    src = bank[6 + h // 2][:, (h % 2) * S:(h % 2 + 1) * S]
                    dve.tensor_scalar(Dm[:, h, 0:S], src, gcol[:, 0, h:h + 1], 0.0, ALU.add, ALU.min)
                    ins = dve.tensor_scalar(Dm[:, h, S:S + P], src[:, P:S], gcol[:, 1, h:h + 1], 0.0, ALU.add, ALU.min)
                ins.then_inc(done["l0_args"], 1)
                dve.wait_ge(done["l0_qk"], 1)
                dve.wait_ge(done["l0_decay"], 1)
                dve.wait_ge(done["l0_decay_masked"], 2)
                for h in range(4):
                    dve.scalar_tensor_tensor(Cm[:, h, :], bank[h][:, 0:384], 32 ** -0.5, Dm[:, h, :], ALU.mult, ALU.mult)\
                        .then_inc(done["l0_cm"], 1)
                dve.wait_ge(done["l0_expm"], 1)
                for t in range(NT):
                    dve.wait_ge(done["l0_h"], t + 1)
                    T = bank[4 + t][:, 0:132].rearrange("p (h c) -> p h c", c=33)
                    d = dn[:, 1, 4 * t:4 * t + 4]
                    link(dve.tensor_copy(d.unsqueeze(2), T[:, :, 32:33]))
                    link(dve.scalar_tensor_tensor(dn[:, 2, 0:4], d, -1.0, d, ALU.mult, ALU.max))
                    link(dve.tensor_tensor(dn[:, 2, 0:4], dn[:, 2, 0:4], dn[:, 0, 4 * t:4 * t + 4], ALU.max))
                    link(dve.tensor_scalar(dn[:, 2, 0:4], dn[:, 2, 0:4], 1e-6, None, ALU.add))
                    link(dve.reciprocal(dn[:, 3, 0:4], dn[:, 2, 0:4]))
                    link(dve.tensor_tensor(hh[:, t, :, :], T[:, :, 0:32], dn[:, 3, 0:4].unsqueeze(2).broadcast_to([P, 4, 32]), ALU.mult))
                H = hh[:, :, :, :].rearrange("p t h d -> p (t h) d")
                for k in range(8):
                    ins = dve.bn_stats(bn8[:, k, :], H[:, k, :])
                link(ins)
                for k in range(8):
                    ins = dve.bn_aggr(mv8[:, k, :], bn8[:, k, :])
                ins.then_inc(done["l0_hstat"], 1)
                dve.wait_ge(done["l0_hrstd"], 1)
                dve.wait_ge(done["l0_hstat"], 1)
                link(dve.tensor_tensor(H, H, mv8[:, :, 0:1].broadcast_to([P, 8, 32]), ALU.subtract))
                link(dve.tensor_tensor(H, H, rstd8[:, :].unsqueeze(2).broadcast_to([P, 8, 32]), ALU.mult))
                H2 = hh[:, :, :, :].rearrange("p t h d -> p t (h d)")
                link(dve.tensor_tensor(H2, H2, w("l0_outnorm").unsqueeze(1).broadcast_to([P, NT, D]), ALU.mult))
                add_to_x(H2, 0)

                def dve_mix(coef_of, values, dst, signal, n_in):
                    m = mixD.rearrange("p (o i d) -> p o i d", i=n_in, d=64)
                    link(dve.tensor_tensor(m, coef_of, values, ALU.mult))
                    dve.tensor_reduce(dst.unsqueeze(3), m.rearrange("p o i d -> p o d i"), X_AXIS, ALU.add).then_inc(done[signal], 1)

                if STAGES > 1:
                    layernorm(1, xs).then_inc(done["ln_y"], 1)
                    dve.wait_ge(done["l0f_gates"], 1)
                    dve.tensor_copy(gv[:, :], bank[0][:, :]).then_inc(done["l0f_gcopied"], 1)
                    dve.wait_ge(done["l0f_gcopied"], 1)
                    top2(gv[:, :], 64, coef[:, :])
                    dve.wait_ge(done["l0f_sig"], 1)
                    link(dve.tensor_scalar(gsig[:, :], gsig[:, :], 1.0, None, ALU.add))
                    link(dve.reciprocal(gsig[:, :], gsig[:, :]))
                    for t in range(NT):
                        a = coef[:, t * 256:t * 256 + 128]
                        ins = dve.tensor_tensor(a, a, gsig[:, t * 256:t * 256 + 128], ALU.mult)
                    ins.then_inc(done["l0f_coef"], 1)
                    dve.wait_ge(done["l0f_coef"], 1)
                    dve.wait_ge(done["l0f_pvcopied"], 2)
                    co = coef[:, :].rearrange("p (t k h e) -> p t k h e", t=NT, k=2, h=16)
                    for part in range(4):
                        hs = slice(4 * part, 4 * part + 4)
                        if some(part):
                            dve.wait_ge(done["l0f_vdve"], part)
                        dve_mix(co[:, 0, 0, hs, :].unsqueeze(3).broadcast_to([P, 4, 8, 64]),
                                pv[:, 0, :].rearrange("p (e d) -> p e d", e=8).unsqueeze(1).broadcast_to([P, 4, 8, 64]),
                                V64[:, 0, hs, 0:64], "l0f_vdve", 8)
                    dve_attention(dve, A0, link)
                    dve.wait_ge(done["normed"], 8)
                    dve.wait_ge(done["l0f_vdve"], 4)
                    for part in range(4):
                        es = slice(2 * part, 2 * part + 2)
                        if some(part):
                            dve.wait_ge(done["l0f_gdve"], part)
                        dve_mix(co[:, 0, 1, :, es].rearrange("p h e -> p e h").unsqueeze(3).broadcast_to([P, 2, 16, 64]),
                                on[:, 0, :].rearrange("p (h d) -> p h d", h=16).unsqueeze(1).broadcast_to([P, 2, 16, 64]),
                                pv[:, 0, :].rearrange("p (e d) -> p e d", e=8)[:, es, :], "l0f_gdve", 16)
                    dve.wait_ge(done["projected"], 1)
                    add_to_x(bank[2][:, 0:S].rearrange("p (t d) -> p t d", t=NT), 1)

                if STAGES > 2:
                    layernorm(2, xs).then_inc(done["ln_y"], 1)
                    dve.wait_ge(done["mask_loaded"], 16)
                    dve.wait_ge(done["maskT_loaded"], 16)
                    for src, dst in ((mask_i, negS), (maskT_i, negT)):
                        ins = dve.tensor_scalar(dst[:, :, :], src, 1.0, -NEG_MASK * 8 ** 0.5, ALU.subtract, ALU.mult)
                    ins.then_inc(done["neg_ready"], 1)
                    dve.wait_ge(done["l1_k"], 1)
                    for g in range(4):
                        dve.tensor_scalar(kS[:, g, :], bank[3 + g // 2][:, (g % 2) * S:(g % 2 + 1) * S], w("l1_kb")[:, g:g + 1], None, ALU.add)
                    dve.wait_ge(done["l1_v"], 1)
                    dve.wait_ge(done["filled"], 3)
                    for t in range(NT):
                        ins = dve.tensor_tensor(V8x[:, t, :, 0:8], bank[5][:, t * D:(t + 1) * D].rearrange("p (h d) -> p h d", d=8),
                                                w("l1_vb").rearrange("p (h d) -> p h d", d=8), ALU.add)
                    ins.then_inc(done["l1_kv_ready"], 1)
                    dve_attention(dve, A1, link)
                    dve.wait_ge(done["projected"], 2)
                    link(dve.tensor_tensor(tmp[:, :, :], bank[1][:, 0:S].rearrange("p (t d) -> p t d", t=NT),
                                           w("l1_bo").unsqueeze(1).broadcast_to([P, NT, D]), ALU.add))
                    add_to_x(tmp[:, :, :], 2)

                if STAGES > 3:
                    layernorm(3, xs).then_inc(done["ln_y"], 1)
                    dve.memset(acc[:, :, :], 0.0).then_inc(done["ex_added"], 1)
                    dve.wait_ge(done["l1f_r1"], 1)
                    link(dve.tensor_tensor(r1, bank[2][:, 0:128].rearrange("p (t d) -> p t d", t=NT),
                                           w("l1f_rb1").unsqueeze(1).broadcast_to([P, NT, 64]), ALU.add))
                    for t in range(NT):
                        link(dve.bn_stats(bn[:, t, :], r1[:, t, :]))
                    for t in range(NT):
                        ins = dve.bn_aggr(mv[:, t, :], bn[:, t, :])
                    ins.then_inc(done["l1f_rvar"], 1)
                    dve.wait_ge(done["l1f_rrstd"], 1)
                    dve.wait_ge(done["l1f_rvar"], 1)
                    for t in range(NT):
                        link(dve.tensor_scalar(r1[:, t, :], r1[:, t, :], mv[:, t, 0:1], rstd[:, t:t + 1], ALU.subtract, ALU.mult))
                    link(dve.tensor_tensor(r1, r1, w("l1f_lng").unsqueeze(1).broadcast_to([P, NT, 64]), ALU.mult))
                    link(dve.tensor_tensor(r1, r1, w("l1f_lnb").unsqueeze(1).broadcast_to([P, NT, 64]), ALU.add))
                    dve.tensor_scalar(r1, r1, 0.0, None, ALU.max).then_inc(done["l1f_r1n"], 1)
                    L3 = routing(1, bank[2][:, 128:128 + NT * E], w("l1f_rb2"))
                    M3 = coef[:, 0:NT * E].rearrange("p (t e) -> p t e", e=E)
                    link(dve.tensor_tensor(gates[:, :, :], L3, M3, ALU.mult))
                    link(dve.tensor_reduce(gs[:, 1, :].unsqueeze(2), gates[:, :, :], X_AXIS, ALU.add))
                    link(dve.reciprocal(gs[:, 2, :], gs[:, 1, :]))
                    dve.tensor_tensor(gates[:, :, :], gates[:, :, :], gs[:, 2, :].unsqueeze(2).broadcast_to([P, NT, E]), ALU.mult)\
                        .then_inc(done["gates_ready"], 1)
                    dve.wait_ge(done["gates_ready"], 1)
                    body_dve(dve, -1, False, False, True)
                    body_dve(dve, 0, False, True, True)
                    with dve.Fori(1, E - 1) as e:
                        body_dve(dve, e, True, True, True)
                    body_dve(dve, E - 1, True, True, False)
                    body_dve(dve, E, True, False, False)
                    dve.wait_ge(done["ex_added"], E + 1)
                    dve.wait_ge(done["l1f_bias"], 1)
                    link(dve.tensor_tensor(acc[:, :, :], acc[:, :, :], bank[6][:, 0:S].rearrange("p (t d) -> p t d", t=NT), ALU.add))
                    add_to_x(acc[:, :, :], 3)

                if STAGES > 4:
                    layernorm(4, xs).then_inc(done["ln_y"], 1)
                    dve.wait_ge(done["l2_kv"], 1)
                    dve.tensor_scalar(kS[:, 0:2, :], bank[1][:, :].rearrange("p (g s) -> p g s", g=2), c("kones16"), None, ALU.add)
                    dve.tensor_copy(V16[:, :, :, 0:16], bank[2][:, 0:S].rearrange("p (t h d) -> p t h d", t=NT, d=16))\
                        .then_inc(done["l2_kv_ready"], 1)
                    dve_attention(dve, A2, link)
                    dve.wait_ge(done["normed"], A2.nb + 2)
                    add_to_x(on[:, :, 0:D], 4)

                if STAGES > 5:
                    layernorm(5, xs).then_inc(done["ln_y"], 1)
                    L3 = routing(2, bank[6][:, 0:NT * E])
                    M3 = coef[:, 0:NT * E].rearrange("p (t e) -> p t e", e=E)
                    link(dve.tensor_reduce(gs[:, 1, :].unsqueeze(2), L3, X_AXIS, ALU.add))
                    link(dve.reciprocal(gs[:, 2, :], gs[:, 1, :]))
                    link(dve.tensor_tensor(gates[:, :, :], L3, M3, ALU.mult))
                    dve.tensor_tensor(gates[:, :, :], gates[:, :, :], gs[:, 2, :].unsqueeze(2).broadcast_to([P, NT, E]), ALU.mult)\
                        .then_inc(done["gates_ready"], 1)
                    dve.wait_ge(done["gates_ready"], 2)
                    link(dve.memset(acc[:, :, :], 0.0))
                    for e in range(E):
                        dve.wait_ge(done["l2f_o"], e + 1)
                        if some(e):
                            dve.wait_ge(done["l2f_oadd"], e)
                        for t in range(NT):
                            ins = dve.scalar_tensor_tensor(acc[:, t, :], bank[2 + e % 2][:, t * P:(t + 1) * P], gates[:, t, e:e + 1],
                                                           acc[:, t, :], ALU.mult, ALU.add)
                        ins.then_inc(done["l2f_oadd"], 1)
                    dve.wait_ge(done["l2f_oadd"], E)
                    dve.wait_ge(done["projected"], 3)
                    link(dve.tensor_tensor(acc[:, :, :], acc[:, :, :], bank[5][:, 0:S].rearrange("p (t d) -> p t d", t=NT), ALU.add))
                    add_to_x(acc[:, :, :], 5)

                if STAGES > 6:
                    layernorm(6, xs).then_inc(done["ln_y"], 1)
                    dve.wait_ge(done["l3_qkv"], 1)
                    dve.tensor_tensor(acc[:, :, :], bank[2][:, 0:S].rearrange("p (t d) -> p t d", t=NT),
                                      w("l3_bv").unsqueeze(1).broadcast_to([P, NT, D]), ALU.add).then_inc(done["l3_v_ready"], 1)
                    dve.wait_ge(done["l3_s"], 1)
                    link(dve.tensor_reduce(gs[:, 0, :].unsqueeze(2), bank[3][:, :].rearrange("p (t s) -> p t s", t=NT), X_AXIS, ALU.max))
                    dve.tensor_scalar(gs[:, 1, :], gs[:, 0, :], -D ** -0.5, None, ALU.mult).then_inc(done["l3_smax"], 1)
                    dve.wait_ge(done["l3_exp"], 2)
                    link(dve.reciprocal(gs[:, 3, :], gs[:, 2, :]))
                    dve.wait_ge(done["l3_out"], 1)
                    for t in range(NT):
                        link(dve.scalar_tensor_tensor(tmp[:, t, :], bank[6][:, t * P:(t + 1) * P], gs[:, 3, t:t + 1], w("l3_bo"),
                                                      ALU.mult, ALU.add))
                    add_to_x(tmp[:, :, :], 6)

                if STAGES > 7:
                    link(layernorm(7, xs, x1))
                    layernorm(8, x1).then_inc(done["ln_y"], 1)
                    for name, dst, extra in (("rope_q", qS, "zero"), ("rope_k", kS, "kones8")):
                        dve.wait_ge(done[name], 1)
                        for g in range(4):
                            cols = slice((g % 2) * S, (g % 2 + 1) * S)
                            link(dve.tensor_tensor(pr[:, 0, :], bank[g // 2][:, cols], c("cos"), ALU.mult))
                            link(dve.tensor_tensor(pr[:, 1, :], bank[2 + g // 2][:, cols], c("sin"), ALU.mult))
                            ins = dve.scalar_tensor_tensor(dst[:, g, :], pr[:, 0, :], c(extra), pr[:, 1, :], ALU.add, ALU.add)
                            if g < 3:
                                link(ins)
                        if name == "rope_q":
                            ins.then_inc(done["rope_q_ready"], 1)
                            dve.wait_ge(done["rope_q_ready"], 1)
                            dve.wait_ge(done["rope_v"], 1)
                            link(dve.tensor_copy(V8[:, :, :, 0:8], bank[6][:, 0:S].rearrange("p (t h d) -> p t h d", t=NT, d=8)))
                        else:
                            ins.then_inc(done["rope_kv_ready"], 1)
                    dve_attention(dve, A3, link)
                    dve.wait_ge(done["projected"], 4)
                    link(dve.tensor_tensor(x1[:, :, :], x1[:, :, :], bank[1][:, 0:S].rearrange("p (t d) -> p t d", t=NT), ALU.add))
                    layernorm(9, x1).then_inc(done["ln_y"], 1)
                    L3 = routing(3, bank[6][:, 0:NT * E])
                    M3 = coef[:, 0:NT * E].rearrange("p (t e) -> p t e", e=E)
                    dve.sem_inc(done["l3f_top"], 1)
                    link(dve.tensor_reduce(gs[:, 1, :].unsqueeze(2), L3, X_AXIS, ALU.add))
                    link(dve.reciprocal(gs[:, 2, :], gs[:, 1, :]))
                    link(dve.tensor_tensor(gates[:, :, :], L3, gs[:, 2, :].unsqueeze(2).broadcast_to([P, NT, E]), ALU.mult))
                    dve.wait_ge(done["l3f_count"], 1)
                    K3 = gsig[:, 0:NT * E].rearrange("p (t e) -> p t e", e=E)
                    link(dve.tensor_tensor(K3, bank[7][:, 0:2 * E].rearrange("p (t e) -> p t e", e=E),
                                           carry[:, :].unsqueeze(1).broadcast_to([P, NT, E]), ALU.add))
                    link(dve.tensor_scalar(K3, K3, float(CAPACITY) + 0.5, None, ALU.is_lt))
                    link(dve.tensor_tensor(carry[:, :], carry[:, :], bank[7][:, 2 * E:3 * E], ALU.add))
                    link(dve.tensor_tensor(K3, K3, M3, ALU.mult))
                    dve.tensor_tensor(gates[:, :, :], gates[:, :, :], K3, ALU.mult).then_inc(done["gates_ready"], 1)
                    dve.wait_ge(done["gates_ready"], 3)
                    for e in range(E):
                        dve.wait_ge(done["l3f_o"], e + 1)
                        if some(e):
                            dve.wait_ge(done["l3f_oadd"], e)
                        for t in range(NT):
                            ins = dve.scalar_tensor_tensor(x1[:, t, :], bank[4 + e % 2][:, t * P:(t + 1) * P], gates[:, t, e:e + 1],
                                                           x1[:, t, :], ALU.mult, ALU.add)
                        ins.then_inc(done["l3f_oadd"], 1)
                    dve.wait_ge(done["l3f_oadd"], E)
                    dve.wait_ge(done["projected"], 5)
                    link(dve.tensor_tensor(x1[:, :, :], x1[:, :, :], bank[0][:, 0:S].rearrange("p (t d) -> p t d", t=NT), ALU.add))
                    add_to_x(x1[:, :, :], 7)
                dve.sem_inc(done["x_final"], 1)
                end_of_batch(dve)


SETUP_DVE = 15


def kernel(**inputs):
    import numpy as _np
    import concourse.bacc as _bacc
    from concourse import mybir as _mybir
    from concourse.bass_utils import run_bass_kernel_spmd as _run

    f32 = _np.float32
    I = {k: _np.asarray(v) for k, v in inputs.items()}

    def spread(cols, dh):
        rows, n = cols.shape
        out = _np.zeros((rows, n // dh, 32), f32)
        out[:, :, :dh] = cols.reshape(rows, n // dh, dh)
        return out.reshape(rows, -1)

    def spread_bias(vec, dh, one):
        out = _np.zeros((vec.size // dh, 32), f32)
        out[:, :dh] = vec.reshape(-1, dh)
        out[:, dh] = one
        return _np.ascontiguousarray(out.reshape(-1, 128).T)

    def rows(vec):
        return _np.broadcast_to(vec.reshape(1, -1), (128, vec.size))

    def experts_to_cols(a):
        return a.transpose(1, 0, 2).reshape(a.shape[1], -1)

    gate = _np.concatenate([I["L0_xattn_ig_kernel"].reshape(3, 128, 4), I["L0_xattn_fg_kernel"].reshape(3, 128, 4)], axis=2)
    gains = _np.stack([I["g_xattn"], I["g_ffn"]], axis=1).reshape(-1)
    qkv = I["L3_ffn_Wqkv"].reshape(128, 16, 24)
    swap = [4, 5, 6, 7, 0, 1, 2, 3]
    q, k, v = (qkv[:, :, a:a + 8] for a in (0, 8, 16))
    vb_cols = _np.zeros((128, 8, 8), f32)
    for e in range(8):
        vb_cols[:, e, e] = I["L1_ffn_vb"][e]
    W = {
        "l0_gate": experts_to_cols(gate), "l0_bias": _np.stack([I["L0_xattn_ig_bias"], I["L0_xattn_fg_bias"]], axis=1),
        "l0_outnorm": rows(I["L0_xattn_outnorm_weight"]), "gains": rows(gains),
        "l0_wq": I["L0_ffn_Wq"].transpose(2, 0, 1).reshape(128, -1), "l0_wk": I["L0_ffn_Wk"].transpose(2, 0, 1).reshape(128, -1),
        "l0_wv": I["L0_ffn_Wv"].transpose(2, 0, 1).reshape(128, -1),
        "l0_wsd": _np.concatenate([I["L0_ffn_Ws"].transpose(2, 0, 1).reshape(128, -1),
                                   I["L0_ffn_Wd"].transpose(2, 0, 1).reshape(128, -1)], axis=1),
        "l0_wo": I["L0_ffn_Wo"].transpose(0, 2, 1).reshape(4, 128, 128).transpose(1, 0, 2).reshape(128, -1),
        "l1_wq": spread(I["L1_xattn_wq_k"], 8), "l1_wk": spread(I["L1_xattn_wk_k"], 8), "l1_wv": I["L1_xattn_wv_k"],
        "l1_qb": spread_bias(I["L1_xattn_wq_b"], 8, 0.0), "l1_kb": spread_bias(I["L1_xattn_wk_b"], 8, 1.0),
        "l1_vb": rows(I["L1_xattn_wv_b"]), "l1_wo": I["L1_xattn_wo_k"], "l1_bo": rows(I["L1_xattn_wo_b"]),
        "l1f_rw1": I["L1_ffn_rW1"].T, "l1f_rb1": rows(I["L1_ffn_rb1"]), "l1f_lng": rows(I["L1_ffn_ln_g"]),
        "l1f_lnb": rows(I["L1_ffn_ln_b"]), "l1f_rw2": I["L1_ffn_rW2"].T, "l1f_rb2": rows(I["L1_ffn_rb2"]),
        "l1f_ow": experts_to_cols(I["L1_ffn_oW"].transpose(0, 2, 1)), "l1f_vb": vb_cols.reshape(128, 64), "l1f_ob": I["L1_ffn_ob"],
        "l2_wq": spread(I["L2_xattn_Wq"].T, 16), "l2_wk": spread(I["L2_xattn_Wk"].T, 16), "l2_wv": I["L2_xattn_Wv"].T,
        "l2f_router": I["L2_ffn_router_w"], "l2f_win": experts_to_cols(I["L2_ffn_w_in"]), "l2f_bin": I["L2_ffn_b_in"].T,
        "l2f_wout": experts_to_cols(I["L2_ffn_w_out"]), "l2f_bout": I["L2_ffn_b_out"],
        "l3_wk": I["L3_xattn_Wk"].T, "l3_wv": I["L3_xattn_Wv"].T, "l3_wq": I["L3_xattn_Wq"].T, "l3_wo": I["L3_xattn_Wo"].T,
        "l3_bq": I["L3_xattn_bq"].reshape(128, 1), "l3_bv": rows(I["L3_xattn_bv"]), "l3_bo": rows(I["L3_xattn_bo"]),
        "l3f_ln": _np.stack([I["L3_ffn_ln1_g"], I["L3_ffn_ln1_b"], I["L3_ffn_ln2_g"], I["L3_ffn_ln2_b"]], axis=1),
        "l3f_wq": spread(q.reshape(128, -1), 8), "l3f_wqs": spread(q[:, :, swap].reshape(128, -1), 8),
        "l3f_wk": spread(k.reshape(128, -1), 8), "l3f_wks": spread(k[:, :, swap].reshape(128, -1), 8),
        "l3f_wv": v.reshape(128, -1), "l3f_wproj": I["L3_ffn_Wproj"], "l3f_wgate": I["L3_ffn_Wgate"],
        "l3f_w1": experts_to_cols(I["L3_ffn_W1"]), "l3f_b1": I["L3_ffn_b1"].reshape(32, 128).T,
        "l3f_w2": experts_to_cols(I["L3_ffn_W2"].reshape(32, 128, 128)), "l3f_b2": I["L3_ffn_b2"],
    }
    at, n = columns(WEIGHTS)
    weights = _np.zeros((128, n), f32)
    for name, (a, width) in at.items():
        weights[:W[name].shape[0], a:a + width] = W[name]

    idx = _np.arange(128)
    ang = _np.arange(256, dtype=f32)[:, None] * (1.0 / 10000.0 ** (_np.arange(0, 8, 2, dtype=f32) / f32(8))).astype(f32)
    cos, sin = _np.zeros((4, 32, 256), f32), _np.zeros((4, 32, 256), f32)
    cos[:, 0:8] = _np.concatenate([_np.cos(ang), _np.cos(ang)], axis=1).T
    sin[:, 0:8] = _np.concatenate([-_np.sin(ang), _np.sin(ang)], axis=1).T
    later = _np.arange(256)
    neg = _np.where(later[:, None] >= later[None, :], 0.0, -1.0e9 * 8 ** 0.5).astype(f32)
    sel4 = _np.zeros((128, 4, 128), f32)
    for h in range(4):
        sel4[h, h] = 1.0
    ones_row = {8: _np.zeros((128, 1), f32), 16: _np.zeros((128, 1), f32)}
    for d, a in ones_row.items():
        a[d::32] = 1.0
    kones_stack = _np.zeros((128, 1), f32)
    kones_stack[[48, 112]] = 1.0
    import ml_dtypes
    sel = _np.zeros((128, 8, 2, 3, 128), ml_dtypes.bfloat16)
    for a, order in enumerate(((0, 0, 1, 0, 1, 2), (0, 1, 0, 2, 1, 0))):
        for tile in range(8):
            for half in range(2):
                for u, part in enumerate(order):
                    for i in range(8):
                        sel[8 * (2 * tile + half) + i, tile, a, part, 64 * half + 8 * u + i] = 1.0
    den8 = _np.zeros((128, 32), f32)
    den8[:, 8] = 1.0
    C = {
        "ident": _np.eye(128, dtype=f32), "ones": _np.ones((128, 128), f32), "upto": (idx[:, None] <= idx[None, :]).astype(f32),
        "rank": _np.broadcast_to(_np.arange(8, 0, -1, dtype=f32), (128, 8)), "sel4": sel4.reshape(128, -1),
        "cos": cos.reshape(128, 256), "sin": sin.reshape(128, 256), "kones8": ones_row[8], "kones16": ones_row[16], "kones_stack": kones_stack,
        "zero": _np.zeros((128, 1), f32), "den8": den8,
    }
    causal = _np.concatenate([neg.reshape(2, 128, 256).transpose(1, 0, 2).reshape(128, -1),
                              neg.T.reshape(2, 128, 256).transpose(1, 0, 2).reshape(128, -1)], axis=1)
    at, n = columns(CONSTS)
    consts = _np.zeros((128, n), f32)
    for name, (a, width) in at.items():
        consts[:, a:a + width] = C[name]

    experts = _np.stack([_np.concatenate([
        I["L1_ffn_qW"][e].T, I["L1_ffn_kW"][e].T, I["L1_ffn_vW"][e].T,
        I["L1_ffn_qb"][e][:, None], I["L1_ffn_kb"][e][:, None]], axis=1) for e in range(8)])

    mask = I["mask_BxSxS2_ik1"]
    arrays = {
        "x": I["x"], "ctx": I["ctx_1024"], "group_prob_T": I["fside_BxSxS2_0"].transpose(0, 2, 1),
        "mask": mask, "mask_T": mask.transpose(0, 2, 1), "weights": weights, "consts": consts, "causal": causal, "sel": sel, "experts": experts,
    }
    nc = _bacc.Bacc("TRN2", target_bir_lowering=False, num_devices=1)
    args = []
    for name in arrays:
        arrays[name] = a = _np.ascontiguousarray(arrays[name])
        args.append(nc.dram_tensor(name, a.shape, _mybir.dt.from_np(a.dtype), kind="ExternalInput").ap())
    args.append(nc.dram_tensor("out", (8, 256, 128), _mybir.dt.float32, kind="ExternalOutput").ap())
    program(nc, *args)
    r = _run(nc, [arrays], core_ids=[0])
    return r.results[0]["out"]
```

```python
import math
from contextlib import ExitStack

import concourse.bass as bass
import numpy as np
from concourse import mybir
from concourse.alu_op_type import AluOpType as ALU

FP32, BF16, I32 = mybir.dt.float32, mybir.dt.bfloat16, mybir.dt.int32
ACT = mybir.ActivationFunctionType
X_AXIS = mybir.AxisListType.X

B, S, D, P = 8, 256, 128, 128
NT = S // P
E = 8
CAPACITY = int(math.ceil(2.0 * B * S / E))
BIG = 1.0e30
NEG_MASK = -1.0e9

WEIGHTS = [
    ("l1f_ow", 1024), ("l1f_vb", 64), ("l1f_ob", 128),
    ("l0_gate", 24), ("l0_bias", 2), ("l0_outnorm", 128), ("gains", 8),
    ("l0_wq", 1024), ("l0_wk", 1024), ("l0_wv", 512), ("l0_wsd", 256), ("l0_wo", 512),
    ("l1_wq", 128), ("l1_wk", 128), ("l1_wv", 128), ("l1_qb", 1), ("l1_kb", 1), ("l1_vb", 128),
    ("l1_wo", 128), ("l1_bo", 128),
    ("l1f_rw1", 64), ("l1f_rb1", 64), ("l1f_lng", 64), ("l1f_lnb", 64), ("l1f_rw2", 8), ("l1f_rb2", 8),
    ("l2_wq", 256), ("l2_wk", 256), ("l2_wv", 128),
    ("l2f_router", 8), ("l2f_win", 1024), ("l2f_bin", 8), ("l2f_wout", 1024), ("l2f_bout", 128),
    ("l3_wk", 128), ("l3_wv", 128), ("l3_wq", 128), ("l3_wo", 128), ("l3_bq", 1), ("l3_bv", 128), ("l3_bo", 128),
    ("l3f_ln", 4), ("l3f_wq", 128), ("l3f_wqs", 128), ("l3f_wk", 128), ("l3f_wks", 128), ("l3f_wv", 128),
    ("l3f_wproj", 128), ("l3f_wgate", 8), ("l3f_w1", 4096), ("l3f_b1", 32), ("l3f_w2", 4096), ("l3f_b2", 128),
]
WEIGHTS.append(("padding", -sum(n for _, n in WEIGHTS) % 64))
CONSTS = [
    ("ident", 128), ("ones", 128), ("upto", 128), ("rank", 8), ("sel4", 512), ("cos", 256), ("sin", 256),
    ("kones16", 1), ("kones_stack", 1), ("den", 32),
]
EXPERT_COLS = 3 * 128 + 2


def columns(layout):
    at, out = 0, {}
    for name, width in layout:
        out[name] = (at, width)
        at += width
    return out, at


class Attention:

    def __init__(self, heads, dh, rows, per, scale, heads_before, groups_before, norms_before, score_banks=3):
        self.heads, self.dh, self.rows, self.per, self.scale = heads, dh, rows, per, scale
        self.groups = heads // per
        self.score_banks = score_banks
        self.hb, self.gb, self.nb = heads_before, groups_before, norms_before
        self.chunk = min(4, self.groups)
        self.chunks = self.groups // self.chunk
        self.turns = {}
        for c in range(self.chunks):
            last = (c + 1) * self.chunk * per - 1
            for t in range(NT):
                self.turns[last + per + 3 + t] = (c, t)
        self.steps = max(self.turns) + 1

    def turns_before(self, step):
        return sum(1 for s in self.turns if s < step)

    def adds_before(self, step):
        return sum(1 for i in range(step) if i % self.per == 0 and self.per <= i <= self.heads)


class Stream:

    def __init__(self, first, qk, v, wo, qk_bias=None, v_bias=None, masks=None, gated=False, experts=False, turned=False):
        self.first, self.qk, self.v, self.wo, self.qk_bias, self.v_bias = first, qk, v, wo, qk_bias, v_bias
        self.masks, self.gated, self.experts, self.turned = masks, gated, experts, turned


def program(nc, x_in, ctx_in, gp_in, mask_in, maskT_in, weights_in, consts_in, causal_in, sel_in, experts_in, out):
    WC, n_weights = columns(WEIGHTS)
    n_first = WC["l1_wq"][0]
    CC, n_consts = columns(CONSTS)
    scope = ExitStack()
    with scope:
        def sb(name, shape, dt=FP32):
            return scope.enter_context(nc.sbuf_tensor(name, shape, dt))

        W = sb("W", [P, n_weights])
        C = sb("C", [P, n_consts])

        def w(name, rows=P):
            a, n = WC[name]
            return W[0:rows, a:a + n]

        def c(name, rows=P):
            a, n = CC[name]
            return C[0:rows, a:a + n]

        ident = c("ident")
        ident_bf = sb("ident_bf", [P, P], BF16)
        causS = sb("causS", [P, NT, S], BF16)
        causT = sb("causT", [P, NT, S], BF16)
        tanh_gain = sb("tanh_gain", [P, 8])
        minus_half = sb("minus_half", [P, 16])
        out_bias1 = sb("out_bias1", [E, D])
        expert = sb("expert", [P, EXPERT_COLS])
        sel = sb("sel_sb", [P, 8, 2, 3, P], BF16)
        kone = sb("kone", [P, 2])

        xn = sb("xn", [P, NT, D])
        xs = sb("xs", [P, NT, D])
        ctxs = sb("ctxs", [P, NT, D])
        ctxT = sb("ctxT", [P, S])
        y = sb("y", [P, NT, D])
        yT = sb("yT", [P, S])
        bn = sb("bn", [P, NT, 6])
        mv = sb("mv", [P, NT, 2])
        rstd = sb("rstd", [P, NT])
        tmp = sb("tmp", [P, NT, D])
        acc = sb("acc", [P, NT, D])

        mix = sb("mix", [P, 4096])
        qk = sb("qk", [P, 8, S])
        qS, kS = qk[:, 0:4, :], qk[:, 4:8, :]
        qk64 = qk[:, :, :].rearrange("p (h a) s -> p h (a s)", a=2)
        qk_bf = sb("qk_bf", [P, 8, S], BF16)
        qk64_bf = qk_bf[:, :, :].rearrange("p (h a) s -> p h (a s)", a=2)
        negmax = {16: sb("negmax16", [P, 2, NT, P]), 64: sb("negmax64", [P, 4, NT, P])}
        F = mix[:, 0:512].rearrange("p (a s) -> p a s", a=2)
        rest = mix[:, 512:1024].rearrange("p (a s) -> p a s", a=2)
        stack = mix[:, 1024:3072].bitcast(BF16).rearrange("p (t a s) -> p t a s", t=8, a=2)
        parts = mix[:, 3072:3840].bitcast(BF16).rearrange("p (c a s) -> p c a s", c=3, a=2)
        Vn = mix[:, 3840:4096].rearrange("p (t h d) -> p t h d", t=NT, d=8)
        negmax_bf = sb("negmax_bf", [P, 2, NT, P], BF16)
        V8 = sb("V8", [P, NT, 16, 32])
        V16 = sb("V16", [P, NT, 8, 32])
        V64s = sb("V64s", [P, NT * 16 * 65])
        V64 = V64s[:, :].rearrange("p (t h d) -> p t h d", t=NT, h=16)
        negS = V64s[:, 1024:1280].bitcast(BF16).rearrange("p (t s) -> p t s", t=NT)
        negT = V64s[:, 1280:1536].bitcast(BF16).rearrange("p (t s) -> p t s", t=NT)
        gpT = V64s[:, 1536:2048].rearrange("p (t s) -> p t s", t=NT)
        PTG = sb("PTG", [P, 6, 2 * S])
        PX = PTG[:, 0:4, :]
        PT, PG = PTG[:, 0:3, :], PTG[:, 3:6, :]
        OT = sb("OT", [P, 8, S])
        on = sb("on", [P, NT, 1024])
        onT = sb("onT", [P, S])
        rden = sb("rden", [P, 16])

        l0r = PTG[0:4, :, :].rearrange("p a (b s) -> p (a b) s", b=2)
        gcol = sb("gcol", [P, NT, 4])
        mcol = sb("mcol", [P, NT, 4])
        mixD, mixP = mix[:, 0:2048], mix[:, 2048:4096]
        mask_i = mix[:, 0:512].bitcast(I32).rearrange("p (t s) -> p t s", t=NT)
        maskT_i = mix[:, 512:1024].bitcast(I32).rearrange("p (t s) -> p t s", t=NT)
        Dm = mix[:, 0:1536].rearrange("p (h s) -> p h s", h=4)
        Cm = mix[:, 1536:3072].rearrange("p (h s) -> p h s", h=4)
        Vm = sb("Vm", [P, NT, 4, 33])
        hh = sb("hh", [P, NT, 4, 32])
        bn8 = sb("bn8", [P, 8, 6])
        mv8 = sb("mv8", [P, 8, 2])
        rstd8 = sb("rstd8", [P, 8])
        dn = sb("dn", [P, 4, NT * 4])
        pv = sb("pv", [P, NT, 512])
        gv = sb("gv", [P, 512])
        t2 = OT[:, :, :].rearrange("p (a b) s -> p a (b s)", b=2)
        t2s = sb("t2s", [P, 2, 64])
        gsig = sb("gsig", [P, 512])
        coef = sb("coef", [P, 512])

        gates = sb("gates", [P, NT, E])
        gatesT = y[0:E, :, :].rearrange("p t d -> p (t d)")
        gs = sb("gs", [P, 4, NT])
        hT = on[:, :, :].rearrange("p t (f s) -> p t f s", f=4)
        GT = hT[:, 0, :, :]
        carry = sb("carry", [P, E])
        x1 = tmp
        pr = sb("pr", [P, 2, S])
        r1 = pr[:, 1, 0:NT * 64].rearrange("p (t d) -> p t d", t=NT)
        r1T = pr[0:64, 0, :]

        bank = [scope.enter_context(nc.psum_tensor(f"bank{i}", [P, 512], FP32)) for i in range(8)]
        MISC = bank[7]

        setup = {n: scope.enter_context(nc.semaphore(n)) for n in (
            "consts_loaded", "causal_loaded", "sel_loaded", "weights_loaded", "later_weights_loaded", "setup_dve", "setup_pool", "setup_pe", "setup_act",
            "x_loaded", "ctx_loaded", "out_stored", "engine_at_end", "cleared", "engine_resumes")}
        done = {n: scope.enter_context(nc.semaphore(n)) for n in (
            "xs_free", "x_taken", "mask_loaded", "maskT_loaded", "gp_loaded", "expert_loaded", "x_final",
            "dve_step", "dve_expert_step", "pool_step", "pool_expert_step", "act_step",
            "ln_var", "ln_rstd", "ln_y", "ln_turned", "ln_yT",
            "scored", "max_taken", "max_turned", "q_shifted", "scoredT", "exped", "group_weighted", "valued",
            "o_copied", "o_turned", "normed",
            "ctx_turned", "ctxT_ready", "projected",
            "l0_gates", "l0_absf", "l0_softplus", "l0_rows", "l0_cols_turned", "l0_negm", "l0_expm", "l0_spread", "l0_args",
            "l0_decay", "l0_decay_masked", "l0_qk", "l0_cm", "l0_h", "l0_hstat", "l0_hrstd",
            "l0f_qk", "l0f_qk_ready", "l0f_pv", "l0f_gates", "l0f_gcopied", "l0f_sig", "l0f_pvcopied", "l0f_coef", "l0f_ocoef", "l0f_vdve",
            "l0f_vpool", "l0f_gdve", "l0f_gpool", "l0f_gturned", "l0f_gT",
            "filled", "neg_ready",
            "l1f_r1", "l1f_rvar", "l1f_rrstd", "l1f_r1n", "l1f_r1turned", "l1f_r1T", "router_logits", "router_shifted", "router_exped", "gates_ready", "gates_turned", "gatesT_ready", "l1f_bias",
            "ex_qk_projected", "ex_F_ready", "ex_split", "ex_spread", "ex_stacked_act", "ex_stacked_dve", "ex_v_projected",
            "ex_v_ready", "ex_v_placed", "ex_scored", "ex_max_taken", "ex_max_turned", "ex_shifted", "ex_scoredT", "ex_exped",
            "ex_valued", "ex_o_copied", "ex_o_turned", "ex_normed", "ex_on_turned", "ex_onT_ready", "ex_projected", "ex_added",
            "l2_q", "l2_kv", "l2_q_ready", "l2_kv_ready",
            "l2f_h", "l2f_gelu", "l2f_o", "l2f_oadd",
            "l3_qkv", "l3_qk_ready", "l3_v_ready", "l3_s", "l3_smax", "l3_exp", "l3_pturned", "l3_pT", "l3_ctx", "l3_ctx_ready", "l3_out",
            "rope_step", "rope_ready",
            "l3f_top", "l3f_count", "l3f_h", "l3f_gelu", "l3f_o",
            "l3f_oadd")}
        A0 = Attention(16, 64, 128, 1, 64 ** -0.5, 0, 0, 0, score_banks=2)
        A2 = Attention(8, 16, 32, 4, 0.25, 16, 16, 8)
        masked = Stream(0, [(w("l1_wq"), yT), (w("l1_wk"), ctxT)], (w("l1_wv"), ctxT), lambda e: w("l1_wo"),
                        qk_bias=[w("l1_qb"), w("l1_kb")], v_bias=w("l1_vb"), masks=(negS, negT), gated=True)
        experts = Stream(1, [(expert[:, 0:P], yT), (expert[:, P:2 * P], yT)], (expert[:, 256:384], yT),
                         lambda e: W[:, bass.ds(e * D + WC["l1f_ow"][0], D)],
                         qk_bias=[expert[:, 384:385], expert[:, 385:386]], experts=True)
        rotary = Stream(1 + E, [(w(name), yT) for name in ("l3f_wq", "l3f_wqs", "l3f_wk", "l3f_wks")], (w("l3f_wv"), yT),
                        lambda e: w("l3f_wproj"), masks=(causS, causT), turned=True)

        def some(n):
            return not isinstance(n, int) or n > 0

        block = scope.enter_context(nc.Block())

        @block.sync
        def _(sp):
            sp.dma_start(C[:, :], consts_in).then_inc(setup["consts_loaded"], 16)
            sp.dma_start(xn[:, :, :], x_in[0].rearrange("(t p) d -> p t d", p=P)).then_inc(setup["x_loaded"], 16)
            sp.dma_start(ctxs[:, :, :], ctx_in[0].rearrange("(t p) d -> p t d", p=P)).then_inc(setup["ctx_loaded"], 16)
            sp.dma_start(mixD[:, 0:1024], causal_in).then_inc(setup["causal_loaded"], 16)
            sp.dma_start(sel[:, :, :, :, :], sel_in).then_inc(setup["sel_loaded"], 16)
            sp.dma_start(W[:, 0:n_first], weights_in[:, 0:n_first]).then_inc(setup["weights_loaded"], 16)
            sp.dma_start(W[:, n_first:n_weights], weights_in[:, n_first:n_weights]).then_inc(setup["later_weights_loaded"], 16)

            def tokens(ap, b):
                return ap[bass.ds(b, 1)].rearrange("a (t p) d -> p (a t) d", p=P)

            def load_tokens(b):
                sp.dma_start(xn[:, :, :], tokens(x_in, b)).then_inc(setup["x_loaded"], 16)
                sp.dma_start(ctxs[:, :, :], tokens(ctx_in, b)).then_inc(setup["ctx_loaded"], 16)

            def batch(b, last):
                sp.wait_ge(done["l0f_gturned"], 2)
                sp.dma_start(gpT, tokens(gp_in, b)).then_inc(done["gp_loaded"], 16)
                sp.dma_start(mask_i, tokens(mask_in, b)).then_inc(done["mask_loaded"], 16)
                sp.dma_start(maskT_i, tokens(maskT_in, b)).then_inc(done["maskT_loaded"], 16)
                sp.dma_start(expert[:, :], experts_in[0]).then_inc(done["expert_loaded"], 16)
                if not last:
                    sp.wait_ge(done["ln_turned"], 2)
                    sp.wait_ge(done["x_taken"], 1)
                    load_tokens(b + 1)
                with sp.Fori(1, E) as e:
                    sp.wait_ge(done["ex_v_projected"], e + 1)
                    sp.wait_ge(done["ex_F_ready"], e + 1)
                    sp.dma_start(expert[:, :], experts_in[bass.ds(e, 1)].rearrange("a p n -> (a p) n"))\
                        .then_inc(done["expert_loaded"], 16)
                sp.wait_ge(done["x_final"], 1)
                sp.dma_start(tokens(out, b), xs[:, :, :]).then_inc(setup["out_stored"], 16)
                for n in ("mask_loaded", "maskT_loaded", "gp_loaded"):
                    sp.wait_ge(done[n], 16)
                sp.wait_ge(done["expert_loaded"], 16 * E)
                sp.wait_ge(setup["engine_at_end"], 4)
                for s in done.values():
                    sp.sem_clear(s)
                sp.sem_clear(setup["engine_at_end"])
                sp.sem_inc(setup["cleared"], 1)
                sp.wait_ge(setup["engine_resumes"], 4)
                sp.sem_clear(setup["cleared"])
                sp.sem_clear(setup["engine_resumes"])
                sp.wait_ge(setup["out_stored"], 16)
                sp.sem_clear(setup["out_stored"])
                sp.sem_inc(done["xs_free"], 1)

            sp.sem_inc(done["xs_free"], 1)
            with sp.Fori(0, B - 1) as b:
                batch(b, False)
            batch(B - 1, True)

        def end_of_batch(eng):
            eng.sem_inc(setup["engine_at_end"], 1)
            eng.wait_ge(setup["cleared"], 1)
            eng.sem_inc(setup["engine_resumes"], 1)

        def q_rows(A, h, n, source=None):
            T = qk if source is None else source
            if A.rows == 128:
                return T[0:n, h % 4 * 2, :]
            j = 32 * (h % 4)
            return T[j:j + n, h // 4, :]

        def k_rows(A, h, n, source=None):
            T = qk if source is None else source
            if A.rows == 128:
                return T[0:n, h % 4 * 2 + 1, :]
            j = 32 * (h % 4)
            return T[j:j + n, 4 + h // 4, :]

        def pe_attention(pe, A, V, before=None):
            per, dh = A.per, A.dh
            for i in range(A.steps):
                if before is not None:
                    before(i)
                if i < A.heads:
                    if some(A.hb + i - A.score_banks + 1):
                        pe.wait_ge(done["max_taken"], A.hb + i - A.score_banks + 1)
                    for t in range(NT):
                        mm = pe.matmul(bank[i % A.score_banks][:, t * S:(t + 1) * S], q_rows(A, i, dh, qk_bf)[:, t * P:(t + 1) * P],
                                       k_rows(A, i, dh, qk_bf), start=True, stop=True)
                    mm.then_inc(done["scored"], 1)
                if i % per == 0 and per <= i <= A.heads:
                    g = i // per - 1
                    pe.wait_ge(done["max_taken"], A.hb + (g + 1) * per)
                    if some(A.gb + g):
                        pe.wait_ge(done["q_shifted"], A.gb + g)
                    if some(A.nb + A.turns_before(i)):
                        pe.wait_ge(done["normed"], A.nb + A.turns_before(i))
                    M = negmax[dh][:, g % 4, :, :]
                    rows = A.rows if A.rows == 128 else 128
                    for t in range(NT):
                        mm = pe.transpose(MISC[0:rows, t * P:(t + 1) * P], M[:, t, :], ident)
                    mm.then_inc(done["max_turned"], 1)
                h = i - per - 1
                if 0 <= h < A.heads:
                    pe.wait_ge(done["q_shifted"], A.gb + h // per + 1)
                    if some(A.hb + h - 1):
                        pe.wait_ge(done["exped"], A.hb + h - 1)
                    for t in range(NT):
                        mm = pe.matmul(bank[3 + h % 2][:, t * S:(t + 1) * S], k_rows(A, h, dh + 1)[:, t * P:(t + 1) * P],
                                       q_rows(A, h, dh + 1), start=True, stop=True)
                    mm.then_inc(done["scoredT"], 1)
                h = i - per - 2
                if 0 <= h < A.heads:
                    g, j = h // per, h % per
                    if j == 0:
                        if some(A.gb + g - 1):
                            pe.wait_ge(done["o_copied"], A.gb + g - 1)
                    pe.wait_ge(done["exped"], A.hb + h + 1)
                    if A.rows == 128:
                        o = bank[5 + g % 2][0:dh + 1, 0:S]
                    else:
                        o = bank[5 + g % 2][32 * j:32 * j + 32, 0:S]
                    for t in range(NT):
                        mm = pe.matmul(o, V[:, t, h, :], PT[:, h % 3, t * S:(t + 1) * S], start=t == 0, stop=t == NT - 1)
                    mm.then_inc(done["valued"], 1)
                if i in A.turns:
                    ch, t = A.turns[i]
                    pe.wait_ge(done["o_copied"], A.gb + (ch + 1) * A.chunk)
                    if some(A.nb + A.turns_before(i)):
                        pe.wait_ge(done["normed"], A.nb + A.turns_before(i))
                    pe.wait_ge(done["q_shifted"], A.gb + A.adds_before(i + 1))
                    n = dh + 1 if A.rows == 128 else 128
                    for s in range(A.chunk):
                        g = ch * A.chunk + s
                        mm = pe.transpose(MISC[:, s * 128:s * 128 + n], OT[0:n, g % 8, t * P:(t + 1) * P], ident[0:n, 0:n])
                    mm.then_inc(done["o_turned"], 1)

        def act_attention(act, A, before=None):
            per = A.per

            def copy_out(g):
                act.wait_ge(done["valued"], A.hb + (g + 1) * per)
                n = A.dh + 1 if A.rows == 128 else 128
                act.activation(OT[0:n, g % 8, :], bank[5 + g % 2][0:n, 0:S], ACT.Copy).then_inc(done["o_copied"], 1)

            for h in range(A.heads):
                if before is not None:
                    before(h)
                act.wait_ge(done["scoredT"], A.hb + h + 1)
                if some(A.hb + h - 2):
                    act.wait_ge(done["valued"], A.hb + h - 2)
                act.activation(PT[:, h % 3, :], bank[3 + h % 2][:, :], ACT.Exp, scale=A.scale).then_inc(done["exped"], 1)
                if h >= 1 and h % per == 0:
                    copy_out(h // per - 1)
            copy_out(A.groups - 1)

        def pool_weight(pool):
            for h in range(16):
                pool.wait_ge(done["ex_exped"], h + 1)
                if some(h - 2):
                    pool.wait_ge(done["ex_valued"], h - 2)
                pool.tensor_tensor(PG[:, h % 3, :], PX[:, h % 3, :], gpT.rearrange("p t s -> p (t s)"), ALU.mult)\
                    .then_inc(done["group_weighted"], 1)

        def dve_attention(dve, A, link, before=None):
            per, dh = A.per, A.dh
            for i in range(A.steps):
                if before is not None:
                    before(i)
                if i < A.heads:
                    dve.wait_ge(done["scored"], A.hb + i + 1)
                    g, j = i // per, i % per
                    dve.tensor_reduce(negmax[dh][:, g % 4, :, j * 32 + dh], bank[i % A.score_banks][:, :].rearrange("p (t s) -> p t s", t=NT),
                                      X_AXIS, ALU.max, negate=True).then_inc(done["max_taken"], 1)
                if i % per == 0 and per <= i <= A.heads:
                    g = i // per - 1
                    dve.wait_ge(done["max_turned"], A.gb + g + 1)
                    if A.rows == 128:
                        dve.tensor_copy(qk64[dh:dh + 1, g % 4, 0:S], MISC[dh:dh + 1, 0:S]).then_inc(done["q_shifted"], 1)
                    else:
                        dve.tensor_tensor(qS[:, g, :], qS[:, g, :], MISC[:, 0:S], ALU.add).then_inc(done["q_shifted"], 1)
                if i in A.turns:
                    ch, t = A.turns[i]
                    dve.wait_ge(done["o_turned"], A.nb + A.turns_before(i) + 1)
                    n = A.chunk * per
                    T = MISC[:, 0:A.chunk * 128].rearrange("p (h c) -> p h c", c=A.rows)
                    r = rden[:, 0:n].unsqueeze(2)
                    link(dve.reciprocal(r, T[:, :, dh:dh + 1]))
                    o = on[:, t, ch * n * dh:(ch + 1) * n * dh].rearrange("p (h d) -> p h d", d=dh)
                    dve.tensor_tensor(o, T[:, :, 0:dh], r.broadcast_to([P, n, dh]), ALU.mult).then_inc(done["normed"], 1)

        SPREAD_AT = {1: 2, 2: 3, 4: 4, 5: 5, 7: 6, 8: 7}
        SPREAD_NEXT_AT = {13: 0, 15: 1}
        KQ = 48

        def body_pe(pe, A, e, prev, own, nxt, steps=range(16)):
            n = e + A.first

            def spread(tile):
                for a in range(2):
                    for part in range(3):
                        mm = pe.matmul(bank[2][:, a * S:(a + 1) * S], sel[:, tile, a, part, :], parts[:, part, a, :],
                                       start=part == 0, stop=part == 2)
                mm.then_inc(done["ex_spread"], 1)

            for i in steps:
                if own:
                    tile, row = i // 2, 64 * (i % 2)
                    if i % 4 == 0:
                        pe.wait_ge(done["ex_stacked_act"], n * 4 + i // 4 + 1)
                    elif i % 2 == 0:
                        pe.wait_ge(done["ex_stacked_dve"], n * 4 + i // 4 + 1)
                    if some(n * 16 + i - 1):
                        pe.wait_ge(done["ex_max_taken"], n * 16 + i - 1)
                    for t in range(NT):
                        keys = (t + 1) * P if A.turned else S
                        o = bank[i % 2][:, t * S:t * S + keys]
                        mm = pe.matmul(o, stack[row:row + KQ, tile, 0, t * P:(t + 1) * P],
                                       stack[row:row + KQ, tile, 1, 0:keys], start=True, stop=A.masks is None)
                        if A.masks is not None:
                            mm = pe.matmul(o, ident_bf[:, :], A.masks[0][:, t, 0:keys], start=False, stop=True)
                    mm.then_inc(done["ex_scored"], 1)
                if prev and i in (5, 7, 9, 11):
                    pe.wait_ge(done["ex_shifted"], n * 8 + (i // 2 if own else 0))
                    if i in (5, 7):
                        t = (i - 5) // 2
                        pe.wait_ge(done["ex_o_copied"], n * 4)
                        if i == 7:
                            pe.wait_ge(done["ex_normed"], n * 2 - 1)
                        for g in range(4):
                            mm = pe.transpose(MISC[:, g * P:(g + 1) * P], OT[:, g, t * P:(t + 1) * P], ident)
                        mm.then_inc(done["ex_o_turned"], 1)
                    if i == 9:
                        pe.wait_ge(done["ex_normed"], n * 2)
                        for t in range(NT):
                            mm = pe.transpose(MISC[:, t * P:(t + 1) * P], on[:, t, 0:D], ident)
                        mm.then_inc(done["ex_on_turned"], 1)
                    if i == 11:
                        pe.wait_ge(done["ex_onT_ready"], n)
                        for t in range(NT):
                            mm = pe.matmul(MISC[:, t * P:(t + 1) * P], onT[:, t * P:(t + 1) * P],
                                           A.wo(e - 1), start=True, stop=True)
                        mm.then_inc(done["ex_projected"], 1)
                if own and i in SPREAD_AT:
                    tile = SPREAD_AT[i]
                    if tile == 6 and nxt:
                        pe.wait_ge(done["ex_F_ready"], n + 2)
                    elif tile % 2 == 0:
                        pe.wait_ge(done["ex_stacked_dve"], n * 4 + tile // 2)
                    else:
                        pe.wait_ge(done["ex_stacked_act"], n * 4 + tile // 2 + 1)
                    spread(tile)
                if nxt and i == 6:
                    if A.experts:
                        pe.wait_ge(done["expert_loaded"], e * 16 + 32)
                    if own:
                        pe.wait_ge(done["ex_stacked_dve"], n * 4 + 3)
                    for a, (weight, data) in enumerate(A.qk):
                        mm = pe.matmul(bank[2 + a // 2][:, (a % 2) * S:(a % 2 + 1) * S], weight, data[:, :], start=True, stop=True)
                    mm.then_inc(done["ex_qk_projected"], 1)
                if nxt and i in SPREAD_NEXT_AT:
                    tile = SPREAD_NEXT_AT[i]
                    pe.wait_ge(done["ex_split"], n + 2)
                    if tile == 0:
                        if own:
                            pe.wait_ge(done["ex_stacked_dve"], n * 4 + 4)
                        else:
                            pe.wait_ge(done["ex_F_ready"], n + 2)
                    else:
                        pe.wait_ge(done["ex_v_ready"], n + 2)
                    spread(tile)
                if nxt and i == 14:
                    pe.wait_ge(done["ex_stacked_act"], n * 4 + 5)
                    for t in range(NT):
                        mm = pe.matmul(bank[2][:, t * D:(t + 1) * D], A.v[1][:, t * P:(t + 1) * P], A.v[0], start=True, stop=True)
                    mm.then_inc(done["ex_v_projected"], 1)
                if i % 2 == 0 and (own if i >= 2 else prev):
                    pe.wait_ge(done["ex_max_taken"], n * 16 + i)
                    if some(n * 8 + i // 2 - 1):
                        pe.wait_ge(done["ex_shifted"], n * 8 + i // 2 - 1)
                    if prev and i in (6, 8):
                        pe.wait_ge(done["ex_normed"], n * 2 + (i - 6) // 2 - 1)
                    if prev and i == 10:
                        pe.wait_ge(done["ex_onT_ready"], n)
                    if prev and i == 12:
                        pe.wait_ge(done["ex_added"], n + 1)
                    for t in range(NT):
                        mm = pe.transpose(MISC[:, :].bitcast(BF16)[:, t * P:(t + 1) * P],
                                          negmax_bf[:, (i // 2 - 1) % 2, t, :], ident_bf[:, :])
                    mm.then_inc(done["ex_max_turned"], 1)
                if own if i >= 3 else prev:
                    h = (i - 3) % 16
                    tile, row = h // 2, 64 * (h % 2)
                    pe.wait_ge(done["ex_shifted"], n * 8 + (i - 3) // 2 + 1)
                    if some(n * 16 + i - 4):
                        pe.wait_ge(done["ex_exped"], n * 16 + i - 4)
                    for t in range(NT):
                        first = t * P if A.turned else 0
                        o = bank[3 + h % 2][:, t * S:(t + 1) * S - first]
                        mm = pe.matmul(o, stack[row:row + KQ + 1, tile, 1, t * P:(t + 1) * P],
                                       stack[row:row + KQ + 1, tile, 0, first:S], start=True, stop=A.masks is None)
                        if A.masks is not None:
                            mm = pe.matmul(o, ident_bf[:, :], A.masks[1][:, t, first:S], start=False, stop=True)
                    mm.then_inc(done["ex_scoredT"], 1)
                if own if i >= 5 else prev:
                    h = (i - 5) % 16
                    g, j = h // 4, h % 4
                    if j == 0:
                        if some(n * 4 + (i - 5) // 4 - 1):
                            pe.wait_ge(done["ex_o_copied"], n * 4 + (i - 5) // 4 - 1)
                        pe.wait_ge(done["ex_v_placed"], n * 2 + (2 if g == 3 else 1) - (0 if i >= 5 else 2))
                    pe.wait_ge(done["ex_exped"], n * 16 + i - 4)
                    o = bank[5 + g % 2][32 * j:32 * j + 32, 0:S]
                    if A.gated:
                        pe.wait_ge(done["group_weighted"], h + 1)
                        for t in range(NT):
                            pe.matmul(o, V8[:, t, h, :], PG[:, h % 3, t * S:(t + 1) * S], start=t == 0, stop=False)
                        for t in range(NT):
                            mm = pe.matmul(o, c("den"), PX[:, h % 3, t * S:(t + 1) * S], start=False, stop=t == NT - 1)
                    else:
                        for t in range(NT):
                            first = t * P if A.turned else 0
                            mm = pe.matmul(o[:, first:S], V8[:, t, h, :], PX[:, h % 4, t * S:(t + 1) * S - first],
                                           start=t == 0, stop=t == NT - 1)
                    mm.then_inc(done["ex_valued"], 1)

        def body_act(act, A, e, prev, own, nxt, steps=range(16)):
            n = e + A.first

            def stack_tile(tile):
                act.activation(stack[:, tile, 0, :], bank[2][:, 0:S], ACT.Copy)
                act.activation(stack[:, tile, 1, :], bank[2][:, S:2 * S], ACT.Identity, bias=c("kones_stack"))\
                    .then_inc(done["ex_stacked_act"], 1)

            for i in steps:
                if own and i in SPREAD_AT and SPREAD_AT[i] % 2 == 0:
                    act.wait_ge(done["ex_spread"], n * 8 + SPREAD_AT[i] + 1)
                    stack_tile(SPREAD_AT[i])
                if nxt and i == 6:
                    act.wait_ge(done["ex_qk_projected"], n + 2)
                    if own:
                        act.wait_ge(done["ex_split"], n + 1)
                    for a in range(2):
                        if A.turned:
                            act.wait_ge(done["rope_ready"], a + 1)
                            ins = act.activation(F[:, a, :], rest[:, a, :], ACT.Copy)
                        else:
                            ins = act.activation(F[:, a, :], bank[2][:, a * S:(a + 1) * S], ACT.Identity, bias=A.qk_bias[a])
                    ins.then_inc(done["ex_F_ready"], 1)
                if nxt and i == 13:
                    act.wait_ge(done["ex_spread"], n * 8 + 9)
                    stack_tile(0)
                if own if i >= 3 else prev:
                    h = (i - 3) % 16
                    act.wait_ge(done["ex_scoredT"], n * 16 + i - 2)
                    slots = 3 if A.gated else 4
                    if some(n * 16 + i - 2 - slots):
                        act.wait_ge(done["ex_valued"], n * 16 + i - 2 - slots)
                    cols = 2 * S - P if A.turned else 2 * S
                    act.activation(PX[:, h % slots, 0:cols], bank[3 + h % 2][:, 0:cols], ACT.Exp, scale=8 ** -0.5).then_inc(done["ex_exped"], 1)
                if i % 4 == 0 and (own if i >= 8 else prev):
                    g = (i - 8) // 4 % 4
                    act.wait_ge(done["ex_valued"], n * 16 + i - 4)
                    if g == 0 and some(n * 2 - 2) and prev:
                        act.wait_ge(done["ex_o_turned"], n * 2)
                    act.activation(OT[:, g, :], bank[5 + g % 2][:, 0:S], ACT.Copy).then_inc(done["ex_o_copied"], 1)
                if prev and i == 9:
                    act.wait_ge(done["ex_on_turned"], n)
                    act.activation(onT[:, :], MISC[:, 0:S], ACT.Copy).then_inc(done["ex_onT_ready"], 1)

        def body_dve(dve, A, e, prev, own, nxt, steps=range(16)):
            n = e + A.first

            n_linked = [0]

            def link(ins, by=1):
                n_linked[0] += by
                ins.then_inc(done["dve_expert_step"], by)
                dve.wait_ge(done["dve_expert_step"], n * 4 + n_linked[0] - 4)

            for i in steps:
                if own:
                    dve.wait_ge(done["ex_scored"], n * 16 + i + 1)
                    if i % 2 == 0 and some(n * 8 + i // 2 - 1):
                        dve.wait_ge(done["ex_max_turned"], n * 8 + i // 2 - 1)
                    M = negmax_bf[:, (i // 2) % 2, :, (i % 2) * 64 + KQ]
                    if A.turned:
                        for t in range(NT):
                            ins = dve.tensor_reduce(M[:, t:t + 1], bank[i % 2][:, t * S:t * S + (t + 1) * P], X_AXIS, ALU.max, negate=True)
                    else:
                        ins = dve.tensor_reduce(M, bank[i % 2][:, :].rearrange("p (t s) -> p t s", t=NT), X_AXIS, ALU.max, negate=True)
                    ins.then_inc(done["ex_max_taken"], 1)
                if i % 2 == 0 and (own if i >= 2 else prev):
                    tile = (i // 2 - 1) % 8
                    dve.wait_ge(done["ex_max_turned"], n * 8 + i // 2)
                    dve.tensor_tensor(stack[:, tile, 0, :], stack[:, tile, 0, :], MISC[:, :].bitcast(BF16)[:, 0:S], ALU.add)\
                        .then_inc(done["ex_shifted"], 1)
                if prev and i in (5, 7):
                    t = (i - 5) // 2
                    dve.wait_ge(done["ex_o_turned"], n * 2 + t - 1)
                    T = MISC[:, :].rearrange("p (h c) -> p h c", c=32)
                    r = rden[:, 0:16].unsqueeze(2)
                    den = 16 if A.gated else 8
                    link(dve.reciprocal(r, T[:, :, den:den + 1]), by=1 if A.experts else 2)
                    if A.experts:
                        link(dve.tensor_scalar(rden[:, 0:16], rden[:, 0:16], gates[:, t, bass.ds(e - 1, 1)], None, ALU.mult))
                    dve.tensor_tensor(on[:, t, 0:D].rearrange("p (h d) -> p h d", d=8), T[:, :, 0:8], r.broadcast_to([P, 16, 8]), ALU.mult)\
                        .then_inc(done["ex_normed"], 1)
                if prev and i == 11:
                    dve.wait_ge(done["ex_projected"], n)
                    dve.wait_ge(done["ex_added"], n)
                    dve.tensor_tensor(acc[:, :, :], acc[:, :, :], MISC[:, 0:S].rearrange("p (t d) -> p t d", t=NT), ALU.add)\
                        .then_inc(done["ex_added"], 1)
                if own and i in SPREAD_AT and SPREAD_AT[i] % 2 == 1:
                    tile = SPREAD_AT[i]
                    dve.wait_ge(done["ex_spread"], n * 8 + tile + 1)
                    dve.tensor_tensor(stack[:, tile, :, :], bank[2][:, :].rearrange("p (a s) -> p a s", a=2), kone1, ALU.add)\
                        .then_inc(done["ex_stacked_dve"], 1)
                if nxt and i == 6 and A.turned:
                    dve.wait_ge(done["ex_qk_projected"], n + 2)
                    for a in range(2):
                        dve.tensor_tensor(pr[:, 0, :], bank[2 + a][:, 0:S], c("cos"), ALU.mult).then_inc(done["rope_step"], 1)
                        dve.tensor_tensor(pr[:, 1, :], bank[2 + a][:, S:2 * S], c("sin"), ALU.mult).then_inc(done["rope_step"], 1)
                        dve.wait_ge(done["rope_step"], 2 * a + 2)
                        dve.tensor_tensor(rest[:, a, :], pr[:, 0, :], pr[:, 1, :], ALU.add).then_inc(done["rope_ready"], 1)
                        dve.wait_ge(done["rope_ready"], a + 1)
                if nxt and i == 14:
                    dve.wait_ge(done["ex_v_projected"], n + 2)
                    if own:
                        dve.wait_ge(done["ex_v_placed"], n * 2 + 2)
                    V = bank[2][:, 0:S].rearrange("p (t h d) -> p t h d", t=NT, d=8)
                    if A.v_bias is None:
                        dve.tensor_copy(Vn, V).then_inc(done["ex_v_ready"], 1)
                    else:
                        dve.tensor_tensor(Vn, V, A.v_bias.rearrange("p (h d) -> p h d", d=8).unsqueeze(1).broadcast_to([P, NT, 16, 8]), ALU.add)\
                            .then_inc(done["ex_v_ready"], 1)
                if nxt and i == 15:
                    dve.wait_ge(done["ex_spread"], n * 8 + 10)
                    dve.tensor_tensor(stack[:, 1, :, :], bank[2][:, :].rearrange("p (a s) -> p a s", a=2), kone1, ALU.add)\
                        .then_inc(done["ex_stacked_dve"], 1)

        kone1 = kone[:, :].unsqueeze(2).broadcast_to([P, 2, S])

        def body_pool(pool, A, e, own):
            n = e + A.first
            pool.wait_ge(done["ex_F_ready"], n + 2)
            if own:
                pool.wait_ge(done["ex_spread"], n * 8 + 8)
            base = n * 3 + 3
            one = c("ones")[:, 0:2]
            pool.tensor_tensor(parts[:, 0, :, :], F, one.unsqueeze(2).broadcast_to([P, 2, S]), ALU.mult).then_inc(done["pool_expert_step"], 1)
            pool.wait_ge(done["pool_expert_step"], base + 1)
            pool.tensor_tensor(rest, F, parts[:, 0, :, :], ALU.subtract).then_inc(done["pool_expert_step"], 1)
            pool.wait_ge(done["pool_expert_step"], base + 2)
            pool.tensor_tensor(parts[:, 1, :, :], rest, one.unsqueeze(2).broadcast_to([P, 2, S]), ALU.mult).then_inc(done["pool_expert_step"], 1)
            pool.wait_ge(done["pool_expert_step"], base + 3)
            pool.tensor_tensor(parts[:, 2, :, :], rest, parts[:, 1, :, :], ALU.subtract).then_inc(done["ex_split"], 1)
            pool.wait_ge(done["ex_v_ready"], n + 2)
            if own:
                pool.wait_ge(done["ex_valued"], n * 16 + 12)
            pool.tensor_tensor(V8[:, :, 0:12, 0:8], Vn[:, :, 0:12, :], one.unsqueeze(2).unsqueeze(3).broadcast_to([P, NT, 12, 8]), ALU.mult).then_inc(done["ex_v_placed"], 1)
            if own:
                pool.wait_ge(done["ex_valued"], n * 16 + 16)
            pool.tensor_tensor(V8[:, :, 12:16, 0:8], Vn[:, :, 12:16, :], one.unsqueeze(2).unsqueeze(3).broadcast_to([P, NT, 4, 8]), ALU.mult).then_inc(done["ex_v_placed"], 1)

        @block.tensor
        def _(pe):
            pe.wait_ge(setup["weights_loaded"], 16)
            pe.wait_ge(setup["consts_loaded"], 16)
            pe.wait_ge(setup["sel_loaded"], 16)
            pe.wait_ge(setup["setup_dve"], SETUP_DVE)
            for e in range(E):
                mm = pe.matmul(bank[0][0:E, 0:D], w("l1f_vb")[:, e * E:(e + 1) * E], w("l1f_ow")[:, e * D:(e + 1) * D],
                               start=e == 0, stop=e == E - 1)
            mm.then_inc(setup["setup_pe"], 1)

            def turn_ln(n):
                pe.wait_ge(done["ln_y"], n + 1)
                for t in range(NT):
                    mm = pe.transpose(MISC[:, t * P:(t + 1) * P], y[:, t, :], ident)
                mm.then_inc(done["ln_turned"], 1)

            with pe.Fori(0, B) as b:
                pe.wait_ge(setup["ctx_loaded"], b * 16 + 16)
                for t in range(NT):
                    mm = pe.transpose(bank[6][:, t * P:(t + 1) * P], ctxs[:, t, :], ident)
                mm.then_inc(done["ctx_turned"], 1)

                turn_ln(0)
                pe.wait_ge(done["ctxT_ready"], 1)
                pe.wait_ge(done["ln_yT"], 1)
                for which in range(2):
                    for part, rhs in enumerate((yT, ctxT, ctxT)):
                        mm = pe.matmul(bank[4][0:4, which * S:(which + 1) * S],
                                       w("l0_gate")[:, part * 8 + which * 4:part * 8 + which * 4 + 4], rhs[:, :],
                                       start=part == 0, stop=part == 2)
                mm.then_inc(done["l0_gates"], 1)
                for h in range(4):
                    r = slice(32 * h, 32 * h + 32)
                    pe.matmul(bank[h][:, 0:S], ctxT[r, 0:P], yT[r, :], start=True, stop=True)
                    mm = pe.matmul(bank[h][:, S:S + P], ctxT[r, P:S], yT[r, P:S], start=True, stop=True)
                mm.then_inc(done["l0_qk"], 1)
                pe.wait_ge(done["l0_rows"], 1)
                for k, row in enumerate((8, 10)):
                    for t in range(NT):
                        mm = pe.transpose(bank[5][:, (k * NT + t) * 4:(k * NT + t) * 4 + 4], l0r[0:4, row, t * P:(t + 1) * P],
                                          ident[0:4, 0:4])
                mm.then_inc(done["l0_cols_turned"], 1)
                for h in range(4):
                    mm = pe.matmul(bank[6 + h // 2][:, (h % 2) * S:(h % 2 + 1) * S], c("sel4", 4)[:, h * P:(h + 1) * P],
                                   l0r[0:4, 9, :], start=True, stop=True)
                mm.then_inc(done["l0_spread"], 1)
                pe.wait_ge(done["l0_cm"], 4)
                for t in range(NT):
                    for h in range(4):
                        o = bank[4 + t][:, h * 33:h * 33 + 33]
                        if t == 0:
                            mm = pe.matmul(o, Cm[:, h, 0:P], Vm[:, 0, h, :], start=True, stop=True)
                        else:
                            pe.matmul(o, Cm[:, h, P:S], Vm[:, 0, h, :], start=True, stop=False)
                            mm = pe.matmul(o, Cm[:, h, S:S + P], Vm[:, 1, h, :], start=False, stop=True)
                    mm.then_inc(done["l0_h"], 1)

                turn_ln(1)
                pe.wait_ge(done["ln_yT"], 2)
                for t in range(NT):
                    for k in range(2):
                        mm = pe.matmul(bank[0][:, k * 256 + t * 128:k * 256 + (t + 1) * 128], yT[:, t * P:(t + 1) * P],
                                       w("l0_wsd")[:, k * 128:(k + 1) * 128], start=True, stop=True)
                mm.then_inc(done["l0f_gates"], 1)
                for t in range(NT):
                    mm = pe.matmul(bank[1 + t][:, :], yT[:, t * P:(t + 1) * P], w("l0_wv"), start=True, stop=True)
                    mm.then_inc(done["l0f_pv"], 1)
                pe.wait_ge(done["l0f_gcopied"], 1)
                pe.wait_ge(done["l0f_pvcopied"], 2)

                def project_qk(h):
                    if some(h):
                        pe.wait_ge(done["l0f_qk_ready"], h)
                    for part, wt in enumerate((w("l0_wq"), w("l0_wk"))):
                        mm = pe.matmul(bank[2][0:64, part * S:(part + 1) * S], wt[:, h * 64:(h + 1) * 64], yT[:, :],
                                       start=True, stop=True)
                    mm.then_inc(done["l0f_qk"], 1)

                def before_step(i):
                    if i == 0:
                        project_qk(0)
                    if i + 1 < 16:
                        project_qk(i + 1)
                    if i < 16:
                        pe.wait_ge(done["l0f_qk_ready"], i + 1)
                    if i == 2:
                        pe.wait_ge(done["filled"], 2)
                    if i == 3:
                        pe.wait_ge(done["l0f_vdve"], 2)
                    if i in (7, 11):
                        pe.wait_ge(done["l0f_vpool"], (i - 3) // 2)
                    if i == 15:
                        pe.wait_ge(done["l0f_vdve"], 4)

                pe_attention(pe, A0, V64, before=before_step)
                for t in (1, 0):
                    pe.wait_ge(done["l0f_gdve"], 3)
                    for q in range(4):
                        mm = pe.transpose(bank[t][:, q * P:(q + 1) * P], pv[:, t, q * P:(q + 1) * P], ident)
                    mm.then_inc(done["l0f_gturned"], 1)
                pe.wait_ge(done["l0f_gT"], 2)
                for t in range(NT):
                    for q in range(4):
                        mm = pe.matmul(bank[2][:, t * P:(t + 1) * P], GT[:, q, t * P:(t + 1) * P], w("l0_wo")[:, q * D:(q + 1) * D],
                                       start=q == 0, stop=q == 3)
                mm.then_inc(done["projected"], 1)

                pe.wait_ge(setup["later_weights_loaded"], 16)
                turn_ln(2)
                pe.wait_ge(done["ln_yT"], 3)
                body_pe(pe, masked, -1, False, False, True)
                pe.wait_ge(done["neg_ready"], 1)
                body_pe(pe, masked, 0, False, True, False)
                body_pe(pe, masked, 1, True, False, False)

                turn_ln(3)
                pe.wait_ge(done["ln_yT"], 4)
                for t in range(NT):
                    mm = pe.matmul(bank[4][:, t * 64:(t + 1) * 64], yT[:, t * P:(t + 1) * P], w("l1f_rw1"), start=True, stop=True)
                mm.then_inc(done["l1f_r1"], 1)
                body_pe(pe, experts, -1, False, False, True, steps=range(0, 7))
                pe.wait_ge(done["l1f_r1n"], 1)
                for t in range(NT):
                    mm = pe.transpose(bank[3][0:64, t * P:(t + 1) * P], r1[:, t, :], ident)
                mm.then_inc(done["l1f_r1turned"], 1)
                pe.wait_ge(done["l1f_r1T"], 1)
                for t in range(NT):
                    mm = pe.matmul(bank[4][:, 128 + t * E:128 + (t + 1) * E], r1T[:, t * P:(t + 1) * P], w("l1f_rw2", 64),
                                   start=True, stop=True)
                mm.then_inc(done["router_logits"], 1)
                body_pe(pe, experts, -1, False, False, True, steps=range(7, 16))
                body_pe(pe, experts, 0, False, True, True)
                with pe.Fori(1, E - 1) as e:
                    body_pe(pe, experts, e, True, True, True)
                body_pe(pe, experts, E - 1, True, True, False)
                for t in range(NT):
                    mm = pe.transpose(bank[2][0:E, t * P:(t + 1) * P], gates[:, t, :], ident)
                mm.then_inc(done["gates_turned"], 1)
                body_pe(pe, experts, E, True, False, False)
                pe.wait_ge(done["gatesT_ready"], 1)
                for t in range(NT):
                    mm = pe.matmul(bank[6][:, t * P:(t + 1) * P], gatesT[:, t * P:(t + 1) * P], out_bias1[:, :],
                                   start=True, stop=True)
                mm.then_inc(done["l1f_bias"], 1)

                turn_ln(4)
                for g in range(2):
                    mm = pe.matmul(bank[1][:, g * S:(g + 1) * S], w("l2_wk")[:, g * P:(g + 1) * P], ctxT[:, :], start=True, stop=True)
                for t in range(NT):
                    mm = pe.matmul(bank[2][:, t * D:(t + 1) * D], ctxT[:, t * P:(t + 1) * P], w("l2_wv"), start=True, stop=True)
                mm.then_inc(done["l2_kv"], 1)
                pe.wait_ge(done["ln_yT"], 5)
                for g in range(2):
                    mm = pe.matmul(bank[0][:, g * S:(g + 1) * S], w("l2_wq")[:, g * P:(g + 1) * P], yT[:, :], start=True, stop=True)
                mm.then_inc(done["l2_q"], 1)
                pe.wait_ge(done["l2_q_ready"], 1)
                pe.wait_ge(done["l2_kv_ready"], 1)
                pe_attention(pe, A2, V16)

                turn_ln(5)
                pe.wait_ge(done["ln_yT"], 6)
                for t in range(NT):
                    mm = pe.matmul(bank[6][:, t * E:(t + 1) * E], yT[:, t * P:(t + 1) * P], w("l2f_router"), start=True, stop=True)
                mm.then_inc(done["router_logits"], 1)
                for e in range(E + 1):
                    if e < E:
                        if some(e - 1):
                            pe.wait_ge(done["l2f_gelu"], e - 1)
                        pe.matmul(bank[e % 2][:, 0:S], w("l2f_win")[:, e * P:(e + 1) * P], yT[:, :], start=True, stop=True)\
                            .then_inc(done["l2f_h"], 1)
                    if e >= 1:
                        k = e - 1
                        pe.wait_ge(done["l2f_gelu"], k + 1)
                        if some(k - 1):
                            pe.wait_ge(done["l2f_oadd"], k - 1)
                        for t in range(NT):
                            mm = pe.matmul(bank[2 + k % 2][:, t * P:(t + 1) * P], hT[:, k % 2, 0, t * P:(t + 1) * P],
                                           w("l2f_wout")[:, k * D:(k + 1) * D], start=True, stop=True)
                        mm.then_inc(done["l2f_o"], 1)
                pe.wait_ge(done["gates_ready"], 2)
                for t in range(NT):
                    mm = pe.transpose(bank[4][0:E, t * P:(t + 1) * P], gates[:, t, :], ident)
                mm.then_inc(done["gates_turned"], 1)
                pe.wait_ge(done["gatesT_ready"], 2)
                for t in range(NT):
                    mm = pe.matmul(bank[5][:, t * P:(t + 1) * P], gatesT[:, t * P:(t + 1) * P], w("l2f_bout", E), start=True, stop=True)
                mm.then_inc(done["projected"], 1)

                turn_ln(6)
                pe.matmul(bank[1][:, 0:S], w("l3_wk"), ctxT[:, :], start=True, stop=True)
                for t in range(NT):
                    mm = pe.matmul(bank[2][:, t * D:(t + 1) * D], ctxT[:, t * P:(t + 1) * P], w("l3_wv"), start=True, stop=True)
                pe.wait_ge(done["ln_yT"], 7)
                pe.matmul(bank[0][:, 0:S], w("l3_wq"), yT[:, :], start=True, stop=True).then_inc(done["l3_qkv"], 1)
                pe.wait_ge(done["l3_qk_ready"], 2)
                pe.wait_ge(done["l3_v_ready"], 1)
                for t in range(NT):
                    mm = pe.matmul(bank[3][:, t * S:(t + 1) * S], qS[:, 0, t * P:(t + 1) * P], kS[:, 0, :], start=True, stop=True)
                mm.then_inc(done["l3_s"], 1)
                pe.wait_ge(done["l3_exp"], 2)
                for t in range(NT):
                    for k in range(NT):
                        mm = pe.transpose(bank[4][:, k * S + t * P:k * S + (t + 1) * P], pr[:, t, k * P:(k + 1) * P], ident)
                mm.then_inc(done["l3_pturned"], 1)
                pe.wait_ge(done["l3_pT"], 1)
                for k in range(NT):
                    mm = pe.matmul(bank[5][:, 0:S], acc[:, k, :], PT[:, 0, k * S:(k + 1) * S], start=k == 0, stop=k == NT - 1)
                mm.then_inc(done["l3_ctx"], 1)
                pe.wait_ge(done["l3_ctx_ready"], 1)
                for t in range(NT):
                    mm = pe.matmul(bank[6][:, t * P:(t + 1) * P], onT[:, t * P:(t + 1) * P], w("l3_wo"), start=True, stop=True)
                mm.then_inc(done["l3_out"], 1)

                turn_ln(7)
                pe.wait_ge(done["ln_yT"], 8)
                body_pe(pe, rotary, -1, False, False, True)
                body_pe(pe, rotary, 0, False, True, False)
                body_pe(pe, rotary, 1, True, False, False)
                turn_ln(8)
                pe.wait_ge(done["ln_yT"], 9)
                for t in range(NT):
                    mm = pe.matmul(bank[6][:, t * E:(t + 1) * E], yT[:, t * P:(t + 1) * P], w("l3f_wgate"), start=True, stop=True)
                mm.then_inc(done["router_logits"], 1)
                pe.wait_ge(done["l3f_top"], 1)
                pe.matmul(bank[7][:, 0:E], c("upto"), coef[:, 0:E], start=True, stop=True)
                pe.matmul(bank[7][:, E:2 * E], c("ones"), coef[:, 0:E], start=True, stop=False)
                pe.matmul(bank[7][:, E:2 * E], c("upto"), coef[:, E:2 * E], start=False, stop=True)
                pe.matmul(bank[7][:, 2 * E:3 * E], c("ones"), coef[:, 0:E], start=True, stop=False)
                pe.matmul(bank[7][:, 2 * E:3 * E], c("ones"), coef[:, E:2 * E], start=False, stop=True)\
                    .then_inc(done["l3f_count"], 1)
                for e in range(E + 1):
                    if e < E:
                        if some(4 * (e - 1)):
                            pe.wait_ge(done["l3f_gelu"], 4 * (e - 1))
                        for f in range(4):
                            pe.matmul(bank[2 * (e % 2) + f // 2][:, (f % 2) * S:(f % 2 + 1) * S],
                                      w("l3f_w1")[:, (e * 4 + f) * P:(e * 4 + f + 1) * P], yT[:, :],
                                      start=True, stop=True).then_inc(done["l3f_h"], 1)
                    if e >= 1:
                        k = e - 1
                        pe.wait_ge(done["l3f_gelu"], 4 * (k + 1))
                        if some(k - 1):
                            pe.wait_ge(done["l3f_oadd"], k - 1)
                        for t in range(NT):
                            for f in range(4):
                                mm = pe.matmul(bank[4 + k % 2][:, t * P:(t + 1) * P], hT[:, k % 2, f, t * P:(t + 1) * P],
                                               w("l3f_w2")[:, (k * 4 + f) * D:(k * 4 + f + 1) * D], start=f == 0, stop=f == 3)
                        mm.then_inc(done["l3f_o"], 1)
                pe.wait_ge(done["gates_ready"], 3)
                for t in range(NT):
                    mm = pe.transpose(bank[6][0:E, t * P:(t + 1) * P], gates[:, t, :], ident)
                mm.then_inc(done["gates_turned"], 1)
                pe.wait_ge(done["gatesT_ready"], 3)
                for t in range(NT):
                    mm = pe.matmul(bank[0][:, t * P:(t + 1) * P], gatesT[:, t * P:(t + 1) * P], w("l3f_b2", E), start=True, stop=True)
                mm.then_inc(done["projected"], 1)
                end_of_batch(pe)

        @block.scalar
        def _(act):
            act.wait_ge(setup["weights_loaded"], 16)
            act.wait_ge(setup["consts_loaded"], 16)
            act.activation(tanh_gain[:, :], w("gains"), ACT.Tanh).then_inc(setup["setup_act"], 1)
            with act.Fori(0, B) as b:
                def copy_ln(n, scale=None, bias=None):
                    act.wait_ge(done["ln_turned"], n + 1)
                    if scale is None:
                        act.activation(yT[:, :], MISC[:, 0:S], ACT.Copy).then_inc(done["ln_yT"], 1)
                    else:
                        act.activation(yT[:, :], MISC[:, 0:S], ACT.Identity, bias=bias, scale=scale).then_inc(done["ln_yT"], 1)

                act.wait_ge(setup["x_loaded"], b * 16 + 16)
                act.wait_ge(done["xs_free"], 1)
                act.activation(xs[:, :, :], xn[:, :, :], ACT.Copy).then_inc(done["x_taken"], 1)
                act.wait_ge(done["ctx_turned"], 1)
                act.activation(ctxT[:, :], bank[6][:, 0:S], ACT.Copy).then_inc(done["ctxT_ready"], 1)
                copy_ln(0)
                act.wait_ge(done["l0_absf"], 1)
                act.activation(l0r[0:4, 3, :], l0r[0:4, 2, :], ACT.Exp, scale=-1.0).then_inc(done["act_step"], 1)
                act.wait_ge(done["act_step"], 1)
                act.activation(l0r[0:4, 4, :], l0r[0:4, 3, :], ACT.Ln, bias=1.0).then_inc(done["l0_softplus"], 1)
                act.wait_ge(done["l0_negm"], 1)
                act.activation(dn[:, 0, :], mcol[:, :, :].rearrange("p t h -> p (t h)"), ACT.Exp).then_inc(done["l0_expm"], 1)
                act.wait_ge(done["l0_args"], 1)
                act.activation(Dm[:, :, :], Dm[:, :, :], ACT.Exp).then_inc(done["l0_decay"], 1)

                copy_ln(1)
                act.wait_ge(done["l0f_gcopied"], 1)
                act.activation(gsig[:, 0:256], gv[:, 0:256], ACT.Exp, scale=-1.0).then_inc(done["l0f_sig"], 1)
                for t in range(NT):
                    act.wait_ge(done["l0f_pv"], t + 1)
                    act.activation(pv[:, t, :], bank[1 + t][:, :], ACT.Copy).then_inc(done["l0f_pvcopied"], 1)

                def copy_qk(first, last):
                    for h in range(first, min(last, 16)):
                        act.wait_ge(done["l0f_qk"], h + 1)
                        act.activation(qk64_bf[0:64, h % 4, :], bank[2][0:64, :], ACT.Copy)
                        act.activation(qk64[0:64, h % 4, :], bank[2][0:64, :], ACT.Copy).then_inc(done["l0f_qk_ready"], 1)

                act_attention(act, A0, before=lambda h: copy_qk(h + 3 if h else 0, h + 4))
                for t in (1, 0):
                    act.wait_ge(done["l0f_gturned"], 2 - t)
                    act.activation(GT[:, :, t * P:(t + 1) * P], bank[t][:, :].rearrange("p (q s) -> p q s", q=4), ACT.Copy)\
                        .then_inc(done["l0f_gT"], 1)

                act.wait_ge(setup["later_weights_loaded"], 16)
                copy_ln(2)
                act.wait_ge(done["neg_ready"], 1)
                body_act(act, masked, -1, False, False, True)
                body_act(act, masked, 0, False, True, False)
                body_act(act, masked, 1, True, False, False)

                copy_ln(3)
                body_act(act, experts, -1, False, False, True, steps=range(0, 7))
                act.wait_ge(done["l1f_r1turned"], 1)
                act.activation(r1T, bank[3][0:64, 0:S], ACT.Copy).then_inc(done["l1f_r1T"], 1)
                body_act(act, experts, -1, False, False, True, steps=range(7, 16))
                act.wait_ge(done["router_shifted"], 1)
                act.activation(gv[:, 0:NT * E], gv[:, 0:NT * E], ACT.Exp).then_inc(done["router_exped"], 1)
                body_act(act, experts, 0, False, True, True)
                with act.Fori(1, E - 1) as e:
                    body_act(act, experts, e, True, True, True)
                body_act(act, experts, E - 1, True, True, False)
                act.wait_ge(done["gates_turned"], 1)
                act.activation(gatesT, bank[2][0:E, 0:S], ACT.Copy).then_inc(done["gatesT_ready"], 1)
                body_act(act, experts, E, True, False, False)

                copy_ln(4)
                act.wait_ge(done["l2_q"], 1)
                act.activation(qk_bf[:, 0:2, :], bank[0][:, :].rearrange("p (g s) -> p g s", g=2), ACT.Copy)
                act.activation(qS[:, 0:2, :], bank[0][:, :].rearrange("p (g s) -> p g s", g=2), ACT.Copy).then_inc(done["l2_q_ready"], 1)
                act_attention(act, A2)

                copy_ln(5)
                act.wait_ge(done["router_shifted"], 2)
                act.activation(gv[:, 0:NT * E], gv[:, 0:NT * E], ACT.Exp).then_inc(done["router_exped"], 1)
                for e in range(E):
                    act.wait_ge(done["l2f_h"], e + 1)
                    if some(e - 1):
                        act.wait_ge(done["l2f_o"], e - 1)
                    act.activation(hT[:, e % 2, 0, :], bank[e % 2][:, 0:S], ACT.Gelu_apprx_tanh, bias=w("l2f_bin")[:, e:e + 1])\
                        .then_inc(done["l2f_gelu"], 1)
                act.wait_ge(done["gates_turned"], 2)
                act.activation(gatesT, bank[4][0:E, 0:S], ACT.Copy).then_inc(done["gatesT_ready"], 1)

                copy_ln(6)
                act.wait_ge(done["l3_qkv"], 1)
                act.activation(qS[:, 0, :], bank[0][:, 0:S], ACT.Identity, bias=w("l3_bq")).then_inc(done["l3_qk_ready"], 1)
                act.activation(kS[:, 0, :], bank[1][:, 0:S], ACT.Copy).then_inc(done["l3_qk_ready"], 1)
                act.wait_ge(done["l3_smax"], 1)
                for t in range(NT):
                    act.activation(pr[:, t, :], bank[3][:, t * S:(t + 1) * S], ACT.Exp, scale=D ** -0.5, bias=gs[:, 1, t:t + 1],
                                   accum_out=gs[:, 2, t:t + 1]).then_inc(done["l3_exp"], 1)
                act.wait_ge(done["l3_pturned"], 1)
                act.activation(PT[:, 0, :], bank[4][:, :], ACT.Copy).then_inc(done["l3_pT"], 1)
                act.wait_ge(done["l3_ctx"], 1)
                act.activation(onT[:, :], bank[5][:, 0:S], ACT.Copy).then_inc(done["l3_ctx_ready"], 1)

                copy_ln(7, w("l3f_ln")[:, 0:1], w("l3f_ln")[:, 1:2])
                body_act(act, rotary, -1, False, False, True)
                body_act(act, rotary, 0, False, True, False)
                body_act(act, rotary, 1, True, False, False)
                copy_ln(8, w("l3f_ln")[:, 2:3], w("l3f_ln")[:, 3:4])
                act.wait_ge(done["router_shifted"], 3)
                act.activation(gv[:, 0:NT * E], gv[:, 0:NT * E], ACT.Exp).then_inc(done["router_exped"], 1)
                for e in range(E):
                    if some(e - 1):
                        act.wait_ge(done["l3f_o"], e - 1)
                    for f in range(4):
                        act.wait_ge(done["l3f_h"], 4 * e + f + 1)
                        if f % 2 == 0:
                            act.wait_ge(done["l3f_h"], 4 * e + f + 2)
                        act.activation(hT[:, e % 2, f, :], bank[2 * (e % 2) + f // 2][:, (f % 2) * S:(f % 2 + 1) * S], ACT.Gelu,
                                       bias=w("l3f_b1")[:, e * 4 + f:e * 4 + f + 1]).then_inc(done["l3f_gelu"], 1)
                act.wait_ge(done["gates_turned"], 3)
                act.activation(gatesT, bank[6][0:E, 0:S], ACT.Copy).then_inc(done["gatesT_ready"], 1)
                end_of_batch(act)

        @block.gpsimd
        def _(pool):
            pool.memset(minus_half[:, :], -0.5).then_inc(setup["setup_pool"], 1)
            pool.wait_ge(setup["setup_pool"], 1)
            with pool.Fori(0, B) as b:
                steps = [0]

                def link(ins):
                    steps[0] += 1
                    ins.then_inc(done["pool_step"], 1)
                    pool.wait_ge(done["pool_step"], steps[0])

                def inv_sqrt(out, var, eps, n):
                    link(pool.tensor_scalar(out, var, eps, None, ALU.add))
                    return pool.tensor_tensor(out, out, minus_half[:, 0:n], ALU.pow)

                def ln_rstd(n, eps=1e-5):
                    pool.wait_ge(done["ln_var"], n + 1)
                    inv_sqrt(rstd[:, :], mv[:, :, 1], eps, NT).then_inc(done["ln_rstd"], 1)

                pool.memset(V64[:, :, :, 64:65], 1.0).then_inc(done["filled"], 1)
                pool.wait_ge(done["filled"], 1)
                pool.memset(qk64[64:65, :, S:2 * S], 1.0).then_inc(done["filled"], 1)
                pool.wait_ge(done["filled"], 2)
                ln_rstd(0)
                pool.wait_ge(done["l0_decay"], 1)
                for a in (0, S):
                    pool.tensor_tensor(Dm[:, :, a:a + P], Dm[:, :, a:a + P], c("upto").unsqueeze(1).broadcast_to([P, 4, P]), ALU.mult)\
                        .then_inc(done["l0_decay_masked"], 1)
                pool.wait_ge(done["l0_hstat"], 1)
                inv_sqrt(rstd8[:, :], mv8[:, :, 1], 1e-6, 8).then_inc(done["l0_hrstd"], 1)

                def pool_mix(coef_of, values, dst, signal):
                    m = mixP.rearrange("p (o i d) -> p o i d", i=8, d=64)
                    link(pool.tensor_tensor(m, coef_of, values, ALU.mult))
                    link(pool.tensor_tensor(m[:, :, 0:4, :], m[:, :, 0:4, :], m[:, :, 4:8, :], ALU.add))
                    link(pool.tensor_tensor(m[:, :, 0:2, :], m[:, :, 0:2, :], m[:, :, 2:4, :], ALU.add))
                    link(pool.tensor_tensor(dst, m[:, :, 0, :], m[:, :, 1, :], ALU.add))
                    pool.sem_inc(done[signal], 1)

                ln_rstd(1)
                pool.wait_ge(done["l0f_coef"], 1)
                pool.wait_ge(done["l0f_pvcopied"], 2)
                co = coef[:, :].rearrange("p (k t h e) -> p t k h e", t=NT, k=2, h=16)
                for part in (1, 2):
                    hs = slice(4 * part, 4 * part + 4)
                    for t in range(NT):
                        pool_mix(co[:, t, 0, hs, :].unsqueeze(3).broadcast_to([P, 4, 8, 64]),
                                 pv[:, t, :].rearrange("p (e d) -> p e d", e=8).unsqueeze(1).broadcast_to([P, 4, 8, 64]),
                                 V64[:, t, hs, 0:64], "l0f_vpool")

                pool.wait_ge(done["l0f_vdve"], 4)
                pool.wait_ge(done["l0f_ocoef"], 1)
                for chunk, t in ((0, 1), (0, 0), (1, 1), (1, 0), (2, 0)):
                    pool.wait_ge(done["normed"], 2 * chunk + 2)
                    m = mixP.rearrange("p (o i d) -> p o i d", i=4, d=64)
                    G = pv[:, t, :].rearrange("p (e d) -> p e d", e=8)
                    link(pool.tensor_tensor(m, co[:, t, 1, 4 * chunk:4 * chunk + 4, :].rearrange("p h e -> p e h").unsqueeze(3)
                                            .broadcast_to([P, 8, 4, 64]),
                                            on[:, t, 256 * chunk:256 * chunk + 256].rearrange("p (h d) -> p h d", h=4).unsqueeze(1)
                                            .broadcast_to([P, 8, 4, 64]), ALU.mult))
                    link(pool.tensor_tensor(m[:, :, 0:2, :], m[:, :, 0:2, :], m[:, :, 2:4, :], ALU.add))
                    if chunk == 0:
                        pool.tensor_tensor(G, m[:, :, 0, :], m[:, :, 1, :], ALU.add).then_inc(done["l0f_gpool"], 1)
                    else:
                        link(pool.tensor_tensor(m[:, :, 0, :], m[:, :, 0, :], m[:, :, 1, :], ALU.add))
                        pool.tensor_tensor(G, G, m[:, :, 0, :], ALU.add).then_inc(done["l0f_gpool"], 1)
                    pool.wait_ge(done["l0f_gpool"], 2 * chunk + 2 - t if chunk < 2 else 5)
                ln_rstd(2)
                body_pool(pool, masked, -1, False)
                pool.wait_ge(done["gp_loaded"], 16)
                pool_weight(pool)
                ln_rstd(3)
                pool.wait_ge(done["l1f_rvar"], 1)
                inv_sqrt(rstd[:, :], mv[:, :, 1], 1e-5, NT).then_inc(done["l1f_rrstd"], 1)
                body_pool(pool, experts, -1, False)
                body_pool(pool, experts, 0, True)
                with pool.Fori(1, E - 1) as e:
                    body_pool(pool, experts, e, True)
                ln_rstd(4)
                ln_rstd(5)
                ln_rstd(6)
                ln_rstd(7)
                ln_rstd(8)
                body_pool(pool, rotary, -1, False)
                ln_rstd(9)
                end_of_batch(pool)

        @block.vector
        def _(dve):
            n_setup = [0]

            def slink(ins):
                n_setup[0] += 1
                ins.then_inc(setup["setup_dve"], 1)

            dve.wait_ge(setup["consts_loaded"], 16)
            slink(dve.tensor_copy(ident_bf[:, :], ident))
            dve.wait_ge(setup["causal_loaded"], 16)
            slink(dve.tensor_copy(causS[:, :, :], mixD[:, 0:512].rearrange("p (t s) -> p t s", t=NT)))
            slink(dve.tensor_copy(causT[:, :, :], mixD[:, 512:1024].rearrange("p (t s) -> p t s", t=NT)))
            for k in (16, 64):
                slink(dve.memset(negmax[k][:, :, :, :], 0.0))
            for V, k in ((V8, 8), (V16, 16)):
                slink(dve.memset(V[:, :, :, :], 0.0))
                dve.wait_ge(setup["setup_dve"], n_setup[0])
                slink(dve.memset(V[:, :, :, k:k + 1], 1.0))
            slink(dve.memset(Vm[:, :, :, 32:33], 1.0))
            slink(dve.memset(carry[:, :], 0.0))
            slink(dve.memset(negmax_bf[:, :, :, :], 0.0))
            slink(dve.memset(kone[:, 0:1], 0.0))
            slink(dve.tensor_copy(kone[:, 1:2], c("kones_stack")))
            assert n_setup[0] == SETUP_DVE, n_setup[0]
            dve.wait_ge(setup["setup_dve"], n_setup[0])
            dve.wait_ge(setup["setup_pe"], 1)
            dve.wait_ge(setup["weights_loaded"], 16)
            dve.wait_ge(setup["setup_act"], 1)
            dve.tensor_tensor(out_bias1[:, :], bank[0][0:E, 0:D], w("l1f_ob", E), ALU.add).then_inc(setup["setup_dve"], 1)
            dve.wait_ge(setup["setup_dve"], n_setup[0] + 1)

            with dve.Fori(0, B) as b:
                steps = [0]

                def link(ins):
                    steps[0] += 1
                    ins.then_inc(done["dve_step"], 1)
                    dve.wait_ge(done["dve_step"], steps[0])

                def layernorm(n, src, dst=y):
                    for t in range(NT):
                        ins = dve.bn_stats(bn[:, t, :], src[:, t, :])
                        if t == 0:
                            ins.then_inc(done["dve_step"], 1)
                            steps[0] += 1
                        else:
                            link(ins)
                    for t in range(NT):
                        ins = dve.bn_aggr(mv[:, t, :], bn[:, t, :])
                    ins.then_inc(done["ln_var"], 1)
                    dve.wait_ge(done["ln_rstd"], n + 1)
                    dve.wait_ge(done["ln_var"], n + 1)
                    for t in range(NT):
                        ins = dve.tensor_scalar(dst[:, t, :], src[:, t, :], mv[:, t, 0:1], rstd[:, t:t + 1], ALU.subtract, ALU.mult)
                        if t == 0:
                            ins.then_inc(done["dve_step"], 1)
                            steps[0] += 1
                    return ins

                def add_to_x(src, k):
                    link(dve.scalar_tensor_tensor(xs[:, :, :], src, tanh_gain[:, k:k + 1], xs[:, :, :], ALU.mult, ALU.add))

                def top2(v, n, mask, scratch, rounds=(0, 1)):
                    v3 = v.rearrange("p (n e) -> p n e", e=8)
                    A_, B_, C_, D_ = (scratch[:, k, 0:8 * n].rearrange("p (n e) -> p n e", e=8) for k in range(4))
                    m, k1 = t2s[:, 0, 0:n].unsqueeze(2), t2s[:, 1, 0:n].unsqueeze(2)
                    rank = c("rank").unsqueeze(1).broadcast_to([P, n, 8])
                    mask3 = mask.rearrange("p (n e) -> p n e", e=8)
                    for r in rounds:
                        hot, src = ((A_, v3), (B_, D_))[r]
                        link(dve.tensor_reduce(m, src, X_AXIS, ALU.max))
                        link(dve.tensor_tensor(C_, src, m.broadcast_to([P, n, 8]), ALU.is_ge))
                        link(dve.tensor_tensor(C_, C_, rank, ALU.mult))
                        link(dve.tensor_reduce(k1, C_, X_AXIS, ALU.max))
                        link(dve.tensor_tensor(hot, C_, k1.broadcast_to([P, n, 8]), ALU.is_equal))
                        if r == 0:
                            link(dve.scalar_tensor_tensor(D_, hot, -BIG, v3, ALU.mult, ALU.add))
                        else:
                            link(dve.tensor_tensor(mask3, A_, B_, ALU.add))

                def routing(n, logits, bias=None):
                    dve.wait_ge(done["router_logits"], n)
                    L = gv[:, 0:NT * E]
                    L3 = L.rearrange("p (t e) -> p t e", e=E)
                    if bias is None:
                        link(dve.tensor_copy(L, logits))
                    else:
                        link(dve.tensor_tensor(L3, logits.rearrange("p (t e) -> p t e", e=E), bias.unsqueeze(1).broadcast_to([P, NT, E]), ALU.add))
                    top2(L, NT, coef[:, 0:NT * E], t2)
                    link(dve.tensor_reduce(gs[:, 0, :].unsqueeze(2), L3, X_AXIS, ALU.max))
                    dve.tensor_tensor(L3, L3, gs[:, 0, :].unsqueeze(2).broadcast_to([P, NT, E]), ALU.subtract)\
                        .then_inc(done["router_shifted"], 1)
                    dve.wait_ge(done["router_exped"], n)
                    return L3

                dve.wait_ge(setup["x_loaded"], b * 16 + 16)
                layernorm(0, xn).then_inc(done["ln_y"], 1)
                dve.wait_ge(setup["ctx_loaded"], b * 16 + 16)
                link(dve.tensor_copy(Vm[:, :, :, 0:32], ctxs[:, :, :].rearrange("p t (h d) -> p t h d", h=4)))
                dve.wait_ge(done["l0_gates"], 1)
                R = l0r[0:4, :, :]
                link(dve.tensor_scalar(R[:, 0, :], bank[4][0:4, 0:S], w("l0_bias", 4)[:, 0:1], None, ALU.add))
                link(dve.tensor_scalar(R[:, 1, :], bank[4][0:4, S:2 * S], w("l0_bias", 4)[:, 1:2], None, ALU.add))
                dve.scalar_tensor_tensor(R[:, 2, :], R[:, 1, :], -1.0, R[:, 1, :], ALU.mult, ALU.max).then_inc(done["l0_absf"], 1)
                dve.wait_ge(done["l0_softplus"], 1)
                link(dve.scalar_tensor_tensor(R[:, 5, :], R[:, 1, :], 0.0, R[:, 4, :], ALU.min, ALU.subtract))
                link(dve.tensor_tensor_scan(R[:, 6, :], c("ones", 4)[:, 0:1].broadcast_to([4, S]), R[:, 5, :], 0.0, ALU.mult, ALU.add))
                link(dve.tensor_tensor(R[:, 8, :], R[:, 0, :], R[:, 6, :], ALU.subtract))
                link(dve.tensor_tensor_scan(R[:, 7, :], c("ones", 4)[:, 0:1].broadcast_to([4, S]), R[:, 8, :], -3.0e38, ALU.mult, ALU.max))
                link(dve.tensor_scalar(R[:, 9, :], R[:, 7, :], -1.0, None, ALU.mult))
                dve.tensor_tensor(R[:, 10, :], R[:, 9, :], R[:, 6, :], ALU.subtract).then_inc(done["l0_rows"], 1)
                dve.wait_ge(done["l0_cols_turned"], 1)
                link(dve.tensor_copy(gcol[:, :, :], bank[5][:, 0:8].rearrange("p (t h) -> p t h", t=NT)))
                dve.tensor_copy(mcol[:, :, :], bank[5][:, 8:16].rearrange("p (t h) -> p t h", t=NT)).then_inc(done["l0_negm"], 1)
                dve.wait_ge(done["l0_spread"], 1)
                for h in range(4):
                    src = bank[6 + h // 2][:, (h % 2) * S:(h % 2 + 1) * S]
                    dve.tensor_scalar(Dm[:, h, 0:S], src, gcol[:, 0, h:h + 1], 0.0, ALU.add, ALU.min)
                    ins = dve.tensor_scalar(Dm[:, h, S:S + P], src[:, P:S], gcol[:, 1, h:h + 1], 0.0, ALU.add, ALU.min)
                ins.then_inc(done["l0_args"], 1)
                dve.wait_ge(done["l0_qk"], 1)
                dve.wait_ge(done["l0_decay"], 1)
                dve.wait_ge(done["l0_decay_masked"], 2)
                for h in range(4):
                    dve.scalar_tensor_tensor(Cm[:, h, :], bank[h][:, 0:384], 32 ** -0.5, Dm[:, h, :], ALU.mult, ALU.mult)\
                        .then_inc(done["l0_cm"], 1)
                dve.wait_ge(done["l0_expm"], 1)
                for t in range(NT):
                    dve.wait_ge(done["l0_h"], t + 1)
                    T = bank[4 + t][:, 0:132].rearrange("p (h c) -> p h c", c=33)
                    d = dn[:, 1, 4 * t:4 * t + 4]
                    link(dve.tensor_copy(d.unsqueeze(2), T[:, :, 32:33]))
                    link(dve.scalar_tensor_tensor(dn[:, 2, 0:4], d, -1.0, d, ALU.mult, ALU.max))
                    link(dve.tensor_tensor(dn[:, 2, 0:4], dn[:, 2, 0:4], dn[:, 0, 4 * t:4 * t + 4], ALU.max))
                    link(dve.tensor_scalar(dn[:, 2, 0:4], dn[:, 2, 0:4], 1e-6, None, ALU.add))
                    link(dve.reciprocal(dn[:, 3, 0:4], dn[:, 2, 0:4]))
                    link(dve.tensor_tensor(hh[:, t, :, :], T[:, :, 0:32], dn[:, 3, 0:4].unsqueeze(2).broadcast_to([P, 4, 32]), ALU.mult))
                H = hh[:, :, :, :].rearrange("p t h d -> p (t h) d")
                for k in range(8):
                    ins = dve.bn_stats(bn8[:, k, :], H[:, k, :])
                link(ins)
                for k in range(8):
                    ins = dve.bn_aggr(mv8[:, k, :], bn8[:, k, :])
                ins.then_inc(done["l0_hstat"], 1)
                dve.wait_ge(done["l0_hrstd"], 1)
                dve.wait_ge(done["l0_hstat"], 1)
                link(dve.tensor_tensor(H, H, mv8[:, :, 0:1].broadcast_to([P, 8, 32]), ALU.subtract))
                link(dve.tensor_tensor(H, H, rstd8[:, :].unsqueeze(2).broadcast_to([P, 8, 32]), ALU.mult))
                H2 = hh[:, :, :, :].rearrange("p t h d -> p t (h d)")
                link(dve.tensor_tensor(H2, H2, w("l0_outnorm").unsqueeze(1).broadcast_to([P, NT, D]), ALU.mult))
                dve.wait_ge(done["x_taken"], 1)
                add_to_x(H2, 0)

                def dve_mix(coef_of, values, dst, signal):
                    m = mixD.rearrange("p (o i d) -> p o i d", i=8, d=64)
                    link(dve.tensor_tensor(m, coef_of, values, ALU.mult))
                    dve.tensor_reduce(dst.unsqueeze(3), m.rearrange("p o i d -> p o d i"), X_AXIS, ALU.add).then_inc(done[signal], 1)

                layernorm(1, xs).then_inc(done["ln_y"], 1)
                dve.wait_ge(done["l0f_gates"], 1)
                dve.tensor_copy(gv[:, :], bank[0][:, :]).then_inc(done["l0f_gcopied"], 1)
                dve.wait_ge(done["l0f_gcopied"], 1)
                top2(gv[:, 0:256], 32, coef[:, 0:256], t2)
                dve.wait_ge(done["l0f_sig"], 1)
                link(dve.tensor_scalar(gsig[:, 0:256], gsig[:, 0:256], 1.0, None, ALU.add))
                link(dve.reciprocal(gsig[:, 0:256], gsig[:, 0:256]))
                dve.tensor_tensor(coef[:, 0:256], coef[:, 0:256], gsig[:, 0:256], ALU.mult).then_inc(done["l0f_coef"], 1)
                dve.wait_ge(done["l0f_coef"], 1)
                dve.wait_ge(done["l0f_pvcopied"], 2)
                co = coef[:, :].rearrange("p (k t h e) -> p t k h e", t=NT, k=2, h=16)
                for t in range(NT):
                    if some(t):
                        dve.wait_ge(done["l0f_vdve"], t)
                    dve_mix(co[:, t, 0, 0:4, :].unsqueeze(3).broadcast_to([P, 4, 8, 64]),
                            pv[:, t, :].rearrange("p (e d) -> p e d", e=8).unsqueeze(1).broadcast_to([P, 4, 8, 64]),
                            V64[:, t, 0:4, 0:64], "l0f_vdve")

                m4 = mixD.rearrange("p (o i d) -> p o i d", i=4, d=64)

                def gate_products(chunk, t):
                    return dve.tensor_tensor(m4, co[:, t, 1, 4 * chunk:4 * chunk + 4, :].rearrange("p h e -> p e h").unsqueeze(3)
                                             .broadcast_to([P, 8, 4, 64]),
                                             on[:, t, 256 * chunk:256 * chunk + 256].rearrange("p (h d) -> p h d", h=4).unsqueeze(1)
                                             .broadcast_to([P, 8, 4, 64]), ALU.mult)

                def gate_sums():
                    return dve.tensor_reduce(gsig[:, :].rearrange("p (o d) -> p o d", d=64).unsqueeze(3),
                                             m4.rearrange("p o i d -> p o d i"), X_AXIS, ALU.add)

                def before_step(i):
                    if i in (2, 3):
                        top2(gv[:, 256:512], 32, coef[:, 256:512], mixD[:, :].rearrange("p (a b) -> p a b", a=4), rounds=(i - 2,))
                    if i == 3:
                        dve.sem_inc(done["l0f_ocoef"], 1)
                    if i == 17:
                        dve.wait_ge(done["normed"], 6)
                        link(gate_products(2, 1))
                    if i == 18:
                        link(gate_sums())
                        dve.wait_ge(done["l0f_gpool"], 3)
                        dve.tensor_tensor(pv[:, 1, :], pv[:, 1, :], gsig[:, :], ALU.add).then_inc(done["l0f_gdve"], 1)
                        dve.wait_ge(done["l0f_gdve"], 1)
                    t, hs = (i - 4) // 2, slice(12, 16)
                    m = mixD.rearrange("p (o i d) -> p o i d", i=8, d=64)
                    if i in (4, 6):
                        link(dve.tensor_tensor(m, co[:, t, 0, hs, :].unsqueeze(3).broadcast_to([P, 4, 8, 64]),
                                               pv[:, t, :].rearrange("p (e d) -> p e d", e=8).unsqueeze(1).broadcast_to([P, 4, 8, 64]),
                                               ALU.mult))
                    if i in (5, 7):
                        dve.tensor_reduce(V64[:, t, hs, 0:64].unsqueeze(3), m.rearrange("p o i d -> p o d i"), X_AXIS, ALU.add)\
                            .then_inc(done["l0f_vdve"], 1)
                        dve.wait_ge(done["l0f_vdve"], t + 3)

                dve_attention(dve, A0, link, before=before_step)
                dve.wait_ge(done["normed"], 8)
                for t in (1, 0):
                    if t == 0:
                        dve.wait_ge(done["l0f_gdve"], 2)
                    link(gate_products(3, t))
                    link(gate_sums())
                    dve.wait_ge(done["l0f_gpool"], 5 if t == 0 else 3)
                    dve.tensor_tensor(pv[:, t, :], pv[:, t, :], gsig[:, :], ALU.add).then_inc(done["l0f_gdve"], 1)
                dve.wait_ge(done["projected"], 1)
                add_to_x(bank[2][:, 0:S].rearrange("p (t d) -> p t d", t=NT), 1)

                dve.wait_ge(setup["later_weights_loaded"], 16)
                layernorm(2, xs).then_inc(done["ln_y"], 1)
                dve.wait_ge(done["mask_loaded"], 16)
                dve.wait_ge(done["maskT_loaded"], 16)
                for src, dst in ((mask_i, negS), (maskT_i, negT)):
                    ins = dve.tensor_scalar(dst[:, :, :], src, 1.0, -NEG_MASK * 8 ** 0.5, ALU.subtract, ALU.mult)
                ins.then_inc(done["neg_ready"], 1)
                dve.tensor_copy(acc[:, :, :], w("l1_bo").unsqueeze(1).broadcast_to([P, NT, D])).then_inc(done["ex_added"], 1)
                body_dve(dve, masked, -1, False, False, True)
                body_dve(dve, masked, 0, False, True, False)
                body_dve(dve, masked, 1, True, False, False)
                dve.wait_ge(done["ex_added"], 2)
                add_to_x(acc[:, :, :], 2)

                layernorm(3, xs).then_inc(done["ln_y"], 1)
                link(dve.memset(acc[:, :, :], 0.0))
                dve.wait_ge(done["l1f_r1"], 1)
                link(dve.tensor_tensor(r1, bank[4][:, 0:128].rearrange("p (t d) -> p t d", t=NT),
                                       w("l1f_rb1").unsqueeze(1).broadcast_to([P, NT, 64]), ALU.add))
                for t in range(NT):
                    link(dve.bn_stats(bn[:, t, :], r1[:, t, :]))
                for t in range(NT):
                    ins = dve.bn_aggr(mv[:, t, :], bn[:, t, :])
                ins.then_inc(done["l1f_rvar"], 1)
                dve.wait_ge(done["l1f_rrstd"], 1)
                dve.wait_ge(done["l1f_rvar"], 1)
                for t in range(NT):
                    link(dve.tensor_scalar(r1[:, t, :], r1[:, t, :], mv[:, t, 0:1], rstd[:, t:t + 1], ALU.subtract, ALU.mult))
                link(dve.tensor_tensor(r1, r1, w("l1f_lng").unsqueeze(1).broadcast_to([P, NT, 64]), ALU.mult))
                link(dve.tensor_tensor(r1, r1, w("l1f_lnb").unsqueeze(1).broadcast_to([P, NT, 64]), ALU.add))
                dve.tensor_scalar(r1, r1, 0.0, None, ALU.max).then_inc(done["l1f_r1n"], 1)
                L3 = routing(1, bank[4][:, 128:128 + NT * E], w("l1f_rb2"))
                M3 = coef[:, 0:NT * E].rearrange("p (t e) -> p t e", e=E)
                link(dve.tensor_tensor(gates[:, :, :], L3, M3, ALU.mult))
                link(dve.tensor_reduce(gs[:, 1, :].unsqueeze(2), gates[:, :, :], X_AXIS, ALU.add))
                link(dve.reciprocal(gs[:, 2, :], gs[:, 1, :]))
                dve.tensor_tensor(gates[:, :, :], gates[:, :, :], gs[:, 2, :].unsqueeze(2).broadcast_to([P, NT, E]), ALU.mult)\
                    .then_inc(done["gates_ready"], 1)
                dve.wait_ge(done["gates_ready"], 1)
                body_dve(dve, experts, -1, False, False, True)
                body_dve(dve, experts, 0, False, True, True)
                with dve.Fori(1, E - 1) as e:
                    body_dve(dve, experts, e, True, True, True)
                body_dve(dve, experts, E - 1, True, True, False)
                body_dve(dve, experts, E, True, False, False)
                dve.wait_ge(done["ex_added"], E + 2)
                dve.wait_ge(done["l1f_bias"], 1)
                link(dve.tensor_tensor(acc[:, :, :], acc[:, :, :], bank[6][:, 0:S].rearrange("p (t d) -> p t d", t=NT), ALU.add))
                add_to_x(acc[:, :, :], 3)

                layernorm(4, xs).then_inc(done["ln_y"], 1)
                dve.wait_ge(done["l2_kv"], 1)
                dve.tensor_copy(qk_bf[:, 4:6, :], bank[1][:, :].rearrange("p (g s) -> p g s", g=2))
                dve.tensor_scalar(kS[:, 0:2, :], bank[1][:, :].rearrange("p (g s) -> p g s", g=2), c("kones16"), None, ALU.add)
                dve.tensor_copy(V16[:, :, :, 0:16], bank[2][:, 0:S].rearrange("p (t h d) -> p t h d", t=NT, d=16))\
                    .then_inc(done["l2_kv_ready"], 1)
                dve_attention(dve, A2, link)
                dve.wait_ge(done["normed"], A2.nb + 2)
                add_to_x(on[:, :, 0:D], 4)

                layernorm(5, xs).then_inc(done["ln_y"], 1)
                L3 = routing(2, bank[6][:, 0:NT * E])
                M3 = coef[:, 0:NT * E].rearrange("p (t e) -> p t e", e=E)
                link(dve.tensor_reduce(gs[:, 1, :].unsqueeze(2), L3, X_AXIS, ALU.add))
                link(dve.reciprocal(gs[:, 2, :], gs[:, 1, :]))
                link(dve.tensor_tensor(gates[:, :, :], L3, M3, ALU.mult))
                dve.tensor_tensor(gates[:, :, :], gates[:, :, :], gs[:, 2, :].unsqueeze(2).broadcast_to([P, NT, E]), ALU.mult)\
                    .then_inc(done["gates_ready"], 1)
                dve.wait_ge(done["gates_ready"], 2)
                link(dve.memset(acc[:, :, :], 0.0))
                for e in range(E):
                    dve.wait_ge(done["l2f_o"], e + 1)
                    if some(e):
                        dve.wait_ge(done["l2f_oadd"], e)
                    for t in range(NT):
                        ins = dve.scalar_tensor_tensor(acc[:, t, :], bank[2 + e % 2][:, t * P:(t + 1) * P], gates[:, t, e:e + 1],
                                                       acc[:, t, :], ALU.mult, ALU.add)
                    ins.then_inc(done["l2f_oadd"], 1)
                dve.wait_ge(done["l2f_oadd"], E)
                dve.wait_ge(done["projected"], 2)
                link(dve.tensor_tensor(acc[:, :, :], acc[:, :, :], bank[5][:, 0:S].rearrange("p (t d) -> p t d", t=NT), ALU.add))
                add_to_x(acc[:, :, :], 5)

                layernorm(6, xs).then_inc(done["ln_y"], 1)
                dve.wait_ge(done["l3_qkv"], 1)
                dve.tensor_tensor(acc[:, :, :], bank[2][:, 0:S].rearrange("p (t d) -> p t d", t=NT),
                                  w("l3_bv").unsqueeze(1).broadcast_to([P, NT, D]), ALU.add).then_inc(done["l3_v_ready"], 1)
                dve.wait_ge(done["l3_s"], 1)
                link(dve.tensor_reduce(gs[:, 0, :].unsqueeze(2), bank[3][:, :].rearrange("p (t s) -> p t s", t=NT), X_AXIS, ALU.max))
                dve.tensor_scalar(gs[:, 1, :], gs[:, 0, :], -D ** -0.5, None, ALU.mult).then_inc(done["l3_smax"], 1)
                dve.wait_ge(done["l3_exp"], 2)
                link(dve.reciprocal(gs[:, 3, :], gs[:, 2, :]))
                dve.wait_ge(done["l3_out"], 1)
                for t in range(NT):
                    link(dve.scalar_tensor_tensor(tmp[:, t, :], bank[6][:, t * P:(t + 1) * P], gs[:, 3, t:t + 1], w("l3_bo"),
                                                  ALU.mult, ALU.add))
                add_to_x(tmp[:, :, :], 6)

                link(layernorm(7, xs, x1))
                layernorm(8, x1).then_inc(done["ln_y"], 1)
                link(dve.memset(acc[:, :, :], 0.0))
                body_dve(dve, rotary, -1, False, False, True)
                body_dve(dve, rotary, 0, False, True, False)
                body_dve(dve, rotary, 1, True, False, False)
                dve.wait_ge(done["ex_added"], E + 3)
                link(dve.tensor_tensor(x1[:, :, :], x1[:, :, :], acc[:, :, :], ALU.add))
                layernorm(9, x1).then_inc(done["ln_y"], 1)
                L3 = routing(3, bank[6][:, 0:NT * E])
                M3 = coef[:, 0:NT * E].rearrange("p (t e) -> p t e", e=E)
                dve.sem_inc(done["l3f_top"], 1)
                link(dve.tensor_reduce(gs[:, 1, :].unsqueeze(2), L3, X_AXIS, ALU.add))
                link(dve.reciprocal(gs[:, 2, :], gs[:, 1, :]))
                link(dve.tensor_tensor(gates[:, :, :], L3, gs[:, 2, :].unsqueeze(2).broadcast_to([P, NT, E]), ALU.mult))
                dve.wait_ge(done["l3f_count"], 1)
                K3 = gsig[:, 0:NT * E].rearrange("p (t e) -> p t e", e=E)
                link(dve.tensor_tensor(K3, bank[7][:, 0:2 * E].rearrange("p (t e) -> p t e", e=E),
                                       carry[:, :].unsqueeze(1).broadcast_to([P, NT, E]), ALU.add))
                link(dve.tensor_scalar(K3, K3, float(CAPACITY) + 0.5, None, ALU.is_lt))
                link(dve.tensor_tensor(carry[:, :], carry[:, :], bank[7][:, 2 * E:3 * E], ALU.add))
                link(dve.tensor_tensor(K3, K3, M3, ALU.mult))
                dve.tensor_tensor(gates[:, :, :], gates[:, :, :], K3, ALU.mult).then_inc(done["gates_ready"], 1)
                dve.wait_ge(done["gates_ready"], 3)
                for e in range(E):
                    dve.wait_ge(done["l3f_o"], e + 1)
                    if some(e):
                        dve.wait_ge(done["l3f_oadd"], e)
                    for t in range(NT):
                        ins = dve.scalar_tensor_tensor(x1[:, t, :], bank[4 + e % 2][:, t * P:(t + 1) * P], gates[:, t, e:e + 1],
                                                       x1[:, t, :], ALU.mult, ALU.add)
                    ins.then_inc(done["l3f_oadd"], 1)
                dve.wait_ge(done["l3f_oadd"], E)
                dve.wait_ge(done["projected"], 3)
                link(dve.tensor_tensor(x1[:, :, :], x1[:, :, :], bank[0][:, 0:S].rearrange("p (t d) -> p t d", t=NT), ALU.add))
                add_to_x(x1[:, :, :], 7)
                dve.sem_inc(done["x_final"], 1)
                end_of_batch(dve)


SETUP_DVE = 14


def kernel(**inputs):
    import numpy as _np
    import concourse.bacc as _bacc
    from concourse import mybir as _mybir
    from concourse.bass_utils import run_bass_kernel_spmd as _run

    f32 = _np.float32
    I = {k: _np.asarray(v) for k, v in inputs.items()}

    def spread(cols, dh):
        rows, n = cols.shape
        out = _np.zeros((rows, n // dh, 32), f32)
        out[:, :, :dh] = cols.reshape(rows, n // dh, dh)
        return out.reshape(rows, -1)

    def rows(vec):
        return _np.broadcast_to(vec.reshape(1, -1), (128, vec.size))

    def experts_to_cols(a):
        return a.transpose(1, 0, 2).reshape(a.shape[1], -1)

    gate = _np.concatenate([I["L0_xattn_ig_kernel"].reshape(3, 128, 4), I["L0_xattn_fg_kernel"].reshape(3, 128, 4)], axis=2)
    gains = _np.stack([I["g_xattn"], I["g_ffn"]], axis=1).reshape(-1)
    qkv = I["L3_ffn_Wqkv"].reshape(128, 16, 24)
    swap = [4, 5, 6, 7, 0, 1, 2, 3]
    q, k, v = (qkv[:, :, a:a + 8] for a in (0, 8, 16))
    vb_cols = _np.zeros((128, 8, 8), f32)
    for e in range(8):
        vb_cols[:, e, e] = I["L1_ffn_vb"][e]
    W = {
        "l0_gate": experts_to_cols(gate), "l0_bias": _np.stack([I["L0_xattn_ig_bias"], I["L0_xattn_fg_bias"]], axis=1),
        "l0_outnorm": rows(I["L0_xattn_outnorm_weight"]), "gains": rows(gains),
        "l0_wq": I["L0_ffn_Wq"].transpose(2, 0, 1).reshape(128, -1), "l0_wk": I["L0_ffn_Wk"].transpose(2, 0, 1).reshape(128, -1),
        "l0_wv": I["L0_ffn_Wv"].transpose(2, 0, 1).reshape(128, -1),
        "l0_wsd": _np.concatenate([I["L0_ffn_Ws"].transpose(2, 0, 1).reshape(128, -1),
                                   I["L0_ffn_Wd"].transpose(2, 0, 1).reshape(128, -1)], axis=1),
        "l0_wo": I["L0_ffn_Wo"].transpose(0, 2, 1).reshape(4, 128, 128).transpose(1, 0, 2).reshape(128, -1),
        "l1_wq": I["L1_xattn_wq_k"], "l1_wk": I["L1_xattn_wk_k"], "l1_wv": I["L1_xattn_wv_k"],
        "l1_qb": I["L1_xattn_wq_b"].reshape(128, 1), "l1_kb": I["L1_xattn_wk_b"].reshape(128, 1),
        "l1_vb": rows(I["L1_xattn_wv_b"]), "l1_wo": I["L1_xattn_wo_k"], "l1_bo": rows(I["L1_xattn_wo_b"]),
        "l1f_rw1": I["L1_ffn_rW1"].T, "l1f_rb1": rows(I["L1_ffn_rb1"]), "l1f_lng": rows(I["L1_ffn_ln_g"]),
        "l1f_lnb": rows(I["L1_ffn_ln_b"]), "l1f_rw2": I["L1_ffn_rW2"].T, "l1f_rb2": rows(I["L1_ffn_rb2"]),
        "l1f_ow": experts_to_cols(I["L1_ffn_oW"].transpose(0, 2, 1)), "l1f_vb": vb_cols.reshape(128, 64), "l1f_ob": I["L1_ffn_ob"],
        "l2_wq": spread(I["L2_xattn_Wq"].T, 16), "l2_wk": spread(I["L2_xattn_Wk"].T, 16), "l2_wv": I["L2_xattn_Wv"].T,
        "l2f_router": I["L2_ffn_router_w"], "l2f_win": experts_to_cols(I["L2_ffn_w_in"]), "l2f_bin": I["L2_ffn_b_in"].T,
        "l2f_wout": experts_to_cols(I["L2_ffn_w_out"]), "l2f_bout": I["L2_ffn_b_out"],
        "l3_wk": I["L3_xattn_Wk"].T, "l3_wv": I["L3_xattn_Wv"].T, "l3_wq": I["L3_xattn_Wq"].T, "l3_wo": I["L3_xattn_Wo"].T,
        "l3_bq": I["L3_xattn_bq"].reshape(128, 1), "l3_bv": rows(I["L3_xattn_bv"]), "l3_bo": rows(I["L3_xattn_bo"]),
        "l3f_ln": _np.stack([I["L3_ffn_ln1_g"], I["L3_ffn_ln1_b"], I["L3_ffn_ln2_g"], I["L3_ffn_ln2_b"]], axis=1),
        "l3f_wq": q.reshape(128, -1), "l3f_wqs": q[:, :, swap].reshape(128, -1),
        "l3f_wk": k.reshape(128, -1), "l3f_wks": k[:, :, swap].reshape(128, -1),
        "l3f_wv": v.reshape(128, -1), "l3f_wproj": I["L3_ffn_Wproj"], "l3f_wgate": I["L3_ffn_Wgate"],
        "l3f_w1": experts_to_cols(I["L3_ffn_W1"]), "l3f_b1": I["L3_ffn_b1"].reshape(32, 128).T,
        "l3f_w2": experts_to_cols(I["L3_ffn_W2"].reshape(32, 128, 128)), "l3f_b2": I["L3_ffn_b2"],
    }
    at, n = columns(WEIGHTS)
    weights = _np.zeros((128, n), f32)
    for name, (a, width) in at.items():
        if name == "padding":
            continue
        weights[:W[name].shape[0], a:a + width] = W[name]

    idx = _np.arange(128)
    ang = _np.arange(256, dtype=f32)[:, None] * (1.0 / 10000.0 ** (_np.arange(0, 8, 2, dtype=f32) / f32(8))).astype(f32)
    cos = _np.tile(_np.concatenate([_np.cos(ang), _np.cos(ang)], axis=1).T, (16, 1))
    sin = _np.tile(_np.concatenate([-_np.sin(ang), _np.sin(ang)], axis=1).T, (16, 1))
    later = _np.arange(256)
    neg = _np.where(later[:, None] >= later[None, :], 0.0, -1.0e9 * 8 ** 0.5).astype(f32)
    sel4 = _np.zeros((128, 4, 128), f32)
    for h in range(4):
        sel4[h, h] = 1.0
    kones16 = _np.zeros((128, 1), f32)
    kones16[16::32] = 1.0
    kones_stack = _np.zeros((128, 1), f32)
    kones_stack[[48, 112]] = 1.0
    import ml_dtypes
    sel = _np.zeros((128, 8, 2, 3, 128), ml_dtypes.bfloat16)
    for a, order in enumerate(((0, 0, 1, 0, 1, 2), (0, 1, 0, 2, 1, 0))):
        for tile in range(8):
            for half in range(2):
                for u, part in enumerate(order):
                    for i in range(8):
                        sel[8 * (2 * tile + half) + i, tile, a, part, 64 * half + 8 * u + i] = 1.0
    den = _np.zeros((128, 32), f32)
    den[:, 16] = 1.0
    C = {
        "ident": _np.eye(128, dtype=f32), "ones": _np.ones((128, 128), f32), "upto": (idx[:, None] <= idx[None, :]).astype(f32),
        "rank": _np.broadcast_to(_np.arange(8, 0, -1, dtype=f32), (128, 8)), "sel4": sel4.reshape(128, -1),
        "cos": cos, "sin": sin, "kones16": kones16, "kones_stack": kones_stack, "den": den,
    }
    causal = _np.concatenate([neg.reshape(2, 128, 256).transpose(1, 0, 2).reshape(128, -1),
                              neg.T.reshape(2, 128, 256).transpose(1, 0, 2).reshape(128, -1)], axis=1)
    at, n = columns(CONSTS)
    consts = _np.zeros((128, n), f32)
    for name, (a, width) in at.items():
        consts[:, a:a + width] = C[name]

    experts = _np.stack([_np.concatenate([
        I["L1_ffn_qW"][e].T, I["L1_ffn_kW"][e].T, I["L1_ffn_vW"][e].T,
        I["L1_ffn_qb"][e][:, None], I["L1_ffn_kb"][e][:, None]], axis=1) for e in range(8)])

    mask = I["mask_BxSxS2_ik1"]
    arrays = {
        "x": I["x"], "ctx": I["ctx_1024"], "group_prob_T": I["fside_BxSxS2_0"].transpose(0, 2, 1),
        "mask": mask, "mask_T": mask.transpose(0, 2, 1), "weights": weights, "consts": consts, "causal": causal, "sel": sel, "experts": experts,
    }
    nc = _bacc.Bacc("TRN2", target_bir_lowering=False, num_devices=1)
    args = []
    for name in arrays:
        arrays[name] = a = _np.ascontiguousarray(arrays[name])
        args.append(nc.dram_tensor(name, a.shape, _mybir.dt.from_np(a.dtype), kind="ExternalInput").ap())
    args.append(nc.dram_tensor("out", (8, 256, 128), _mybir.dt.float32, kind="ExternalOutput").ap())
    program(nc, *args)
    r = _run(nc, [arrays], core_ids=[0])
    return r.results[0]["out"]
```
